# Optimizing a Trainium2 kernel written in Bass

```python
import numpy as np
import jax
import jax.numpy as jnp

def _softmax(x, axis=-1):
    return jax.nn.softmax(x, axis=axis)

def _gelu(x):
    return jax.nn.gelu(x, approximate=True)

def _silu(x):
    return jax.nn.silu(x)

def _sigmoid(x):
    return jax.nn.sigmoid(x)

def _layernorm(x, axis=-1, eps=1e-05):
    m = jnp.mean(x, axis=axis, keepdims=True)
    v = jnp.var(x, axis=axis, keepdims=True)
    return (x - m) / jnp.sqrt(v + eps)

def _scatter_add(tgt, idx, src, axis=0):
    return tgt.at[idx].add(src)

def _segment_sum(src, seg, n):
    return jax.ops.segment_sum(src, seg, n)
kernel_name = 'mk_gnn_ffn_d2_gnn_r32_f16cb8'

def setup_inputs(seed: int=0):
    np.random.seed(seed)
    _w = jnp.asarray

    def _rec_inputs():
        import jax
        import jax.numpy as jnp
        _gk = jax.random.key(seed)
        x = -0.0003713 + 1 * jax.random.normal(jax.random.fold_in(_gk, 1), (3125, 256), jnp.float32)
        src = jax.random.randint(jax.random.fold_in(_gk, 2), (50000,), 0, 3125, jnp.int32)
        dst = jax.random.randint(jax.random.fold_in(_gk, 3), (50000,), 0, 3125, jnp.int32)
        _o = jnp.argsort(dst, stable=True)
        src = src[_o]
        dst = dst[_o]
        return (x, src, dst)
    x, src, dst = _rec_inputs()

    def _L0_gnn_setup():
        import jax, jax.numpy as jnp
        import numpy as np
        N_NODES = 50000
        N_EDGES = 50000
        IN_DIM, OUT_DIM, N_HEADS = (256, 64, 4)
        EPS = 1e-12
        key = jax.random.key(seed)
        k1, k2, k3, k4, k5 = jax.random.split(key, 5)
        h = jax.random.normal(k1, (N_NODES, IN_DIM), dtype=jnp.float32)
        edge_index = jax.random.randint(k2, (2, N_EDGES), 0, N_NODES, dtype=jnp.int32)
        W = jax.random.normal(k3, (IN_DIM, OUT_DIM), dtype=jnp.float32) * 0.05
        Wl = jax.random.normal(k4, (N_HEADS, OUT_DIM), dtype=jnp.float32) * 0.05
        Wr = jax.random.normal(k5, (N_HEADS, OUT_DIM), dtype=jnp.float32) * 0.05
        b = jnp.zeros((OUT_DIM,), dtype=jnp.float32)
        return {'h': h, 'W': W, 'Wl': Wl, 'Wr': Wr, 'b': b, 'edge_index': edge_index}
    _L0_gnn_all = _L0_gnn_setup()
    _L0_gnn_in = {k: v for k, v in _L0_gnn_all.items() if k in ('W', 'Wl', 'Wr', 'b')}
    del _L0_gnn_all

    def _L0_ffn_setup():
        import jax, jax.numpy as jnp
        import numpy as np
        E = 8
        K = 2
        D = 256
        H = 512
        DOUT = 256
        EPS = 1e-05
        key = jax.random.key(seed)
        ks = jax.random.split(key, 9)
        s = 0.02
        return {'x': jax.random.normal(ks[0], (4, 256, D), jnp.float32), 'gamma': 1.0 + 0.05 * jax.random.normal(ks[1], (D,), jnp.float32), 'beta': 0.05 * jax.random.normal(ks[2], (D,), jnp.float32), 'Wr': 0.01 * jax.random.normal(ks[3], (D, E), jnp.float32), 'br': jnp.zeros((E,), jnp.float32), 'W1': s * jax.random.normal(ks[4], (E, D, H), jnp.float32), 'b1': s * jax.random.normal(ks[5], (E, H), jnp.float32), 'W2': s * jax.random.normal(ks[6], (E, H, DOUT), jnp.float32), 'b2': s * jax.random.normal(ks[7], (E, DOUT), jnp.float32)}
    _L0_ffn_all = _L0_ffn_setup()
    _L0_ffn_in = {k: v for k, v in _L0_ffn_all.items() if k in ('gamma', 'beta', 'Wr', 'br', 'W1', 'b1', 'W2', 'b2')}
    del _L0_ffn_all

    def _L1_gnn_setup():
        import jax, jax.numpy as jnp
        import numpy as np
        N = 50000
        E = 25000
        D = 256
        O = 256
        P = 0.5
        key = jax.random.key(seed)
        k1, k2, k3, k4, k5 = jax.random.split(key, 5)
        x = jax.random.normal(k1, (N, D), dtype=jnp.float32)
        rows = jax.random.randint(k2, (E,), 0, N, dtype=jnp.int32)
        cols = jax.random.randint(k3, (E,), 0, N, dtype=jnp.int32)
        cols = jnp.where(cols == rows, (cols + 1) % N, cols)
        edge_index = jnp.stack([rows, cols])
        W = jax.random.normal(k4, (6, O, D), dtype=jnp.float32) / np.sqrt(D).astype(np.float32)
        b = jax.random.normal(k5, (6, O), dtype=jnp.float32) * 0.01
        return {'x': x, 'edge_index': edge_index, 'W': W, 'b': b}
    _L1_gnn_all = _L1_gnn_setup()
    _L1_gnn_in = {k: v for k, v in _L1_gnn_all.items() if k in ('W', 'b')}
    del _L1_gnn_all

    def _L1_ffn_setup():
        import jax, jax.numpy as jnp
        import numpy as np
        NUM_EXPERTS = 8
        TOP_K = 2
        B, S, D = (8, 256, 256)

        def _moe(tokens, router_w, w1, b1, w2, b2):
            N = tokens.shape[0]
            E = router_w.shape[0]
            logits = tokens.astype(jnp.float32) @ router_w.astype(jnp.float32).T
            probs = jax.nn.softmax(logits, axis=-1)
            rw, re = jax.lax.top_k(probs, TOP_K)
            if TOP_K > 1:
                rw = rw / jnp.maximum(rw.sum(-1, keepdims=True), 1e-12)
            rw = rw.astype(tokens.dtype)
            combine = jnp.zeros((N, E), tokens.dtype).at[jnp.arange(N)[:, None], re].set(rw)
            out = tokens
            for e in range(E):
                h = jax.nn.gelu(tokens @ w1[e] + b1[e], approximate=False)
                y = h @ w2[e] + b2[e]
                out = out + combine[:, e:e + 1] * y
            return out
        key = jax.random.key(seed)
        ks = jax.random.split(key, 4)
        scale = 1.0 / np.sqrt(D).astype(np.float32)
        return {'input_embeddings': jax.random.normal(ks[0], (B, S, D), jnp.float32), 'router_w': jax.random.normal(ks[1], (NUM_EXPERTS, D), jnp.float32) * scale, 'w1': jax.random.normal(ks[2], (NUM_EXPERTS, D, D), jnp.float32) * scale, 'b1': jnp.zeros((NUM_EXPERTS, D), jnp.float32), 'w2': jax.random.normal(ks[3], (NUM_EXPERTS, D, D), jnp.float32) * scale, 'b2': jnp.zeros((NUM_EXPERTS, D), jnp.float32)}
    _L1_ffn_all = _L1_ffn_setup()
    _L1_ffn_in = {k: v for k, v in _L1_ffn_all.items() if k in ('router_w', 'w1', 'b1', 'w2', 'b2')}
    del _L1_ffn_all
    return {'x': x, 'src': src, 'dst': dst, 'L0_gnn_W': _L0_gnn_in['W'], 'L0_gnn_Wl': _L0_gnn_in['Wl'], 'L0_gnn_Wr': _L0_gnn_in['Wr'], 'L0_gnn_b': _L0_gnn_in['b'], 'L0_ffn_gamma': _L0_ffn_in['gamma'], 'L0_ffn_beta': _L0_ffn_in['beta'], 'L0_ffn_Wr': _L0_ffn_in['Wr'], 'L0_ffn_br': _L0_ffn_in['br'], 'L0_ffn_W1': _L0_ffn_in['W1'], 'L0_ffn_b1': _L0_ffn_in['b1'], 'L0_ffn_W2': _L0_ffn_in['W2'], 'L0_ffn_b2': _L0_ffn_in['b2'], 'L1_gnn_W': _L1_gnn_in['W'], 'L1_gnn_b': _L1_gnn_in['b'], 'L1_ffn_router_w': _L1_ffn_in['router_w'], 'L1_ffn_w1': _L1_ffn_in['w1'], 'L1_ffn_b1': _L1_ffn_in['b1'], 'L1_ffn_w2': _L1_ffn_in['w2'], 'L1_ffn_b2': _L1_ffn_in['b2']}

def reference(x, src, dst, L0_gnn_W, L0_gnn_Wl, L0_gnn_Wr, L0_gnn_b, L0_ffn_gamma, L0_ffn_beta, L0_ffn_Wr, L0_ffn_br, L0_ffn_W1, L0_ffn_b1, L0_ffn_W2, L0_ffn_b2, L1_gnn_W, L1_gnn_b, L1_ffn_router_w, L1_ffn_w1, L1_ffn_b1, L1_ffn_w2, L1_ffn_b2):
    import jax
    import jax.numpy as jnp

    def _L0_gnn_ref(h, W, Wl, Wr, b, edge_index):
        import jax, jax.numpy as jnp
        import numpy as np
        N_NODES = 50000
        N_EDGES = 50000
        IN_DIM, OUT_DIM, N_HEADS = (256, 64, 4)
        EPS = 1e-12
        N = h.shape[0]
        H = Wl.shape[0]
        x = h @ W
        el = x @ Wl.T
        er = x @ Wr.T
        src, dst = (edge_index[0], edge_index[1])
        e = el[src] + er[dst]
        e = jnp.exp(jax.nn.leaky_relu(e, negative_slope=0.2))
        rowsum = jax.ops.segment_sum(e, src, num_segments=N)
        w = e / jnp.maximum(rowsum, EPS)[src]
        heads = [jax.ops.segment_sum(w[:, hd:hd + 1] * x[dst], src, num_segments=N) for hd in range(H)]
        out = jnp.stack(heads, axis=1)
        out = jax.nn.elu(out + b)
        return out.reshape(N, H * x.shape[1])

    def _L0_ffn_ref(x, gamma, beta, Wr, br, W1, b1, W2, b2):
        import jax, jax.numpy as jnp
        import numpy as np
        E = 8
        K = 2
        D = 256
        H = 512
        DOUT = 256
        EPS = 1e-05
        mu = jnp.mean(x, axis=-1, keepdims=True)
        var = jnp.mean(jnp.square(x - mu), axis=-1, keepdims=True)
        xn = (x - mu) * jax.lax.rsqrt(var + EPS) * gamma + beta
        logits = jnp.einsum('bsd,de->bse', xn, Wr) + br
        top_vals, top_idx = jax.lax.top_k(logits, K)
        w = jax.nn.softmax(top_vals, axis=-1)
        w_full = jnp.einsum('bsk,bske->bse', w, jax.nn.one_hot(top_idx, E, dtype=w.dtype))
        y = jnp.zeros(x.shape[:-1] + (DOUT,), x.dtype)
        for e in range(E):
            h = jax.nn.gelu(jnp.einsum('bsd,dh->bsh', xn, W1[e]) + b1[e], approximate=False)
            y_e = jnp.einsum('bsh,hd->bsd', h, W2[e]) + b2[e]
            y = y + y_e * w_full[..., e, None]
        return y

    def _L1_gnn_ref(x, edge_index, W, b):
        import jax, jax.numpy as jnp
        import numpy as np
        N = 50000
        E = 25000
        D = 256
        O = 256
        P = 0.5
        n = x.shape[0]
        rows, cols = (edge_index[0], edge_index[1])
        seg = lambda vals, idx: jax.ops.segment_sum(vals, idx, num_segments=n)
        spmm_A = lambda z: seg(z[cols], rows)
        spmm_AT = lambda z: seg(z[rows], cols)
        ones = jnp.ones(rows.shape[0], dtype=x.dtype)
        rowsum = seg(ones, rows)
        colsum = seg(ones, cols)

        def inv(d, e):
            return jnp.where(d > 0, d ** e, jnp.zeros_like(d))
        deg_pairs = [(colsum + 1.0, rowsum + 1.0), (rowsum + 1.0, colsum + 1.0), (spmm_AT(colsum), spmm_A(rowsum)), (spmm_A(colsum), spmm_A(colsum)), (spmm_AT(rowsum), spmm_AT(rowsum)), (spmm_A(rowsum), spmm_AT(colsum))]
        in_inv = [inv(i, P - 1.0)[:, None] for i, _ in deg_pairs]
        out_inv = [inv(o, -P)[:, None] for _, o in deg_pairs]
        z0 = x * in_inv[0]
        xs = [out_inv[0] * (spmm_A(z0) + z0)]
        z1 = x * in_inv[1]
        xs.append(out_inv[1] * (spmm_AT(z1) + z1))
        xs.append(out_inv[2] * spmm_A(spmm_A(x * in_inv[2])))
        xs.append(out_inv[3] * spmm_A(spmm_AT(x * in_inv[3])))
        xs.append(out_inv[4] * spmm_AT(spmm_A(x * in_inv[4])))
        xs.append(out_inv[5] * spmm_AT(spmm_AT(x * in_inv[5])))
        total = jnp.zeros((n, W.shape[1]), dtype=x.dtype)
        for k in range(6):
            total = total + jnp.einsum('nd,od->no', xs[k], W[k]) + b[k]
        return total

    def _L1_ffn_ref(input_embeddings, router_w, w1, b1, w2, b2):
        import jax, jax.numpy as jnp
        import numpy as np
        NUM_EXPERTS = 8
        TOP_K = 2
        B, S, D = (8, 256, 256)

        def _moe(tokens, router_w, w1, b1, w2, b2):
            N = tokens.shape[0]
            E = router_w.shape[0]
            logits = tokens.astype(jnp.float32) @ router_w.astype(jnp.float32).T
            probs = jax.nn.softmax(logits, axis=-1)
            rw, re = jax.lax.top_k(probs, TOP_K)
            if TOP_K > 1:
                rw = rw / jnp.maximum(rw.sum(-1, keepdims=True), 1e-12)
            rw = rw.astype(tokens.dtype)
            combine = jnp.zeros((N, E), tokens.dtype).at[jnp.arange(N)[:, None], re].set(rw)
            out = tokens
            for e in range(E):
                h = jax.nn.gelu(tokens @ w1[e] + b1[e], approximate=False)
                y = h @ w2[e] + b2[e]
                out = out + combine[:, e:e + 1] * y
            return out
        b, s, d = input_embeddings.shape
        tokens = input_embeddings.reshape(b * s, d)
        return _moe(tokens, router_w, w1, b1, w2, b2).reshape(b, s, d)
    edge_index = jnp.stack([src, dst])
    x = x + _L0_gnn_ref(_layernorm(x, axis=-1), L0_gnn_W, L0_gnn_Wl, L0_gnn_Wr, L0_gnn_b, edge_index)
    x = x + _L0_ffn_ref(_layernorm(x, axis=-1)[None], L0_ffn_gamma, L0_ffn_beta, L0_ffn_Wr, L0_ffn_br, L0_ffn_W1, L0_ffn_b1, L0_ffn_W2, L0_ffn_b2)[0]
    x = x + _L1_gnn_ref(_layernorm(x, axis=-1), edge_index, L1_gnn_W, L1_gnn_b)
    x = x + _L1_ffn_ref(_layernorm(x, axis=-1)[None], L1_ffn_router_w, L1_ffn_w1, L1_ffn_b1, L1_ffn_w2, L1_ffn_b2)[0]
    return x

_drawn_inputs = setup_inputs


def setup_inputs(seed=0):
    import zlib

    import numpy as np

    out = dict(_drawn_inputs(seed))
    spreads = {'L0_gnn_b': (0.0, 0.1),
     'L0_ffn_br': (0.0, 0.1),
     'L1_ffn_b1': (0.0, 0.336),
     'L1_ffn_b2': (0.0, 0.1)}
    factors = {'L0_ffn_gamma': 4.202, 'L0_ffn_beta': 3.111, 'L0_ffn_b1': 4.944}
    for name, (base, spread) in spreads.items():
        noise = np.random.default_rng([zlib.crc32(name.encode()), seed]).standard_normal(out[name].shape)
        drawn = base * np.exp(spread * noise) if base else spread * noise
        out[name] = jnp.asarray(drawn.astype(out[name].dtype))
    for name, factor in factors.items():
        out[name] = (out[name] * factor).astype(out[name].dtype)
    return out
```

```python
from contextlib import ExitStack

import concourse.bass as bass
import concourse.mybir as mybir
import numpy as np

F32 = mybir.dt.float32
F16 = mybir.dt.float16
I32 = mybir.dt.int32
U32 = mybir.dt.uint32
ALU = mybir.AluOpType
ACT = mybir.ActivationFunctionType
AX = mybir.AxisListType

N = 3125
E = 50000
D = 256
TP = 125
NT = N // TP
GT = 5
NG = NT // GT
GW = GT * TP
BANK = 512
BANKS = [(b, min(BANK, N - b)) for b in range(0, N, BANK)]
NB = len(BANKS)
WC = 18
WE = WC * TP
GC = 20
GWIN = E // (GC * TP)
RING = 6
MID = 1600


def for_tiles(eng, step, n=NT):
    peel = 2 + n % 2
    for t in range(peel):
        step(t, t % 2, t // 2)
    with eng.Fori(0, (n - peel) // 2) as i:
        for j in range(2):
            step(i * 2 + (peel + j), (peel + j) % 2, i + (peel + j) // 2)


SR = 5


def for_ring(eng, step):
    for j in range(SR):
        step(j, j, 0)
    with eng.Fori(1, NT // SR) as g:
        for j in range(SR):
            step(g * SR + j, j, g)


def for_ring2(eng, step):
    for t in range(SR):
        step(t, t, 0, t % 2)
    with eng.Fori(0, (NT - SR) // (2 * SR)) as i:
        for n in range(2 * SR):
            t = SR + n
            step(i * (2 * SR) + t, n % SR, i * 2 + (1 + n // SR), t % 2)


def clear_semaphores(nc):
    nums = sorted(nc.released_uncleared_semaphores)
    with nc.Block() as block:
        @block.gpsimd
        def _(pool):
            first = 0
            for n in range(1, len(nums) + 1):
                if n == len(nums) or nums[n] != nums[n - 1] + 1:
                    pool.sem_clear(range(nums[first], nums[n - 1] + 1))
                    first = n


class Scratch:

    def __init__(self, nc, ctx):
        self.pool_sem = lambda name: ctx.enter_context(nc.semaphore(name))
        self.adj_t = nc.dram_tensor("adj_t", [NT, 128, NT, TP], F16).ap()
        self.slot_x = nc.dram_tensor("slot_x", [NBLK * SLOT, D], F32).ap()
        self.slot_y = nc.dram_tensor("slot_y", [NBLK * SLOT, D], F32).ap()
        self.y = [nc.dram_tensor(f"y{k}", [NT, TP, 2 * D], F16).ap() for k in (2, 3, 4, 5)]
        self.adj = nc.dram_tensor("adj", [NT, 128, NT, TP], F16).ap()


def consts(nc, ctx):
    ident = ctx.enter_context(nc.sbuf_tensor("ident", [128, 128], F32))
    ident16 = ctx.enter_context(nc.sbuf_tensor("ident16", [128, 128], F16))
    ones = ctx.enter_context(nc.sbuf_tensor("ones", [128, 128], F32))
    ones16 = ctx.enter_context(nc.sbuf_tensor("ones16", [128, 1], F16))
    made = ctx.enter_context(nc.semaphore("consts_made"))
    with nc.Block() as block:
        @block.gpsimd
        def _(pool):
            nc.gpsimd.memset(ident[:], 0.0).then_inc(made, 1)
            nc.gpsimd.memset(ident16[:], 0.0).then_inc(made, 1)
            nc.gpsimd.memset(ones[:], 1.0).then_inc(made, 1)
            nc.gpsimd.memset(ones16[:], 1.0).then_inc(made, 1)
            pool.wait_ge(made, 4)
            for m in (ident, ident16):
                nc.gpsimd.affine_select(out=m[:], in_=m[:], compare_op=ALU.not_equal, fill=1.0, base=0,
                                        pattern=[[-1, 128]], channel_multiplier=1).then_inc(made, 1)
            pool.wait_ge(made, 6)
    return ident, ident16, ones, ones16


def build_adjacency(nc, src, dst, dram, ones, col_part):
    with ExitStack() as ctx:
        def sb(name, shape, dt):
            return ctx.enter_context(nc.sbuf_tensor(name, shape, dt))

        def sem(name):
            return ctx.enter_context(nc.semaphore(name))

        EP = E // TP
        iota_r = sb("iota_r", [128, N], F16)
        iota_c = sb("iota_c", [128, TP], F16)
        dst_a = sb("dst_a", [128, EP], I32)
        dst_b = sb("dst_b", [128, EP], I32)
        dst_f = sb("dst_f", [128, EP], F32)
        less = sb("less", [128, 2, EP], F32)
        cnt = sb("cnt", [128, NT + 2], F32)
        row = sb("row", [1, 8, NT + 2], F32)
        off_i = sb("off_i", [1, NT], I32)
        flag_i = sb("flag_i", [1, 1], I32)
        tile_base = sb("tile_base", [128, NT, WC], F32)
        win_src = sb("win_src", [128, NT, WC], I32)
        win_dst = sb("win_dst", [128, NT, WC], I32)
        loc_src = sb("loc_src", [128, NT, WC], F32)
        loc_dst = sb("loc_dst", [128, NT, WC], F32)
        gwin = sb("gwin", [128, 2, GC], I32)
        gloc = sb("gloc", [128, 2, GC], F32)
        hot_c = sb("hot_c", [128, RING, TP], F16)
        hot_r = sb("hot_r", [128, RING, N], F16)
        zeros = sb("zeros", [128, TP], F16)
        strip = sb("strip", [128, 2, N], F16)
        acc = ctx.enter_context(nc.psum_tensor("acc", [128, NB, BANK], F32))
        small = ctx.enter_context(nc.psum_tensor("small", [128, BANK], F32))

        edges_in = sem("edges_in")
        iotas = sem("iotas")
        dve_chain = sem("dve_chain")
        counted = sem("counted")
        summed = sem("summed")
        offsets = sem("offsets")
        windows_in = sem("windows_in")
        local = sem("local")
        cleared = sem("cleared")
        hot_ready = sem("hot_ready")
        hot_used = sem("hot_used")
        bank_done = sem("bank_done")
        bank_free = sem("bank_free")
        strip_out = [sem("strip_out0"), sem("strip_out1")]
        gwin_in = sem("gwin_in")
        gwin_used = sem("gwin_used")
        ghot_ready = sem("ghot_ready")
        ghot_used = sem("ghot_used")
        slots_seen = sem("slots_seen")

        with nc.Block() as block:
            @block.sync
            def _(sp):
                last = (TP - 1) * EP
                sp.dma_start(dst_a[0:TP, :], dst.rearrange("(p k) -> p k", k=EP)).then_inc(edges_in, 16)
                sp.dma_start(dst_b[0:TP - 1, :], dst[1:last + 1].rearrange("(p k) -> p k", k=EP)).then_inc(edges_in, 16)
                sp.dma_start(dst_b[TP - 1:TP, 0:EP - 1], dst[last + 1:E].rearrange("(p k) -> p k", p=1)).then_inc(edges_in, 16)
                sp.dma_start(dst_b[TP - 1:TP, EP - 1:EP], dst[E - 1:E].rearrange("(p k) -> p k", p=1)).then_inc(edges_in, 16)
                sp.wait_ge(offsets, 1)
                with sp.Fori(0, NT) as t:
                    off = sp.value_load(off_i[0:1, bass.ds(t, 1)], min_val=0, max_val=E - WE)
                    sp.dma_start(win_src[0:TP, bass.ds(t, 1), :].rearrange("p a k -> p (a k)"),
                                 src[bass.ds(off, WE)].rearrange("(p k) -> p k", k=WC)).then_inc(windows_in, 16)
                    sp.dma_start(win_dst[0:TP, bass.ds(t, 1), :].rearrange("p a k -> p (a k)"),
                                 dst[bass.ds(off, WE)].rearrange("(p k) -> p k", k=WC)).then_inc(windows_in, 16)
                general = sp.value_load(flag_i[0:1, 0:1], min_val=0, max_val=1)

                def tile(t, par, before):
                    with sp.If(general):
                        with sp.Fori(0, GWIN) as w:
                            sp.wait_ge(gwin_used, (t * GWIN + w) * 2 + 1)
                            first = w * (GC * TP)
                            sp.dma_start(gwin[0:TP, 0, :], src[bass.ds(first, GC * TP)].rearrange("(p k) -> p k", k=GC)).then_inc(gwin_in, 16)
                            sp.dma_start(gwin[0:TP, 1, :], dst[bass.ds(first, GC * TP)].rearrange("(p k) -> p k", k=GC)).then_inc(gwin_in, 16)
                    sp.wait_ge(bank_free, (t + 2) * NB)
                    sp.dma_start(dram.adj_t[:, :, bass.ds(t, 1), :].rearrange("g c a r -> c g (a r)"),
                                 strip[:, par, :].rearrange("c (g r) -> c g r", g=NT)).then_inc(strip_out[par], 16)

                for_tiles(sp, tile)
                sp.wait_ge(strip_out[0], 16 * (NT // 2 + 1))
                sp.wait_ge(strip_out[1], 16 * (NT // 2))

            @block.gpsimd
            def _(pool):
                nc.gpsimd.iota(iota_r[:], [[1, N]], base=-MID, channel_multiplier=0,
                               allow_small_or_imprecise_dtypes=True).then_inc(iotas, 1)
                nc.gpsimd.iota(iota_c[:], [[1, TP]], base=0, channel_multiplier=0,
                               allow_small_or_imprecise_dtypes=True).then_inc(iotas, 1)
                nc.gpsimd.iota(tile_base[:], [[TP, NT], [0, WC]], base=0, channel_multiplier=0,
                               allow_small_or_imprecise_dtypes=True).then_inc(iotas, 1)
                nc.gpsimd.memset(zeros[:], 0.0).then_inc(cleared, 1)
                nc.gpsimd.memset(strip[:], 0.0).then_inc(cleared, 1)

            @block.vector
            def _(dve):
                chain = [0]

                def link(ins):
                    chain[0] += 1
                    ins.then_inc(dve_chain, 1)
                    dve.wait_ge(dve_chain, chain[0])

                dve.wait_ge(edges_in, 64)
                link(nc.vector.tensor_copy(dst_f[0:TP, :], dst_a[0:TP, :]))
                nc.vector.memset(cnt[:], 0.0).then_inc(dve_chain, 1)
                chain[0] += 1
                dve.wait_ge(dve_chain, chain[0])
                for t in range(1, NT + 1):
                    link(nc.vector.tensor_scalar(less[0:TP, t % 2, :], dst_f[0:TP, :], float(TP * t), 0.0, ALU.is_lt,
                                                 ALU.add, accum_out=cnt[0:TP, t:t + 1]))
                link(nc.vector.tensor_tensor(less[0:TP, 0, :], dst_a[0:TP, :], dst_b[0:TP, :], ALU.is_gt))
                nc.vector.tensor_reduce(cnt[0:TP, NT + 1:NT + 2], less[0:TP, 0, :], AX.X, ALU.add).then_inc(counted, 1)
                dve.wait_ge(summed, 1)
                link(nc.vector.tensor_copy(row[:, 0, :], small[0:1, 0:NT + 2]))
                link(nc.vector.tensor_tensor(row[:, 1, 0:NT], row[:, 0, 1:NT + 1], row[:, 0, 0:NT], ALU.subtract))
                link(nc.vector.tensor_scalar(row[:, 2, 0:NT], row[:, 1, 0:NT], float(WE), None, ALU.is_gt))
                link(nc.vector.tensor_reduce(row[:, 3, 0:1], row[:, 2, 0:NT], AX.X, ALU.add))
                link(nc.vector.tensor_tensor(row[:, 4, 0:1], row[:, 3, 0:1], row[:, 0, NT + 1:NT + 2], ALU.add))
                link(nc.vector.tensor_scalar(flag_i[:], row[:, 4, 0:1], 0.5, None, ALU.is_gt))
                nc.vector.tensor_scalar(off_i[:], row[:, 0, 0:NT], float(E - WE), None, ALU.min).then_inc(offsets, 1)

                dve.wait_ge(iotas, 3)
                dve.wait_ge(windows_in, 32 * NT)
                nc.vector.tensor_scalar(loc_src[0:TP], win_src[0:TP], float(MID), None, ALU.subtract).then_inc(local, 1)
                nc.vector.tensor_tensor(loc_dst[0:TP], win_dst[0:TP], tile_base[0:TP], ALU.subtract).then_inc(local, 1)
                dve.wait_ge(local, 2)
                general = dve.value_load(flag_i[0:1, 0:1], min_val=0, max_val=1)
                dve.sem_inc(gwin_used, 1)

                def chunk(ready, slot, c_of_edge, r_of_edge):
                    nc.vector.tensor_scalar(hot_c[0:TP, slot, :], iota_c[0:TP, :], c_of_edge, None,
                                            ALU.is_equal).then_inc(ready, 1)
                    nc.vector.tensor_scalar(hot_r[0:TP, slot, :], iota_r[0:TP, :], r_of_edge, None,
                                            ALU.is_equal).then_inc(ready, 1)

                def tile(t, par, before):
                    for k in range(WC):
                        dve.wait_ge(hot_used, t * WC + k + 1)
                        c = loc_dst[0:TP, bass.ds(t, 1), k:k + 1].rearrange("p a k -> p (a k)")
                        r = loc_src[0:TP, bass.ds(t, 1), k:k + 1].rearrange("p a k -> p (a k)")
                        chunk(hot_ready, k % RING, c, r)
                    with dve.If(general):
                        dve.wait_ge(hot_used, t * WC + WC + RING)
                        dve.sem_inc(slots_seen, 1)
                        with dve.Fori(0, GWIN) as w:
                            dve.wait_ge(gwin_in, (t * GWIN + w) * 32 + 32)
                            nc.vector.tensor_scalar(gloc[0:TP, 0, :], gwin[0:TP, 0, :], float(MID), None,
                                                    ALU.subtract).then_inc(gwin_used, 1)
                            nc.vector.tensor_scalar(gloc[0:TP, 1, :], gwin[0:TP, 1, :], tile_base[0:TP, bass.ds(t, 1), 0:1].rearrange("p a k -> p (a k)"), None,
                                                    ALU.subtract).then_inc(gwin_used, 1)
                            dve.wait_ge(gwin_used, (t * GWIN + w) * 2 + 3)
                            for k in range(GC):
                                dve.wait_ge(ghot_used, (t * GWIN + w) * GC + k + 1)
                                chunk(ghot_ready, k % 5, gloc[0:TP, 1, k:k + 1], gloc[0:TP, 0, k:k + 1])
                        dve.wait_ge(ghot_used, (t * GWIN + GWIN) * GC + 5)
                        dve.sem_inc(slots_seen, 1)

                for_tiles(dve, tile)

            @block.tensor
            def _(pe):
                pe.wait_ge(counted, 1)
                nc.tensor.matmul(small[0:1, 0:NT + 2], ones[0:TP, 0:1], cnt[0:TP, :], start=True, stop=True).then_inc(summed, 1)
                pe.sem_inc(hot_used, RING)
                pe.sem_inc(ghot_used, 5)
                pe.wait_ge(offsets, 1)
                general = pe.value_load(flag_i[0:1, 0:1], min_val=0, max_val=1)
                pe.wait_ge(cleared, 1)
                pe.wait_ge(iotas, 3)

                def tile(t, par, before):
                    for k in range(WC):
                        pe.wait_ge(hot_ready, t * (2 * WC) + 2 * k + 2)
                        for b, (lo, n) in enumerate(BANKS):
                            if k == 0:
                                pe.wait_ge(bank_free, t * NB + b + 1)
                            mm = nc.tensor.matmul(acc[0:TP, b, 0:n], hot_c[0:TP, k % RING, :],
                                                  hot_r[0:TP, k % RING, lo:lo + n], start=(k == 0), stop=(k == WC - 1))
                        mm.then_inc(hot_used, 1)
                    with pe.If(general):
                        for b, (lo, n) in enumerate(BANKS):
                            nc.tensor.matmul(acc[0:TP, b, 0:n], zeros[0:TP, :], iota_r[0:TP, lo:lo + n], start=True,
                                             stop=False, skip_group_check=True)
                        with pe.Fori(0, GWIN) as w:
                            for k in range(GC):
                                pe.wait_ge(ghot_ready, (t * GWIN + w) * (2 * GC) + 2 * k + 2)
                                for b, (lo, n) in enumerate(BANKS):
                                    mm = nc.tensor.matmul(acc[0:TP, b, 0:n], hot_c[0:TP, k % 5, :],
                                                          hot_r[0:TP, k % 5, lo:lo + n], start=False, stop=False,
                                                          skip_group_check=True)
                                mm.then_inc(ghot_used, 1)
                    nc.tensor.matmul(small[0:TP, 0:TP], zeros[0:TP, :], zeros[0:TP, :], start=True,
                                     stop=True).then_inc(bank_done, 1)

                for_tiles(pe, tile)

            @block.scalar
            def _(act):
                act.sem_inc(bank_free, NB)
                act.wait_ge(cleared, 2)

                def tile(t, par, before):
                    act.wait_ge(bank_done, t + 1)
                    if not isinstance(before, int) or before:
                        act.wait_ge(strip_out[par], before * 16)
                    for b, (lo, n) in enumerate(BANKS):
                        col = col_part[0:TP, bass.ds(t, 1), b:b + 1].rearrange("p a k -> p (a k)")
                        nc.scalar.activation(strip[0:TP, par, lo:lo + n], acc[0:TP, b, 0:n], ACT.Copy,
                                             accum_out=col).then_inc(bank_free, 1)

                for_tiles(act, tile)


def transpose_adjacency(nc, dram, ident16, ones16, col_part, deg):
    with ExitStack() as ctx:
        def sb(name, shape, dt):
            return ctx.enter_context(nc.sbuf_tensor(name, shape, dt))

        def sem(name):
            return ctx.enter_context(nc.semaphore(name))

        SLOTS = 3
        PB = 8
        rounds = [(q, min(PB, NT - q)) for q in range(0, NT, PB)]
        NR = len(rounds)
        strip = sb("strip_in", [128, 2, NT, TP], F16)
        turned = sb("turned", [128, 2, NT, TP], F16)
        turn = ctx.enter_context(nc.psum_tensor("turn", [128, NR, PB, 128], F16))
        sums = ctx.enter_context(nc.psum_tensor("sums", [128, BANK], F32))

        strip_in = [sem("strip_in0"), sem("strip_in1")]
        strip_used = sem("strip_used")
        turn_done = sem("turn_done")
        act_free = sem("act_free")
        dve_free = sem("dve_free")
        cleared = sem("cleared")
        turned_out = [dram.pool_sem("turned_out0"), dram.pool_sem("turned_out1")]
        sums_done = sem("sums_done")

        with nc.Block() as block:
            @block.sync
            def _(sp):
                sp.sem_inc(strip_used, 2)

                def tile(t, par, before):
                    sp.wait_ge(strip_used, t + 1)
                    sp.dma_start(strip[:, par], dram.adj_t[:, :, bass.ds(t, 1), :].rearrange("g c a r -> c g (a r)")
                                 ).then_inc(strip_in[par], 16)

                for_tiles(sp, tile)

            @block.tensor
            def _(pe):
                pe.sem_inc(act_free, 2)
                pe.sem_inc(dve_free, 2)

                def tile(t, par, before):
                    flat = strip[:, par].rearrange("c g r -> c (g r)")
                    pe.wait_ge(strip_in[par], before * 16 + 16)
                    for q, (rt0, n) in enumerate(rounds):
                        pe.wait_ge((act_free, dve_free)[q % 2], t * 2 + q // 2 + 1)
                        for j in range(n):
                            blk = flat[0:TP, (rt0 + j) * TP:(rt0 + j + 1) * TP]
                            mm = nc.tensor.transpose(turn[0:TP, q, j, 0:TP], blk, ident16[0:TP, 0:TP])
                        mm.then_inc(turn_done, 1)
                    for rt in range(NT):
                        first = isinstance(t, int) and t == 0 and rt == 0
                        mm = nc.tensor.matmul(sums[0:TP, rt:rt + 1], flat[0:TP, rt * TP:(rt + 1) * TP], ones16[0:TP, 0:1],
                                              start=first, stop=False, skip_group_check=True)
                    mm.then_inc(strip_used, 1)

                for_tiles(pe, tile)

            def copy_out(eng, copy, mine, free):
                eng.wait_ge(cleared, 1)
                def tile(t, par, before):
                    if not isinstance(before, int) or before:
                        eng.wait_ge(turned_out[par], before * 16)
                    for q in mine:
                        rt0, n = rounds[q]
                        eng.wait_ge(turn_done, t * NR + q + 1)
                        copy(turned[0:TP, par, rt0:rt0 + n, :], turn[0:TP, q, 0:n, 0:TP]).then_inc(free, 1)

                for_tiles(eng, tile)

            @block.scalar
            def _(act):
                copy_out(act, nc.scalar.copy, (0, 2), act_free)

            @block.vector
            def _(dve):
                copy_out(dve, nc.vector.tensor_copy, (1, 3), dve_free)
                nc.vector.tensor_reduce(deg[0:TP, :, 1], col_part[0:TP], AX.X, ALU.add).then_inc(sums_done, 1)
                dve.wait_ge(strip_used, NT + 2)
                nc.vector.tensor_copy(deg[0:TP, :, 0], sums[0:TP, 0:NT]).then_inc(sums_done, 1)

            @block.gpsimd
            def _(pool):
                nc.gpsimd.memset(turned[:], 0.0).then_inc(cleared, 1)

                def tile(t, par, before):
                    pool.wait_ge(act_free, t * 2 + 4)
                    pool.wait_ge(dve_free, t * 2 + 4)
                    pool.dma_start(dram.adj[bass.ds(t, 1)].rearrange("a r k c -> r (a k) c"), turned[:, par]
                                   ).then_inc(turned_out[par], 16)

                for_tiles(pool, tile)
                pool.wait_ge(turned_out[0], 16 * (NT // 2 + 1))
                pool.wait_ge(turned_out[1], 16 * (NT // 2))


def layer_norm_dve(nc, dve, chain, x, out, work, square_ready, rooted, turn):
    chain(nc.vector.bn_stats(work[0:TP, 0:6], x))
    dve.sem_inc(chain.passed, 1)
    nc.vector.bn_aggr(work[0:TP, 6:8], work[0:TP, 0:6]).then_inc(square_ready, 1)
    dve.wait_ge(rooted, turn)
    chain(nc.vector.reciprocal(work[0:TP, 9:10], work[0:TP, 8:9]))
    return nc.vector.tensor_scalar(out, x, work[0:TP, 6:7], work[0:TP, 9:10], ALU.subtract, ALU.mult)


class Chain:

    def __init__(self, eng, sem, passed=None):
        self.eng, self.sem, self.count, self.base = eng, sem, 0, 0
        self.passed = passed

    def __call__(self, ins):
        self.count += 1
        ins.then_inc(self.sem, 1)
        self.eng.wait_ge(self.sem, self.base + self.count)

    def at(self, base):
        self.base, self.count = base, 0


HEADS = 4
HD = 64
HF = 2 * (HD + 1)
HROOM = 8192.0


def graph_attention(nc, x, w, wlr, wl_rows, dram, ident, ones, deg, xs, den, scales):
    EL = 0
    ER = HEADS
    MR = 5
    with ExitStack() as ctx:
        def sb(name, shape, dt):
            return ctx.enter_context(nc.sbuf_tensor(name, shape, dt))

        def sem(name):
            return ctx.enter_context(nc.semaphore(name))

        feats = sb("feats", [128, NT, HEADS, 2, HF], F16)
        rows = sb("el_rows", [128, HEADS, N], F32)
        lr = sb("lr", [128, NT, 2 * HEADS], F32)
        ner = sb("ner", [128, NT, HEADS], F32)
        pows = sb("pows", [128, 4, NT, HEADS], F32)
        vdeg = sb("vdeg", [128, NT, 4], F16)

        with ExitStack() as ctx2:
            def sb2(name, shape, dt):
                return ctx2.enter_context(nc.sbuf_tensor(name, shape, dt))

            w_sb = sb2("w_sb", [128, 2, HD], F32)
            wlr_sb = sb2("wlr_sb", [HD, 2 * HEADS], F32)
            wl_sb = sb2("wl_sb", [HD, HEADS, TP], F32)
            xt = sb2("xt", [128, 2, D], F32)
            ht = sb2("ht", [128, 2, D], F32)
            work = sb2("work", [128, 16], F32)
            hT = sb2("hT", [128, 2, 128], F32)
            xw = sb2("xw", [128, NT, HD], F32)
            xwT = sb2("xwT", [HD, 128], F32)
            xwT_all = sb2("xwT_all", [HD, N], F32)
            f = sb2("f", [128, 2, NT, HD + 1], F32)
            mx = sb2("mx", [128, 4], F32)
            mrow = sb2("mrow", [1, 8], F32)
            p_turn = ctx2.enter_context(nc.psum_tensor("p_turn", [128, 2, 256], F32))
            p_xw = ctx2.enter_context(nc.psum_tensor("p_xw", [128, BANK], F32))
            p_xwT = ctx2.enter_context(nc.psum_tensor("p_xwT", [128, BANK], F32))
            p_lr = ctx2.enter_context(nc.psum_tensor("p_lr", [128, BANK], F32))
            p_rows = ctx2.enter_context(nc.psum_tensor("p_rows", [128, 2, BANK], F32))

            w_in = sem("w_in")
            x_in = [sem("x_in0"), sem("x_in1")]
            h_made = sem("h_made")
            dve_chain = sem("g_dve_chain")
            act_chain = sem("g_act_chain")
            square_ready = sem("square_ready")
            passed = sem("passed")
            rooted = sem("rooted")
            turned = sem("g_turned")
            hT_made = sem("hT_made")
            xw_done = sem("xw_done")
            xw_made = sem("xw_made")
            lr_done = sem("lr_done")
            lr_made = sem("lr_made")
            rows_done = sem("rows_done")
            rows_made = sem("rows_made")
            maxima = sem("maxima")
            maxima_row = sem("maxima_row")
            scale_row = sem("scale_row")
            scale_all = sem("scale_all")
            pows_made = sem("pows_made")
            f_made = sem("f_made")
            hi_made = sem("hi_made")
            lo_made = sem("lo_made")

            with nc.Block() as block:
                @block.sync
                def _(sp):
                    sp.dma_start(w_sb[:], w.rearrange("(k p) n -> p k n", k=2)).then_inc(w_in, 16)
                    sp.dma_start(wlr_sb[:], wlr).then_inc(w_in, 16)
                    sp.dma_start(wl_sb[:], wl_rows).then_inc(w_in, 16)

                    def tile(t, par, before):
                        if not isinstance(t, int) or t >= 2:
                            sp.wait_ge(h_made, t - 1)
                        sp.dma_start(xt[0:TP, par, :], x[bass.ds(t * TP, TP), :]).then_inc(x_in[par], 16)

                    for_tiles(sp, tile)

                @block.vector
                def _(dve):
                    link = Chain(dve, dve_chain, passed)

                    def tile(t, par, before):
                        link.at(t * 2)
                        dve.wait_ge(x_in[par], before * 16 + 16)
                        if not isinstance(t, int) or t >= 2:
                            dve.wait_ge(turned, t - 1)
                        layer_norm_dve(nc, dve, link, xt[0:TP, par, :], ht[0:TP, par, :], work, square_ready, rooted,
                                       t + 1).then_inc(h_made, 1)
                        dve.wait_ge(lr_done, t + 1)
                        nc.vector.tensor_copy(lr[0:TP, bass.ds(t, 1), :].rearrange("p a k -> p (a k)"),
                                              p_lr[0:TP, 0:2 * HEADS]).then_inc(lr_made, 1)

                    for_tiles(dve, tile)
                    link.at(2 * NT)
                    dve.wait_ge(lr_made, NT)
                    dve.wait_ge(xw_made, 2 * NT)
                    link(nc.vector.tensor_scalar(ner[0:TP], lr[0:TP, :, ER:ER + HEADS], -1.0, None, ALU.mult))
                    dve.wait_ge(pows_made, 4)
                    link(nc.vector.tensor_reduce(mx[0:TP, 0:1], xw[0:TP], AX.XY, ALU.max, apply_absolute_value=True))
                    nc.vector.tensor_reduce(mx[0:TP, 1:2], pows[0:TP, 2:4], AX.XYZ, ALU.max).then_inc(maxima, 1)
                    dve.wait_ge(maxima_row, 1)
                    link(nc.vector.tensor_reduce(mrow[:, 0:2], p_turn[0:1, :, 0:TP], AX.X, ALU.max))
                    link(nc.vector.tensor_scalar(mrow[:, 2:3], mrow[:, 0:1], 1.0, None, ALU.max))
                    link(nc.vector.tensor_tensor(mrow[:, 3:4], mrow[:, 2:3], mrow[:, 1:2], ALU.mult))
                    link(nc.vector.tensor_scalar(mrow[:, 5:6], mrow[:, 3:4], 1.0 / HROOM, None, ALU.mult))
                    nc.vector.reciprocal(mrow[:, 4:5], mrow[:, 5:6]).then_inc(scale_row, 1)
                    dve.wait_ge(scale_all, 1)
                    link(nc.vector.tensor_copy(scales[0:TP, 0:2], p_lr[0:TP, 0:2]))
                    link(nc.vector.tensor_scalar(pows[0:TP, 2:4], pows[0:TP, 2:4], scales[0:TP, 0:1], None, ALU.mult))
                    for n in range(2 * HEADS):
                        h, kind = n // 2, n % 2
                        fb = f[0:TP, n % 2]
                        if n >= 2:
                            dve.wait_ge(hi_made, n - 1)
                            dve.wait_ge(lo_made, n - 1)
                        p = pows[0:TP, 2 + kind, :, h:h + 1]
                        nc.vector.tensor_copy(fb[:, :, HD:HD + 1], p).then_inc(f_made, 1)
                        nc.vector.tensor_tensor(fb[:, :, 0:HD], xw[0:TP], p.to_broadcast([TP, NT, HD]), ALU.mult).then_inc(f_made, 1)
                        dve.wait_ge(f_made, 2 * n + 2)
                        dve.wait_ge(hi_made, n + 1)
                        o = kind * (HD + 1)
                        nc.vector.tensor_tensor(feats[0:TP, :, h, 1, o:o + HD + 1], fb, feats[0:TP, :, h, 0, o:o + HD + 1],
                                                ALU.subtract).then_inc(lo_made, 1)
                    link(nc.vector.tensor_copy(vdeg[0:TP, :, 0:2], deg[0:TP, :, 0:2]))
                    link(nc.vector.tensor_tensor(vdeg[0:TP, :, 2:4], deg[0:TP, :, 0:2], vdeg[0:TP, :, 0:2], ALU.subtract))

                @block.scalar
                def _(act):
                    def tile(t, par, before):
                        act.wait_ge(square_ready, t + 1)
                        nc.scalar.activation(work[0:TP, 8:9], work[0:TP, 7:8], ACT.Sqrt, bias=scales[0:TP, 3:4]).then_inc(rooted, 1)
                        act.wait_ge(turned, t + 1)
                        nc.scalar.copy(hT[:, :, 0:TP], p_turn[:, :, 0:TP]).then_inc(hT_made, 1)
                        act.wait_ge(xw_done, t + 1)
                        nc.scalar.copy(xwT[:, 0:TP], p_xwT[0:HD, 0:TP]).then_inc(xw_made, 1)
                        nc.scalar.copy(xwT_all[:, bass.ds(t * TP, TP)], p_xwT[0:HD, 0:TP]).then_inc(act_chain, 1)
                        nc.scalar.copy(xw[0:TP, bass.ds(t, 1), :].rearrange("p a k -> p (a k)"), p_xw[0:TP, 0:HD]).then_inc(xw_made, 1)

                    for_tiles(act, tile)
                    act.wait_ge(lr_made, NT)
                    for n, (kind, scale) in enumerate(((EL, 1.0), (EL, 0.2), (ER, 1.0), (ER, 0.2))):
                        nc.scalar.activation(pows[0:TP, n], lr[0:TP, :, kind:kind + HEADS], ACT.Exp, scale=scale).then_inc(pows_made, 1)
                    for n in range(HEADS * NB):
                        h, b = n // NB, n % NB
                        lo, k = BANKS[b]
                        act.wait_ge(rows_done, n + 1)
                        nc.scalar.copy(rows[0:TP, h, lo:lo + k], p_rows[0:TP, n % 2, 0:k]).then_inc(rows_made, 1)
                    for n in range(2 * HEADS):
                        act.wait_ge(f_made, 2 * n + 2)
                        o = (n % 2) * (HD + 1)
                        nc.scalar.copy(feats[0:TP, :, n // 2, 0, o:o + HD + 1], f[0:TP, n % 2]).then_inc(hi_made, 1)

                @block.tensor
                def _(pe):
                    pe.wait_ge(w_in, 48)

                    def tile(t, par, before):
                        pe.wait_ge(h_made, t + 1)
                        for k in range(2):
                            mm = nc.tensor.transpose(p_turn[:, k, 0:TP], ht[0:TP, par, k * 128:(k + 1) * 128], ident[0:TP, 0:TP])
                        mm.then_inc(turned, 1)
                        pe.wait_ge(hT_made, t + 1)
                        for k in range(2):
                            nc.tensor.matmul(p_xwT[0:HD, 0:TP], w_sb[:, k, :], hT[:, k, 0:TP], start=(k == 0), stop=(k == 1))
                        for k in range(2):
                            mm = nc.tensor.matmul(p_xw[0:TP, 0:HD], hT[:, k, 0:TP], w_sb[:, k, :], start=(k == 0), stop=(k == 1))
                        mm.then_inc(xw_done, 1)
                        pe.wait_ge(xw_made, 2 * t + 2)
                        nc.tensor.matmul(p_lr[0:TP, 0:2 * HEADS], xwT[:, 0:TP], wlr_sb[:], start=True, stop=True).then_inc(lr_done, 1)

                    for_tiles(pe, tile)
                    pe.wait_ge(act_chain, NT)
                    for n in range(HEADS * NB):
                        h, b = n // NB, n % NB
                        lo, k = BANKS[b]
                        if n >= 2:
                            pe.wait_ge(rows_made, n - 1)
                        nc.tensor.matmul(p_rows[0:TP, n % 2, 0:k], wl_sb[:, h, :], xwT_all[:, lo:lo + k], start=True,
                                         stop=True).then_inc(rows_done, 1)
                    pe.wait_ge(maxima, 1)
                    for k in range(2):
                        mm = nc.tensor.transpose(p_turn[0:1, k, 0:TP], mx[0:TP, k:k + 1], ident[0:TP, 0:TP])
                    mm.then_inc(maxima_row, 1)
                    pe.wait_ge(scale_row, 1)
                    nc.tensor.matmul(p_lr[0:TP, 0:2], ones[0:1, 0:TP], mrow[:, 4:6], start=True, stop=True).then_inc(scale_all, 1)

        strip = sb("g_strip", [128, NT, GT, TP], F16)
        mask = sb("mask", [128, MR, GW], F16)
        tot = sb("tot", [128, GT, 2 * HF + 4], F32)
        got = sb("got", [128, 2, GT, 2 * HF], F32)
        tmp = sb("tmp", [128, 4, GT, HF], F32)
        acc = ctx.enter_context(nc.psum_tensor("g_acc", [128, GT, BANK], F32))
        strip_in = [sem(f"g_strip_in{j}") for j in range(GT)]
        mask_ready = sem("mask_ready")
        mask_used = sem("mask_used")
        phase_done = sem("phase_done")
        acc_free = sem("acc_free")
        tot_used = sem("tot_used")
        got_used = sem("got_used")
        pool_chain = sem("pool_chain")
        PD = GT + HEADS * (GT - 1)
        NP_ = HEADS + 1

        with nc.Block() as block:
            @block.sync
            def _(sp):
                def load(g):
                    for j in range(GT):
                        if not isinstance(g, int):
                            sp.wait_ge(mask_ready, g * (HEADS * NT) - NT + (j + 1) * GT)
                            sp.wait_ge(phase_done, g * PD - HEADS * (GT - 1))
                        for rt in range(GT):
                            sp.dma_start(strip[:, j * GT:(j + 1) * GT, rt, :],
                                         dram.adj_t[bass.ds(g * GT + rt, 1), :, j * GT:(j + 1) * GT, :].rearrange("g c a r -> c (g a) r")
                                         ).then_inc(strip_in[j], 16)

                load(0)
                with sp.Fori(1, NG) as g:
                    load(g)

            @block.vector
            def _(dve):
                with dve.Fori(0, NG) as g:
                    for h in range(HEADS):
                        for ct in range(NT):
                            if h == 0 and ct % GT == 0:
                                dve.wait_ge(strip_in[ct // GT], g * (16 * GT) + 16 * GT)
                            dve.wait_ge(mask_used, g * (HEADS * NT) + (h * NT + ct + 1))
                            nc.vector.scalar_tensor_tensor(out=mask[0:TP, ct % MR, :], in0=rows[0:TP, h, bass.ds(g * GW, GW)],
                                                           scalar=ner[0:TP, ct, h:h + 1], in1=strip[0:TP, ct].rearrange("c g r -> c (g r)"),
                                                           op0=ALU.is_ge, op1=ALU.mult).then_inc(mask_ready, 1)

            @block.tensor
            def _(pe):
                pe.sem_inc(mask_used, MR)
                with pe.Fori(0, NG) as g:
                    for ct in range(NT):
                        if ct % GT == 0:
                            pe.wait_ge(strip_in[ct // GT], g * (16 * GT) + 16 * GT)
                        for rt in range(GT):
                            if ct == 0:
                                pe.wait_ge(acc_free, g * (NP_ * GT) + rt + 1)
                            blk = strip[0:TP, ct, rt, :]
                            for part in range(2):
                                nc.tensor.matmul(acc[0:TP, rt, 0:HEADS * (HD + 1)], blk, feats[0:TP, ct, :, part, HD + 1:HF],
                                                 start=(ct == 0 and part == 0), stop=False, skip_group_check=True)
                            mm = nc.tensor.matmul(acc[0:TP, rt, 2 * HF:2 * HF + 4], blk, vdeg[0:TP, ct, :], start=False,
                                                  stop=(ct == NT - 1), skip_group_check=True)
                            if ct == NT - 1:
                                mm.then_inc(phase_done, 1)
                    for h in range(HEADS):
                        for ct in range(NT):
                            pe.wait_ge(mask_ready, g * (HEADS * NT) + (h * NT + ct + 1))
                            for rt in range(GT):
                                if ct == 0:
                                    pe.wait_ge(acc_free, g * (NP_ * GT) + ((h + 1) * GT + rt + 1))
                                mm = nc.tensor.matmul(acc[0:TP, rt, 0:2 * HF], mask[0:TP, ct % MR, rt * TP:(rt + 1) * TP],
                                                      feats[0:TP, ct, h].rearrange("p a n -> p (a n)"), start=(ct == 0),
                                                      stop=(ct == NT - 1))
                                if ct == NT - 1 and rt < GT - 1:
                                    mm.then_inc(phase_done, 1)
                            mm.then_inc(mask_used, 1)

            @block.scalar
            def _(act):
                act.sem_inc(acc_free, GT)
                with act.Fori(0, NG) as g:
                    for ph in range(NP_):
                        for rt in range(GT):
                            if ph == 0 or rt < GT - 1:
                                act.wait_ge(phase_done, g * PD + (ph * (GT - 1) + (ph > 0) + rt + 1))
                            else:
                                act.wait_ge(mask_used, g * (HEADS * NT) + (ph * NT + MR))
                            if ph == 0:
                                if rt == 0:
                                    act.wait_ge(tot_used, g + 1)
                                nc.scalar.copy(tot[0:TP, rt, 0:2 * HF + 4], acc[0:TP, rt, 0:2 * HF + 4]).then_inc(acc_free, 1)
                            else:
                                if rt == 0:
                                    act.wait_ge(got_used, g * HEADS + ph)
                                nc.scalar.copy(got[0:TP, ph % 2, rt, :], acc[0:TP, rt, 0:2 * HF]).then_inc(acc_free, 1)

            @block.gpsimd
            def _(pool):
                pool.sem_inc(tot_used, 1)
                pool.sem_inc(got_used, 2)
                link = Chain(pool, pool_chain)
                with pool.Fori(0, NG) as g:
                    link.at(g * (HEADS * 6 + 1))
                    pool.wait_ge(acc_free, g * (NP_ * GT) + 2 * GT)
                    link(nc.gpsimd.tensor_tensor(deg[0:TP, bass.ds(g * GT, GT), 2:4], tot[0:TP, :, 2 * HF:2 * HF + 2],
                                                 tot[0:TP, :, 2 * HF + 2:2 * HF + 4], ALU.add))
                    for h in range(HEADS):
                        s = got[0:TP, (h + 1) % 2]
                        a = pows[0:TP, 0, bass.ds(g * GT, GT), h:h + 1].to_broadcast([TP, GT, HD + 1])
                        a5 = pows[0:TP, 1, bass.ds(g * GT, GT), h:h + 1].to_broadcast([TP, GT, HD + 1])
                        pool.wait_ge(acc_free, g * (NP_ * GT) + (h + 3) * GT)
                        link(nc.gpsimd.tensor_tensor(tmp[0:TP, 0], s[:, :, 0:HF], s[:, :, HF:2 * HF], ALU.add))
                        link(nc.gpsimd.tensor_tensor(tmp[0:TP, 1, :, 0:HD + 1], tot[0:TP, :, h * (HD + 1):(h + 1) * (HD + 1)],
                                                     tmp[0:TP, 0, :, HD + 1:HF], ALU.subtract))
                        link(nc.gpsimd.tensor_tensor(tmp[0:TP, 2, :, 0:HD + 1], tmp[0:TP, 0, :, 0:HD + 1], a, ALU.mult))
                        link(nc.gpsimd.tensor_tensor(tmp[0:TP, 3, :, 0:HD + 1], tmp[0:TP, 1, :, 0:HD + 1], a5, ALU.mult))
                        link(nc.gpsimd.tensor_tensor(xs[0:TP, bass.ds(g * GT, GT), h * HD:(h + 1) * HD], tmp[0:TP, 2, :, 0:HD],
                                                     tmp[0:TP, 3, :, 0:HD], ALU.add))
                        link(nc.gpsimd.tensor_tensor(den[0:TP, bass.ds(g * GT, GT), h:h + 1], tmp[0:TP, 2, :, HD:HD + 1],
                                                     tmp[0:TP, 3, :, HD:HD + 1], ALU.add))
                        pool.sem_inc(got_used, 1)
                    pool.sem_inc(tot_used, 1)


def finish_attention(nc, x, gat_b, den, scales, xs):
    with ExitStack() as ctx:
        def sb(name, shape, dt):
            return ctx.enter_context(nc.sbuf_tensor(name, shape, dt))

        def sem(name):
            return ctx.enter_context(nc.semaphore(name))

        bias = sb("e_bias", [128, D], F32)
        x_all = sb("x_all", [128, NT, D], F32)
        v = sb("e_v", [128, 2, D], F32)
        low = sb("e_low", [128, 2, D], F32)
        x_in = sem("e_x_in")
        chain = sem("e_chain")
        low_made = sem("low_made")
        exp_made = sem("exp_made")
        with nc.Block() as block:
            @block.sync
            def _(sp):
                sp.dma_start(bias[0:TP, :], gat_b).then_inc(x_in, 16)
                sp.dma_start(x_all[0:TP], x.rearrange("(t p) d -> p t d", p=TP)).then_inc(x_in, 16)

            @block.vector
            def _(dve):
                link = Chain(dve, chain)
                link(nc.vector.tensor_scalar(den[0:TP], den[0:TP], scales[0:TP, 1:2], 1e-12, ALU.mult, ALU.max))
                link(nc.vector.reciprocal(den[0:TP], den[0:TP]))
                link(nc.vector.tensor_scalar(den[0:TP], den[0:TP], scales[0:TP, 1:2], None, ALU.mult))
                dve.wait_ge(x_in, 32)

                def first(t, par, base):
                    link.at(base)
                    vt = v[0:TP, par]
                    gt = xs[0:TP, bass.ds(t, 1), :].rearrange("p a (h k) -> p (a h) k", h=HEADS)
                    dt_ = den[0:TP, bass.ds(t, 1), :].rearrange("p a h -> p (a h)").to_broadcast([TP, HEADS, HD])
                    link(nc.vector.tensor_tensor(vt.rearrange("p (h k) -> p h k", h=HEADS), gt, dt_, ALU.mult))
                    link(nc.vector.tensor_tensor(vt, vt, bias[0:TP], ALU.add))
                    nc.vector.tensor_scalar(low[0:TP, par], vt, 0.0, None, ALU.min).then_inc(low_made, 1)
                    dve.wait_ge(exp_made, t + 1)
                    link(nc.vector.scalar_tensor_tensor(out=vt, in0=vt, scalar=0.0, in1=low[0:TP, par], op0=ALU.max, op1=ALU.add))
                    xt = xs[0:TP, bass.ds(t, 1), :].rearrange("p a d -> p (a d)")
                    xa = x_all[0:TP, bass.ds(t, 1), :].rearrange("p a d -> p (a d)")
                    link(nc.vector.scalar_tensor_tensor(out=xt, in0=vt, scalar=-1.0, in1=xa, op0=ALU.add, op1=ALU.add))

                for_tiles(dve, lambda t, par, before: first(t, par, t * 4 + 3))

            @block.scalar
            def _(act):
                def tile(t, par, before):
                    act.wait_ge(low_made, t + 1)
                    nc.scalar.activation(low[0:TP, par], low[0:TP, par], ACT.Exp).then_inc(exp_made, 1)

                for_tiles(act, tile)


NE = 8
SLOT = 128
NBLK = (2 * N + NE * (SLOT - 1)) // SLOT


def mixture(nc, layer, xs, par, ident, ones, scales, dram_x, dram_y, hidden, pool_sem):
    norms = 2 if layer == 0 else 1
    KD = D // 128
    KH = hidden // 128
    with ExitStack() as ctx:
        def sb(name, shape, dt):
            return ctx.enter_context(nc.sbuf_tensor(f"m{layer}_{name}", shape, dt))

        def sem(name):
            return ctx.enter_context(nc.semaphore(f"m{layer}_{name}"))

        tok = sb("tok", [128, NT, D], F32)
        w1 = sb("w1", [128, NE, KD, hidden], F32)
        w2 = sb("w2", [128, NE, KH, D], F32)
        b1 = sb("b1", [128, NE, hidden], F32)
        b2 = sb("b2", [128, NE, D], F32)
        weight = sb("weight", [128, 2, NT], F32)
        pos = sb("pos", [128, 2, NT], U32)
        expert = sb("expert", [1, NBLK], I32)
        w_in = sem("w_in")
        zero_out = sem("zero_out")
        placed = pool_sem(f"m{layer}_placed")

        with ExitStack() as ctx2:
            def sb2(name, shape, dt):
                return ctx2.enter_context(nc.sbuf_tensor(f"r{layer}_{name}", shape, dt))

            def ps(name, shape):
                return ctx2.enter_context(nc.psum_tensor(f"r{layer}_{name}", shape, F32))

            def sem2(name):
                return ctx2.enter_context(nc.semaphore(f"r{layer}_{name}"))

            wr = sb2("wr", [128, KD, NE], F32)
            br = sb2("br", [1, NE], F32)
            gb = sb2("gb", [128, 2, D], F32)
            work = sb2("work", [128, 16], F32)
            mid = sb2("mid", [128, D], F32)
            ht = sb2("ht", [128, 2, D], F32)
            tT = sb2("tT", [128, KD, 128], F32)
            logit = sb2("logit", [128, NT, NE], F32)
            best = sb2("best", [128, NT, 8], F32)
            besti = sb2("besti", [128, NT, 8], U32)
            bestf = sb2("bestf", [128, NT, 2], F32)
            one = sb2("one", [128, 3, NT, NE], F32)
            iota8 = sb2("iota8", [128, NT, NE], F32)
            iota128 = sb2("iota128", [128, NE, NT], F32)
            iotab = sb2("iotab", [1, NBLK, NE - 1], F32)
            before = sb2("before", [128, 128], F32)
            place = sb2("place", [128, NT, NE], F32)
            sums = sb2("sums", [128, 3, NT, NE], F32)
            blocks = sb2("blocks", [128, NE, NT], F32)
            nblk = sb2("nblk", [128, 4, NE], F32)
            eb = sb2("eb", [1, NBLK, NE - 1], F32)
            ebs = sb2("ebs", [1, NBLK], F32)
            s25 = sb2("s25", [128, 4, NT], F32)
            zero = sb2("zero", [128, 8, D], F32)
            p_turn = ps("p_turn", [128, KD, 256])
            p_log = ps("p_log", [128, BANK])
            p_pre = ps("p_pre", [128, BANK])
            p_tot = ps("p_tot", [128, BANK])

            r_in = sem2("r_in")
            chain = sem2("chain")
            passed = sem2("passed")
            square_ready = sem2("square_ready")
            rooted = sem2("rooted")
            tok_made = sem2("tok_made")
            turned = sem2("turned")
            tT_made = sem2("tT_made")
            log_done = sem2("log_done")
            log_made = sem2("log_made")
            made = sem2("made")
            shifted = sem2("shifted")
            expd = sem2("expd")
            ones_made = sem2("ones_made")
            counted = sem2("counted")
            placed_at = sem2("placed_at")

            with nc.Block() as block:
                @block.sync
                def _(sp):
                    sp.dma_start(wr[:], par["wr"].rearrange("(k p) e -> p k e", p=128)).then_inc(r_in, 16)
                    sp.dma_start(br[:], par["br"]).then_inc(r_in, 16)
                    if layer == 0:
                        sp.dma_start(gb[0:TP], par["gb"]).then_inc(r_in, 16)
                    sp.wait_ge(made, 1)
                    for lo in range(0, NBLK, 8):
                        n = min(8, NBLK - lo)
                        sp.dma_start(dram_x[lo * SLOT:(lo + n) * SLOT, :].rearrange("(k p) d -> p k d", p=SLOT),
                                     zero[:, 0:n, :]).then_inc(zero_out, 16)
                    sp.dma_start(w1[:], par["w1"].rearrange("e (k p) h -> p e k h", p=128)).then_inc(w_in, 16)
                    sp.dma_start(w2[:], par["w2"].rearrange("e (k p) h -> p e k h", p=128)).then_inc(w_in, 16)
                    sp.dma_start(b1[:], par["b1"]).then_inc(w_in, 16)
                    sp.dma_start(b2[:], par["b2"]).then_inc(w_in, 16)

                @block.gpsimd
                def _(pool):
                    nc.gpsimd.memset(zero[:], 0.0).then_inc(made, 1)
                    nc.gpsimd.iota(iota8[:], [[0, NT], [1, NE]], base=0, channel_multiplier=0,
                                   allow_small_or_imprecise_dtypes=True).then_inc(made, 1)
                    nc.gpsimd.iota(iota128[:], [[0, NE], [SLOT, NT]], base=0, channel_multiplier=0,
                                   allow_small_or_imprecise_dtypes=True).then_inc(made, 1)
                    nc.gpsimd.iota(iotab[:], [[1, NBLK], [0, NE - 1]], base=0, channel_multiplier=0,
                                   allow_small_or_imprecise_dtypes=True).then_inc(made, 1)
                    nc.gpsimd.affine_select(out=before[:], in_=ones[:], compare_op=ALU.is_gt, fill=0.0, base=0,
                                            pattern=[[1, 128]], channel_multiplier=-1).then_inc(made, 1)
                    pool.wait_ge(placed_at, 1)
                    pool.wait_ge(zero_out, 16 * -(-NBLK // 8))
                    for t in range(NT):
                        for c in range(2):
                            pool.indirect_dma_start(dram_x[:, :], bass.IndirectOffsetOnAxis(ap=pos[0:TP, c, t:t + 1], axis=0),
                                                    tok[0:TP, t, :], None).then_inc(placed, 16)
                    pool.wait_ge(placed, 16 * 2 * NT)

                @block.vector
                def _(dve):
                    link = Chain(dve, chain, passed)
                    dve.wait_ge(r_in, 32 + 16 * (layer == 0))

                    def tile(t, par_, earlier):
                        link.at(t * (7 if layer == 0 else 2))
                        xt = xs[0:TP, bass.ds(t, 1), :].rearrange("p a d -> p (a d)")
                        if not isinstance(t, int) or t >= 2:
                            dve.wait_ge(turned, t - 1)
                        if layer == 0:
                            link(layer_norm_dve(nc, dve, link, xt, mid[0:TP], work, square_ready, rooted, t * 2 + 1))
                            link(layer_norm_dve(nc, dve, link, mid[0:TP], ht[0:TP, par_], work, square_ready, rooted, t * 2 + 2))
                            link(nc.vector.tensor_tensor(ht[0:TP, par_], ht[0:TP, par_], gb[0:TP, 0], ALU.mult))
                            nc.vector.tensor_tensor(ht[0:TP, par_], ht[0:TP, par_], gb[0:TP, 1], ALU.add).then_inc(tok_made, 1)
                        else:
                            layer_norm_dve(nc, dve, link, xt, ht[0:TP, par_], work, square_ready, rooted, t + 1).then_inc(tok_made, 1)

                    for_tiles(dve, tile)
                    link.at(NT * (7 if layer == 0 else 2))
                    dve.wait_ge(log_made, NT)
                    if layer == 1:
                        link(nc.vector.tensor_reduce(s25[0:TP, 0], logit[0:TP], AX.X, ALU.max))
                        nc.vector.tensor_tensor(logit[0:TP], logit[0:TP], s25[0:TP, 0].to_broadcast([TP, NT, NE]),
                                                ALU.subtract).then_inc(shifted, 1)
                        dve.wait_ge(expd, 1)
                        link(nc.vector.tensor_reduce(s25[0:TP, 1], logit[0:TP], AX.X, ALU.add))
                        link(nc.vector.reciprocal(s25[0:TP, 2], s25[0:TP, 1]))
                        link(nc.vector.tensor_tensor(logit[0:TP], logit[0:TP], s25[0:TP, 2].to_broadcast([TP, NT, NE]), ALU.mult))
                    for t in range(NT):
                        m = nc.vector.max(best[0:TP, t, :], logit[0:TP, t, :])
                    link(m)
                    for t in range(NT):
                        m = nc.vector.max_index(besti[0:TP, t, :], best[0:TP, t, :], logit[0:TP, t, :])
                    link(m)
                    if layer == 0:
                        nc.vector.tensor_tensor(s25[0:TP, 0], best[0:TP, :, 1], best[0:TP, :, 0], ALU.subtract).then_inc(shifted, 1)
                        dve.wait_ge(expd, 1)
                        link(nc.vector.tensor_scalar(s25[0:TP, 2], s25[0:TP, 1], 1.0, None, ALU.add))
                        link(nc.vector.reciprocal(weight[0:TP, 0], s25[0:TP, 2]))
                        link(nc.vector.tensor_tensor(weight[0:TP, 1], weight[0:TP, 0], s25[0:TP, 1], ALU.mult))
                    else:
                        link(nc.vector.tensor_tensor(s25[0:TP, 1], best[0:TP, :, 1], best[0:TP, :, 0], ALU.add))
                        link(nc.vector.tensor_scalar(s25[0:TP, 1], s25[0:TP, 1], 1e-12, None, ALU.max))
                        link(nc.vector.reciprocal(s25[0:TP, 2], s25[0:TP, 1]))
                        link(nc.vector.tensor_tensor(weight[0:TP, 0], best[0:TP, :, 0], s25[0:TP, 2], ALU.mult))
                        link(nc.vector.tensor_tensor(weight[0:TP, 1], best[0:TP, :, 1], s25[0:TP, 2], ALU.mult))
                    link(nc.vector.tensor_copy(bestf[0:TP], besti[0:TP, :, 0:2]))
                    dve.wait_ge(made, 5)
                    for c in range(2):
                        link(nc.vector.tensor_tensor(one[0:TP, c], iota8[0:TP], bestf[0:TP, :, c].to_broadcast([TP, NT, NE]),
                                                     ALU.is_equal))
                    nc.vector.tensor_tensor(one[0:TP, 2], one[0:TP, 0], one[0:TP, 1], ALU.add).then_inc(ones_made, 1)
                    dve.wait_ge(counted, 1)
                    link(nc.vector.tensor_copy(sums[0:TP, 0], p_tot[0:TP, 0:NT * NE].rearrange("p (t e) -> p t e", e=NE)))
                    cur = 0
                    step = 1
                    while step < NT:
                        new = 1 - cur
                        link(nc.vector.tensor_copy(sums[0:TP, new, 0:step], sums[0:TP, cur, 0:step]))
                        link(nc.vector.tensor_tensor(sums[0:TP, new, step:NT], sums[0:TP, cur, step:NT], sums[0:TP, cur, 0:NT - step], ALU.add))
                        cur, step = new, step * 2
                    link(nc.vector.tensor_tensor(blocks[0:TP], sums[0:TP, cur, NT - 1].to_broadcast([TP, NE, NT]), iota128[0:TP], ALU.is_gt))
                    link(nc.vector.tensor_reduce(nblk[0:TP, 0], blocks[0:TP], AX.X, ALU.add))
                    link(nc.vector.memset(nblk[0:TP, 1], 0.0))
                    for e in range(1, NE):
                        link(nc.vector.tensor_tensor(nblk[0:TP, 1, e:e + 1], nblk[0:TP, 1, e - 1:e], nblk[0:TP, 0, e - 1:e], ALU.add))
                    link(nc.vector.tensor_scalar(nblk[0:TP, 2], nblk[0:TP, 1], float(SLOT), None, ALU.mult))
                    link(nc.vector.tensor_tensor(place[0:TP], p_pre[0:TP, 0:NT * NE].rearrange("p (t e) -> p t e", e=NE),
                                                 nblk[0:TP, 2:3, :].to_broadcast([TP, NT, NE]), ALU.add))
                    link(nc.vector.tensor_tensor(place[0:TP, 1:NT], place[0:TP, 1:NT], sums[0:TP, cur, 0:NT - 1], ALU.add))
                    for c in range(2):
                        link(nc.vector.tensor_tensor(sums[0:TP, 2], place[0:TP], one[0:TP, c], ALU.mult))
                        link(nc.vector.tensor_reduce(s25[0:TP, 3], sums[0:TP, 2], AX.X, ALU.add))
                        link(nc.vector.tensor_copy(pos[0:TP, c], s25[0:TP, 3]))
                    link(nc.vector.tensor_tensor(eb[:], nblk[0:1, 1:2, 1:NE].to_broadcast([1, NBLK, NE - 1]), iotab[:], ALU.is_le))
                    link(nc.vector.tensor_reduce(ebs[:], eb[:], AX.X, ALU.add))
                    nc.vector.tensor_copy(expert[:], ebs[:]).then_inc(placed_at, 1)

                @block.scalar
                def _(act):
                    def tile(t, par_, earlier):
                        for n in range(norms):
                            act.wait_ge(square_ready, t * norms + n + 1)
                            nc.scalar.activation(work[0:TP, 8:9], work[0:TP, 7:8], ACT.Sqrt, bias=scales[0:TP, 3:4]).then_inc(rooted, 1)
                        act.wait_ge(turned, t + 1)
                        nc.scalar.copy(tok[0:TP, bass.ds(t, 1), :].rearrange("p a d -> p (a d)"), ht[0:TP, par_]).then_inc(tT_made, 1)
                        nc.scalar.copy(tT[:, :, 0:TP], p_turn[:, :, 0:TP]).then_inc(tT_made, 1)
                        act.wait_ge(log_done, t + 1)
                        nc.scalar.copy(logit[0:TP, bass.ds(t, 1), :].rearrange("p a d -> p (a d)"), p_log[0:TP, 0:NE]).then_inc(log_made, 1)

                    for_tiles(act, tile)
                    act.wait_ge(shifted, 1)
                    if layer == 0:
                        nc.scalar.activation(s25[0:TP, 1], s25[0:TP, 0], ACT.Exp).then_inc(expd, 1)
                    else:
                        nc.scalar.activation(logit[0:TP], logit[0:TP], ACT.Exp).then_inc(expd, 1)

                @block.tensor
                def _(pe):
                    pe.wait_ge(r_in, 32 + 16 * (layer == 0))

                    def tile(t, par_, earlier):
                        pe.wait_ge(tok_made, t + 1)
                        for k in range(KD):
                            mm = nc.tensor.transpose(p_turn[:, k, 0:TP], ht[0:TP, par_, k * 128:(k + 1) * 128], ident[0:TP, 0:TP])
                        mm.then_inc(turned, 1)
                        pe.wait_ge(tT_made, 2 * t + 2)
                        for k in range(KD):
                            nc.tensor.matmul(p_log[0:TP, 0:NE], tT[:, k, 0:TP], wr[:, k, :], start=(k == 0), stop=False)
                        nc.tensor.matmul(p_log[0:TP, 0:NE], ones[0:1, 0:TP], br[:], start=False, stop=True).then_inc(log_done, 1)

                    for_tiles(pe, tile)
                    pe.wait_ge(ones_made, 1)
                    flat = one[0:TP, 2].rearrange("p t e -> p (t e)")
                    nc.tensor.matmul(p_pre[0:TP, 0:NT * NE], before[0:TP, 0:TP], flat, start=True, stop=True)
                    nc.tensor.matmul(p_tot[0:TP, 0:NT * NE], ones[0:TP, 0:TP], flat, start=True, stop=True).then_inc(counted, 1)

        with ExitStack() as ctx2:
            def sb2(name, shape, dt):
                return ctx2.enter_context(nc.sbuf_tensor(f"f{layer}_{name}", shape, dt))

            def ps(name, shape):
                return ctx2.enter_context(nc.psum_tensor(f"f{layer}_{name}", shape, F32))

            def sem2(name):
                return ctx2.enter_context(nc.semaphore(f"f{layer}_{name}"))

            xt = sb2("xt", [128, 2, D], F32)
            xT = sb2("xT", [128, 2, KD, 128], F32)
            hb = sb2("hb", [128, 2, hidden], F32)
            hT = sb2("hT", [128, 2, KH, 128], F32)
            yt = sb2("yt", [128, 2, D], F32)
            p_x = ps("p_x", [128, BANK])
            p_h = ps("p_h", [128, 2, BANK])
            p_t = ps("p_t", [128, 2, BANK])
            p_y = ps("p_y", [128, 2, BANK])
            x_in = [sem2("x_in0"), sem2("x_in1")]
            x_turned = sem2("x_turned")
            xT_made = sem2("xT_made")
            h_done = sem2("h_done")
            h_biased = sem2("h_biased")
            h_made = sem2("h_made")
            h_turned = sem2("h_turned")
            hT_made = sem2("hT_made")
            y_done = sem2("y_done")
            y_made = sem2("y_made")
            y_out = [pool_sem(f"f{layer}_y_out{n}") for n in range(2)]

            with nc.Block() as block:
                @block.sync
                def _(sp):
                    def blk(b, p, earlier):
                        if not isinstance(b, int) or b >= 2:
                            sp.wait_ge(x_turned, b - 1)
                        sp.dma_start(xt[:, p], dram_x[bass.ds(b * SLOT, SLOT), :]).then_inc(x_in[p], 16)

                    for_tiles(sp, blk, NBLK)

                @block.tensor
                def _(pe):
                    pe.wait_ge(w_in, 64)

                    def turn_x(b, p, earlier):
                        pe.wait_ge(x_in[p], earlier * 16 + 16)
                        if not isinstance(b, int) or b >= 1:
                            pe.wait_ge(xT_made, b)
                        for k in range(KD):
                            mm = nc.tensor.transpose(p_x[:, k * 128:(k + 1) * 128], xt[:, p, k * 128:(k + 1) * 128], ident[:])
                        mm.then_inc(x_turned, 1)

                    def up(b, p):
                        e = pe.value_load(expert[0:1, bass.ds(b, 1)], min_val=0, max_val=NE - 1)
                        pe.wait_ge(xT_made, b + 1)
                        if not isinstance(b, int) or b >= 2:
                            pe.wait_ge(h_biased, b - 1)
                        for k in range(KD):
                            mm = nc.tensor.matmul(p_h[:, p, 0:hidden], xT[:, p, k, :],
                                                  w1[:, bass.ds(e, 1), k, :].rearrange("p a h -> p (a h)"), start=(k == 0), stop=(k == KD - 1))
                        mm.then_inc(h_done, 1)

                    def turn_h(b, p):
                        pe.wait_ge(h_made, b + 1)
                        if not isinstance(b, int) or b >= 2:
                            pe.wait_ge(hT_made, b - 1)
                        for k in range(KH):
                            mm = nc.tensor.transpose(p_t[:, p, k * 128:(k + 1) * 128], hb[:, p, k * 128:(k + 1) * 128], ident[:])
                        mm.then_inc(h_turned, 1)

                    def down(b, p):
                        e = pe.value_load(expert[0:1, bass.ds(b, 1)], min_val=0, max_val=NE - 1)
                        pe.wait_ge(hT_made, b + 1)
                        if not isinstance(b, int) or b >= 2:
                            pe.wait_ge(y_made, b - 1)
                        for k in range(KH):
                            mm = nc.tensor.matmul(p_y[:, p, 0:D], hT[:, p, k, :],
                                                  w2[:, bass.ds(e, 1), k, :].rearrange("p a h -> p (a h)"), start=(k == 0), stop=(k == KH - 1))
                        mm.then_inc(y_done, 1)

                    def blk(b, p, earlier):
                        turn_x(b, p, earlier)
                        if not isinstance(b, int) or b >= 1:
                            turn_h(b - 1, 1 - p)
                        up(b, p)
                        if not isinstance(b, int) or b >= 1:
                            down(b - 1, 1 - p)

                    for_tiles(pe, blk, NBLK)
                    turn_h(NBLK - 1, (NBLK - 1) % 2)
                    down(NBLK - 1, (NBLK - 1) % 2)

                @block.scalar
                def _(act):
                    def gelu(b, p):
                        act.wait_ge(h_biased, b + 1)
                        nc.scalar.activation(hb[:, p], hb[:, p], ACT.Gelu).then_inc(h_made, 1)

                    def blk(b, p, earlier):
                        act.wait_ge(x_turned, b + 1)
                        if not isinstance(b, int) or b >= 2:
                            act.wait_ge(h_done, b - 1)
                        nc.scalar.copy(xT[:, p].rearrange("p k n -> p (k n)"), p_x[:, 0:D]).then_inc(xT_made, 1)
                        gelu(b, p)

                    for_tiles(act, blk, NBLK)

                @block.vector
                def _(dve):
                    def bias_h(b, p):
                        e = dve.value_load(expert[0:1, bass.ds(b, 1)], min_val=0, max_val=NE - 1)
                        dve.wait_ge(h_done, b + 1)
                        if not isinstance(b, int) or b >= 2:
                            dve.wait_ge(h_turned, b - 1)
                        nc.vector.tensor_tensor(hb[:, p], p_h[:, p, 0:hidden], b1[:, bass.ds(e, 1), :].rearrange("p a h -> p (a h)"),
                                                ALU.add).then_inc(h_biased, 1)

                    def copy_h(b, p):
                        dve.wait_ge(h_turned, b + 1)
                        if not isinstance(b, int) or b >= 2:
                            dve.wait_ge(y_done, b - 1)
                        nc.vector.tensor_copy(hT[:, p].rearrange("p k n -> p (k n)"), p_t[:, p, 0:hidden]).then_inc(hT_made, 1)

                    def bias_y(b, p, earlier):
                        e = dve.value_load(expert[0:1, bass.ds(b, 1)], min_val=0, max_val=NE - 1)
                        dve.wait_ge(y_done, b + 1)
                        if not isinstance(earlier, int) or earlier:
                            dve.wait_ge(y_out[p], earlier * 16)
                        nc.vector.tensor_tensor(yt[:, p], p_y[:, p, 0:D], b2[:, bass.ds(e, 1), :].rearrange("p a h -> p (a h)"),
                                                ALU.add).then_inc(y_made, 1)

                    def blk(b, p, earlier):
                        if not isinstance(b, int) or b >= 1:
                            copy_h(b - 1, 1 - p)
                        bias_h(b, p)
                        if not isinstance(b, int) or b >= 1:
                            bias_y(b - 1, 1 - p, earlier if p == 1 else earlier - 1)

                    dve.wait_ge(w_in, 64)
                    for_tiles(dve, blk, NBLK)
                    copy_h(NBLK - 1, (NBLK - 1) % 2)
                    bias_y(NBLK - 1, (NBLK - 1) % 2, (NBLK - 1) // 2)

                @block.gpsimd
                def _(pool):
                    def blk(b, p, earlier):
                        pool.wait_ge(y_made, b + 1)
                        pool.dma_start(dram_y[bass.ds(b * SLOT, SLOT), :], yt[:, p]).then_inc(y_out[p], 16)

                    for_tiles(pool, blk, NBLK)
                    pool.wait_ge(y_out[0], 16 * ((NBLK + 1) // 2))
                    pool.wait_ge(y_out[1], 16 * (NBLK // 2))

        with ExitStack() as ctx2:
            GB = 4
            got = ctx2.enter_context(nc.sbuf_tensor(f"c{layer}_got", [128, GB, 2, D], F32))
            got_in = [pool_sem(f"c{layer}_got_in{i}") for i in range(GB)]
            added = ctx2.enter_context(nc.semaphore(f"c{layer}_added"))
            with nc.Block() as block:
                @block.gpsimd
                def _(pool):
                    for t in range(NT):
                        if t >= GB:
                            pool.wait_ge(added, (t - GB) * 3 + 3)
                        for c in range(2):
                            pool.indirect_dma_start(got[0:TP, t % GB, c, :], None, dram_y[:, :],
                                                    bass.IndirectOffsetOnAxis(ap=pos[0:TP, c, t:t + 1], axis=0)).then_inc(got_in[t % GB], 16)

                @block.vector
                def _(dve):
                    for t in range(NT):
                        if layer == 1:
                            nc.vector.tensor_tensor(xs[0:TP, t], xs[0:TP, t], tok[0:TP, t], ALU.add).then_inc(added, 1)
                        else:
                            dve.sem_inc(added, 1)
                        dve.wait_ge(added, t * 3 + 1)
                        dve.wait_ge(got_in[t % GB], (t // GB) * 32 + 32)
                        for c in range(2):
                            nc.vector.scalar_tensor_tensor(out=xs[0:TP, t], in0=got[0:TP, t % GB, c], scalar=weight[0:TP, c, t:t + 1],
                                                           in1=xs[0:TP, t], op0=ALU.mult, op1=ALU.add).then_inc(added, 1)
                            dve.wait_ge(added, t * 3 + c + 2)


ZS = 1024.0
YROOM = 2048.0
ROWS, COLS, A_ROWS, A_COLS, T_ROWS, T_COLS = range(6)
IN_DEG = (COLS, ROWS, T_COLS, A_COLS, T_ROWS, A_ROWS)
OUT_DEG = (ROWS, COLS, A_ROWS, A_COLS, T_ROWS, T_COLS)


def graph_convolution(nc, xs, gw, gbias, dram, ident, ones, deg, scales):
    with ExitStack() as ctx:
        def sb(name, shape, dt):
            return ctx.enter_context(nc.sbuf_tensor(name, shape, dt))

        xl = sb("xl", [128, NT, D], F32)
        roots = sb("roots", [128, 2, 6, NT], F32)
        both = sb("both", [128, 2, NT], F32)

        with ExitStack() as ctx2:
            def sb2(name, shape, dt):
                return ctx2.enter_context(nc.sbuf_tensor(name, shape, dt))

            def sem(name):
                return ctx2.enter_context(nc.semaphore(name))

            strip = sb2("d_strip", [128, 2, NT, TP], F16)
            vdeg = sb2("d_vdeg", [128, NT, 4], F16)
            work = sb2("d_work", [128, 16], F32)
            big = sb2("d_big", [128, 6, NT], F32)
            pos = sb2("d_pos", [128, 6, NT], F32)
            inv = sb2("d_inv", [128, 6, NT], F32)
            mx = sb2("d_mx", [128, 1], F32)
            mrow = sb2("d_mrow", [1, 4], F32)
            p_deg = ctx2.enter_context(nc.psum_tensor("p_deg", [128, 2, BANK], F32))
            p_mx = ctx2.enter_context(nc.psum_tensor("p_mx", [128, BANK], F32))
            strip_in = [sem("d_strip_in0"), sem("d_strip_in1")]
            vdeg_made = sem("vdeg_made")
            deg_done = sem("deg_done")
            deg_made = sem("deg_made")
            chain = sem("d_chain")
            passed = sem("d_passed")
            square_ready = sem("d_square_ready")
            rooted = sem("d_rooted")
            max_made = sem("max_made")
            max_turned = sem("max_turned")
            max_row = sem("max_row")
            max_all = sem("max_all")
            big_made = sem("big_made")
            big_rooted = sem("big_rooted")
            with nc.Block() as block:
                @block.sync
                def _(sp):
                    def tile(t, par, before):
                        if not isinstance(t, int) or t >= 2:
                            sp.wait_ge(deg_done, t - 1)
                        sp.dma_start(strip[:, par], dram.adj[bass.ds(t, 1)].rearrange("a r k c -> r (a k) c")).then_inc(strip_in[par], 16)

                    for_tiles(sp, tile)

                @block.tensor
                def _(pe):
                    pe.wait_ge(vdeg_made, 2)

                    def tile(t, par, before):
                        pe.wait_ge(strip_in[par], before * 16 + 16)
                        if not isinstance(t, int) or t >= 2:
                            pe.wait_ge(deg_made, t - 1)
                        for rt in range(NT):
                            mm = nc.tensor.matmul(p_deg[0:TP, par, 0:4], strip[0:TP, par, rt, :], vdeg[0:TP, rt, :],
                                                  start=(rt == 0), stop=(rt == NT - 1))
                        mm.then_inc(deg_done, 1)

                    for_tiles(pe, tile)
                    pe.wait_ge(max_made, 1)
                    nc.tensor.transpose(p_mx[0:1, 0:TP], mx[0:TP, 0:1], ident[0:TP, 0:TP]).then_inc(max_turned, 1)
                    pe.wait_ge(max_row, 1)
                    nc.tensor.matmul(p_mx[0:TP, 128:130], ones[0:1, 0:TP], mrow[:, 1:3], start=True, stop=True).then_inc(max_all, 1)

                @block.scalar
                def _(act):
                    def tile(t, par, before):
                        act.wait_ge(square_ready, t + 1)
                        nc.scalar.activation(work[0:TP, 8:9], work[0:TP, 7:8], ACT.Sqrt, bias=scales[0:TP, 3:4]).then_inc(rooted, 1)

                    for_tiles(act, tile)
                    act.wait_ge(big_made, 1)
                    nc.scalar.activation(big[0:TP], big[0:TP], ACT.Sqrt).then_inc(big_rooted, 1)

                @block.vector
                def _(dve):
                    link = Chain(dve, chain, passed)
                    nc.vector.tensor_copy(vdeg[0:TP, :, 0:2], deg[0:TP, :, 0:2]).then_inc(vdeg_made, 1)
                    dve.wait_ge(vdeg_made, 1)
                    nc.vector.tensor_tensor(vdeg[0:TP, :, 2:4], deg[0:TP, :, 0:2], vdeg[0:TP, :, 0:2], ALU.subtract).then_inc(vdeg_made, 1)

                    def tile(t, par, before):
                        link.at(t * 4)
                        layer_norm = layer_norm_dve(nc, dve, link, xs[0:TP, bass.ds(t, 1), :].rearrange("p a d -> p (a d)"),
                                                    xl[0:TP, bass.ds(t, 1), :].rearrange("p a d -> p (a d)"), work, square_ready,
                                                    rooted, t + 1)
                        link(layer_norm)
                        dve.wait_ge(deg_done, t + 1)
                        link(nc.vector.tensor_copy(work[0:TP, 10:12], p_deg[0:TP, par, 0:2]))
                        nc.vector.tensor_tensor(deg[0:TP, bass.ds(t, 1), T_ROWS:T_COLS + 1].rearrange("p a k -> p (a k)"),
                                                work[0:TP, 10:12], p_deg[0:TP, par, 2:4], ALU.add).then_inc(deg_made, 1)

                    for_tiles(dve, tile)
                    link.at(4 * NT)
                    dve.wait_ge(deg_made, NT)
                    nc.vector.tensor_reduce(mx[0:TP], deg[0:TP, :, 0:2], AX.XY, ALU.max).then_inc(max_made, 1)
                    link(nc.vector.tensor_scalar(big[0:TP, 0:2], deg[0:TP, :, 0:2].rearrange("p t k -> p k t"), 1.0, None, ALU.add))
                    link(nc.vector.tensor_copy(big[0:TP, 2:6], deg[0:TP, :, 2:6].rearrange("p t k -> p k t")))
                    link(nc.vector.tensor_scalar(pos[0:TP], big[0:TP], 0.0, None, ALU.is_gt))
                    nc.vector.tensor_scalar(big[0:TP], big[0:TP], 1.0, None, ALU.max).then_inc(big_made, 1)
                    dve.wait_ge(big_rooted, 1)
                    link(nc.vector.reciprocal(inv[0:TP], big[0:TP]))
                    link(nc.vector.tensor_tensor(inv[0:TP], inv[0:TP], pos[0:TP], ALU.mult))
                    dve.wait_ge(max_turned, 1)
                    link(nc.vector.tensor_reduce(mrow[:, 3:4], p_mx[0:1, 0:TP], AX.X, ALU.max))
                    link(nc.vector.tensor_scalar(mrow[:, 2:3], mrow[:, 3:4], 1.0 / YROOM, None, ALU.mult))
                    link(nc.vector.reciprocal(mrow[:, 0:1], mrow[:, 2:3]))
                    nc.vector.tensor_scalar(mrow[:, 1:2], mrow[:, 0:1], 1.0 / ZS, None, ALU.mult).then_inc(max_row, 1)
                    dve.wait_ge(max_all, 1)
                    link(nc.vector.tensor_copy(scales[0:TP, 4:6], p_mx[0:TP, 128:130]))
                    for k in range(6):
                        link(nc.vector.tensor_scalar(roots[0:TP, 0, k], inv[0:TP, IN_DEG[k]], ZS, None, ALU.mult))
                        s = 1.0 / ZS if k < 2 else scales[0:TP, 5:6]
                        link(nc.vector.tensor_scalar(roots[0:TP, 1, k], inv[0:TP, OUT_DEG[k]], s, None, ALU.mult))
                        if k < 2:
                            link(nc.vector.tensor_tensor(both[0:TP, k], inv[0:TP, IN_DEG[k]], inv[0:TP, OUT_DEG[k]], ALU.mult))

        def inner(name, src, ks, ys):
            with ExitStack() as ctx2:
                def sb2(n, shape, dt):
                    return ctx2.enter_context(nc.sbuf_tensor(f"{name}_{n}", shape, dt))

                def sem(n):
                    return ctx2.enter_context(nc.semaphore(f"{name}_{n}"))

                strip = sb2("strip", [128, SR, NT, TP], F16)
                z = sb2("z", [128, NT, 2, 2, D], F16)
                y = sb2("y", [128, SR, 2, 2, D], F16)
                acc = ctx2.enter_context(nc.psum_tensor(f"{name}_acc", [128, SR, BANK], F32))
                strip_in = [sem(f"strip_in{j}") for j in range(SR)]
                hi_made = sem("hi_made")
                lo_made = sem("lo_made")
                sum_done = sem("sum_done")
                y_hi = sem("y_hi")
                y_lo = sem("y_lo")
                y_out = [dram.pool_sem(f"{name}_y_out{j}") for j in range(SR)]
                with nc.Block() as block:
                    @block.sync
                    def _(sp):
                        def tile(t, j, before):
                            if not isinstance(before, int):
                                sp.wait_ge(sum_done, t + (1 - SR))
                            sp.dma_start(strip[:, j], src[bass.ds(t, 1)].rearrange("a r k c -> r (a k) c")).then_inc(strip_in[j], 16)

                        for_ring(sp, tile)

                    @block.tensor
                    def _(pe):
                        pe.wait_ge(lo_made, 2 * NT)

                        def tile(t, j, before):
                            pe.wait_ge(strip_in[j], before * 16 + 16)
                            if not isinstance(before, int):
                                pe.wait_ge(y_lo, t + (1 - SR))
                            for kt in range(NT):
                                for part in range(2):
                                    mm = nc.tensor.matmul(acc[0:TP, j, :], strip[0:TP, j, kt, :],
                                                          z[0:TP, kt, part].rearrange("p k d -> p (k d)"),
                                                          start=(kt == 0 and part == 0), stop=(kt == NT - 1 and part == 1))
                            mm.then_inc(sum_done, 1)

                        for_ring(pe, tile)

                    @block.scalar
                    def _(act):
                        def split(t, j, before):
                            for i, k in enumerate(ks):
                                nc.scalar.activation(z[0:TP, bass.ds(t, 1), 0, i, :].rearrange("p a d -> p (a d)"),
                                                     xl[0:TP, bass.ds(t, 1), :].rearrange("p a d -> p (a d)"), ACT.Copy,
                                                     scale=roots[0:TP, 0, k, bass.ds(t, 1)]).then_inc(hi_made, 1)

                        for_ring(act, split)

                        def tile(t, j, before):
                            act.wait_ge(sum_done, t + 1)
                            if not isinstance(before, int):
                                act.wait_ge(y_out[j], before * 32)
                            nc.scalar.activation(y[0:TP, j, :, 0, :], acc[0:TP, j, :].rearrange("p (k d) -> p k d", k=2), ACT.Copy,
                                                 scale=scales[0:TP, 4:5]).then_inc(y_hi, 1)

                        for_ring(act, tile)

                    @block.vector
                    def _(dve):
                        def split(t, j, before):
                            for i, k in enumerate(ks):
                                dve.wait_ge(hi_made, t * 2 + i + 1)
                                nc.vector.scalar_tensor_tensor(
                                    out=z[0:TP, bass.ds(t, 1), 1, i, :].rearrange("p a d -> p (a d)"),
                                    in0=xl[0:TP, bass.ds(t, 1), :].rearrange("p a d -> p (a d)"), scalar=roots[0:TP, 0, k, bass.ds(t, 1)],
                                    in1=z[0:TP, bass.ds(t, 1), 0, i, :].rearrange("p a d -> p (a d)"), op0=ALU.mult,
                                    op1=ALU.subtract).then_inc(lo_made, 1)

                        for_ring(dve, split)

                        def tile(t, j, before):
                            dve.wait_ge(y_hi, t + 1)
                            nc.vector.scalar_tensor_tensor(out=y[0:TP, j, :, 1, :], in0=acc[0:TP, j, :].rearrange("p (k d) -> p k d", k=2),
                                                           scalar=scales[0:TP, 4:5], in1=y[0:TP, j, :, 0, :], op0=ALU.mult,
                                                           op1=ALU.subtract).then_inc(y_lo, 1)

                        for_ring(dve, tile)

                    @block.gpsimd
                    def _(pool):
                        def tile(t, j, before):
                            pool.wait_ge(y_lo, t + 1)
                            for i in range(2):
                                pool.dma_start(ys[i][bass.ds(t, 1)].rearrange("a p n -> p (a n)"),
                                               y[0:TP, j, i].rearrange("p s d -> p (s d)")).then_inc(y_out[j], 16)

                        for_ring(pool, tile)
                        for j in range(SR):
                            pool.wait_ge(y_out[j], 32 * (NT // SR))

        def outer(name, src, ks, ys):
            with ExitStack() as ctx2:
                def sb2(n, shape, dt):
                    return ctx2.enter_context(nc.sbuf_tensor(f"{name}_{n}", shape, dt))

                def sem(n):
                    return ctx2.enter_context(nc.semaphore(f"{name}_{n}"))

                def ps(n, shape):
                    return ctx2.enter_context(nc.psum_tensor(f"{name}_{n}", shape, F32))

                KD = D // 128
                strip = sb2("strip", [128, SR, NT, TP], F16)
                z = sb2("z", [128, NT, 3, 2, D], F16)
                u = sb2("u", [128, 2, 3, D], F32)
                own = sb2("own", [128, 2, D], F32)
                uT = sb2("uT", [128, 3 * KD, 128], F32)
                w = sb2("w", [128, 3, KD, D], F32)
                b = sb2("b", [3, D], F32)
                acc = ps("acc", [128, 2, 2, BANK])
                turn = ps("turn", [128, 2, BANK])
                p_out = ps("out", [128, 2, BANK])
                strip_in = [sem(f"strip_in{j}") for j in range(SR)]
                z_in = sem("z_in")
                w_in = sem("w_in")
                hi_made = sem("hi_made")
                lo_made = sem("lo_made")
                sum_done = sem("sum_done")
                own_made = sem("own_made")
                u_made = sem("u_made")
                u0_made = sem("u0_made")
                turned = sem("turned")
                uT_made = sem("uT_made")
                out_done = sem("out_done")
                added = sem("added")
                with nc.Block() as block:
                    @block.sync
                    def _(sp):
                        for n, k in enumerate(ks):
                            sp.dma_start(w[:, n], gw[k].rearrange("(k p) o -> p k o", p=128)).then_inc(w_in, 16)
                            sp.dma_start(b[n:n + 1, :], gbias[k:k + 1, :]).then_inc(w_in, 16)
                        for i in range(2):
                            sp.dma_start(z[0:TP, :, i + 1].rearrange("p t s d -> p t (s d)"), ys[i].rearrange("t p n -> p t n")).then_inc(z_in, 16)

                        def tile(t, j, before):
                            if not isinstance(before, int):
                                sp.wait_ge(sum_done, t + (1 - SR))
                            sp.dma_start(strip[:, j], src[bass.ds(t, 1)].rearrange("a r k c -> r (a k) c")).then_inc(strip_in[j], 16)

                        for_ring(sp, tile)

                    @block.tensor
                    def _(pe):
                        pe.wait_ge(z_in, 32)
                        pe.wait_ge(w_in, 96)
                        pe.wait_ge(lo_made, NT)

                        def sums(j, p, kts):
                            for kt in kts:
                                for part in range(2):
                                    for half, (k0, k1) in enumerate(((1, 3), (0, 1))):
                                        mm = nc.tensor.matmul(acc[0:TP, p, half, 0:(k1 - k0) * D].rearrange("p (k d) -> p k d", d=D),
                                                              strip[0:TP, j, kt, :], z[0:TP, kt, k0:k1, part, :],
                                                              start=(kt == 0 and part == 0), stop=(kt == NT - 1 and part == 1))
                            return mm

                        def turn_u(t, p):
                            pe.wait_ge(u_made, t * 2 + 2)
                            pe.wait_ge(u0_made, t + 1)
                            if not isinstance(t, int) or t >= 1:
                                pe.wait_ge(uT_made, t * 2)
                            for n in range(3 * KD):
                                mm = nc.tensor.transpose(turn[:, n // 4, (n % 4) * 128:(n % 4) * 128 + TP],
                                                         u[0:TP, p, n // KD, (n % KD) * 128:(n % KD + 1) * 128], ident[0:TP, 0:TP])
                            mm.then_inc(turned, 1)

                        def weigh(t, p):
                            pe.wait_ge(uT_made, t * 2 + 2)
                            if not isinstance(t, int) or t >= 2:
                                pe.wait_ge(added, t - 1)
                            for n in range(3 * KD):
                                nc.tensor.matmul(p_out[0:TP, p, 0:D], uT[:, n, 0:TP], w[:, n // KD, n % KD, :], start=(n == 0), stop=False)
                            nc.tensor.matmul(p_out[0:TP, p, 0:D], ones[0:3, 0:TP], b[:], start=False, stop=True).then_inc(out_done, 1)

                        def tile(t, j, before, p):
                            pe.wait_ge(strip_in[j], before * 16 + 16)
                            if not isinstance(t, int) or t >= 2:
                                pe.wait_ge(u_made, (t - 1) * 2)
                                pe.wait_ge(u0_made, t - 1)
                            sums(j, p, range(0, 8))
                            if not isinstance(t, int) or t >= 1:
                                turn_u(t - 1, 1 - p)
                            sums(j, p, range(8, 16))
                            if not isinstance(t, int) or t >= 1:
                                weigh(t - 1, 1 - p)
                            sums(j, p, range(16, NT)).then_inc(sum_done, 1)

                        for_ring2(pe, tile)
                        turn_u(NT - 1, (NT - 1) % 2)
                        weigh(NT - 1, (NT - 1) % 2)

                    @block.scalar
                    def _(act):
                        def split(t, j, before):
                            nc.scalar.activation(z[0:TP, bass.ds(t, 1), 0, 0, :].rearrange("p a d -> p (a d)"),
                                                 xl[0:TP, bass.ds(t, 1), :].rearrange("p a d -> p (a d)"), ACT.Copy,
                                                 scale=roots[0:TP, 0, ks[0], bass.ds(t, 1)]).then_inc(hi_made, 1)

                        for_ring(act, split)

                        def copy_turned(t):
                            act.wait_ge(turned, t + 1)
                            if not isinstance(t, int) or t >= 1:
                                act.wait_ge(out_done, t)
                            nc.scalar.copy(uT[:, 0:4, 0:TP], turn[:, 0].rearrange("p (n m) -> p n m", m=128)[:, :, 0:TP]).then_inc(uT_made, 1)
                            nc.scalar.copy(uT[:, 4:6, 0:TP], turn[:, 1, 0:256].rearrange("p (n m) -> p n m", m=128)[:, :, 0:TP]).then_inc(uT_made, 1)

                        def tile(t, j, before, p):
                            if not isinstance(t, int) or t >= 1:
                                copy_turned(t - 1)
                            if not isinstance(t, int) or t >= 2:
                                act.wait_ge(u0_made, t - 1)
                            nc.scalar.activation(own[0:TP, p], xl[0:TP, bass.ds(t, 1), :].rearrange("p a d -> p (a d)"), ACT.Copy,
                                                 scale=both[0:TP, ks[0], bass.ds(t, 1)]).then_inc(own_made, 1)
                            act.wait_ge(sum_done, t + 1)
                            if not isinstance(t, int) or t >= 2:
                                act.wait_ge(turned, t - 1)
                            nc.scalar.activation(u[0:TP, p, 1], acc[0:TP, p, 0, 0:D], ACT.Copy,
                                                 scale=roots[0:TP, 1, ks[1], bass.ds(t, 1)]).then_inc(u_made, 1)
                            nc.scalar.activation(u[0:TP, p, 2], acc[0:TP, p, 0, D:2 * D], ACT.Copy,
                                                 scale=roots[0:TP, 1, ks[2], bass.ds(t, 1)]).then_inc(u_made, 1)

                        for_ring2(act, tile)
                        copy_turned(NT - 1)

                    @block.vector
                    def _(dve):
                        def split(t, j, before):
                            dve.wait_ge(hi_made, t + 1)
                            nc.vector.scalar_tensor_tensor(
                                out=z[0:TP, bass.ds(t, 1), 0, 1, :].rearrange("p a d -> p (a d)"),
                                in0=xl[0:TP, bass.ds(t, 1), :].rearrange("p a d -> p (a d)"), scalar=roots[0:TP, 0, ks[0], bass.ds(t, 1)],
                                in1=z[0:TP, bass.ds(t, 1), 0, 0, :].rearrange("p a d -> p (a d)"), op0=ALU.mult,
                                op1=ALU.subtract).then_inc(lo_made, 1)

                        for_ring(dve, split)

                        def add(t, p):
                            dve.wait_ge(out_done, t + 1)
                            xt = xs[0:TP, bass.ds(t, 1), :].rearrange("p a d -> p (a d)")
                            nc.vector.tensor_tensor(xt, xt, p_out[0:TP, p, 0:D], ALU.add).then_inc(added, 1)

                        def tile(t, j, before, p):
                            dve.wait_ge(own_made, t + 1)
                            dve.wait_ge(sum_done, t + 1)
                            if not isinstance(t, int) or t >= 2:
                                dve.wait_ge(turned, t - 1)
                            nc.vector.scalar_tensor_tensor(out=u[0:TP, p, 0], in0=acc[0:TP, p, 1, 0:D],
                                                           scalar=roots[0:TP, 1, ks[0], bass.ds(t, 1)], in1=own[0:TP, p],
                                                           op0=ALU.mult, op1=ALU.add).then_inc(u0_made, 1)
                            if not isinstance(t, int) or t >= 1:
                                add(t - 1, 1 - p)

                        for_ring2(dve, tile)
                        add(NT - 1, (NT - 1) % 2)

        inner("ia", dram.adj_t, (2, 4), (dram.y[0], dram.y[2]))
        inner("it", dram.adj, (3, 5), (dram.y[1], dram.y[3]))
        outer("oa", dram.adj_t, (0, 2, 3), (dram.y[0], dram.y[1]))
        outer("ot", dram.adj, (1, 4, 5), (dram.y[2], dram.y[3]))


def gnn_and_experts(nc, ap, out):
    with ExitStack() as ctx:
        dram = Scratch(nc, ctx)
        ident, ident16, ones, ones16 = consts(nc, ctx)
        col_part = ctx.enter_context(nc.sbuf_tensor("col_part", [128, NT, NB], F32))
        deg = ctx.enter_context(nc.sbuf_tensor("deg", [128, NT, 6], F32))
        build_adjacency(nc, ap["src"], ap["dst"], dram, ones, col_part)
        transpose_adjacency(nc, dram, ident16, ones16, col_part, deg)
        xs = ctx.enter_context(nc.sbuf_tensor("xs", [128, NT, D], F32))
        scales = ctx.enter_context(nc.sbuf_tensor("scales", [128, 8], F32))
        fill = ctx.enter_context(nc.semaphore("fill"))
        with nc.Block() as block:
            @block.vector
            def _(dve):
                nc.vector.memset(scales[:, 3:4], 1e-5).then_inc(fill, 1)
                dve.wait_ge(fill, 1)
        den = ctx.enter_context(nc.sbuf_tensor("den", [128, NT, HEADS], F32))
        graph_attention(nc, ap["x"], ap["w"], ap["wlr"], ap["wl_rows"], dram, ident, ones, deg, xs, den, scales)
        finish_attention(nc, ap["x"], ap["gat_b"], den, scales, xs)
        mixture(nc, 0, xs, {k[3:]: v for k, v in ap.items() if k.startswith("f0_")}, ident, ones, scales, dram.slot_x, dram.slot_y, 512, dram.pool_sem)
        clear_semaphores(nc)
        graph_convolution(nc, xs, ap["g1_w"], ap["g1_b"], dram, ident, ones, deg, scales)
        clear_semaphores(nc)
        mixture(nc, 1, xs, {k[3:]: v for k, v in ap.items() if k.startswith("f1_")}, ident, ones, scales, dram.slot_x, dram.slot_y, 256, dram.pool_sem)
        stored = ctx.enter_context(nc.semaphore("stored"))
        with nc.Block() as block:
            @block.sync
            def _(sp):
                sp.dma_start(out.rearrange("(t p) d -> p t d", p=TP), xs[0:TP]).then_inc(stored, 16)
                sp.wait_ge(stored, 16)



def lay_out(inputs):
    inputs = {k: np.asarray(v) for k, v in inputs.items()}
    laid = {
        "x": inputs["x"], "src": inputs["src"], "dst": inputs["dst"],
        "w": inputs["L0_gnn_W"],
        "wlr": np.concatenate([inputs["L0_gnn_Wl"], inputs["L0_gnn_Wr"]]).T,
        "gat_b": np.broadcast_to(np.tile(inputs["L0_gnn_b"], HEADS), (TP, D)),
        "f0_gb": np.broadcast_to(np.stack([inputs["L0_ffn_gamma"], inputs["L0_ffn_beta"]]), (TP, 2, D)),
        "f0_wr": inputs["L0_ffn_Wr"], "f0_br": inputs["L0_ffn_br"][None],
        "f0_w1": inputs["L0_ffn_W1"], "f0_w2": inputs["L0_ffn_W2"],
        "f0_b1": np.broadcast_to(inputs["L0_ffn_b1"], (128, NE, 512)),
        "f0_b2": np.broadcast_to(inputs["L0_ffn_b2"], (128, NE, D)),
        "g1_w": inputs["L1_gnn_W"].transpose(0, 2, 1), "g1_b": inputs["L1_gnn_b"],
        "f1_wr": inputs["L1_ffn_router_w"].T, "f1_br": np.zeros((1, NE), np.float32),
        "f1_w1": inputs["L1_ffn_w1"], "f1_w2": inputs["L1_ffn_w2"],
        "f1_b1": np.broadcast_to(inputs["L1_ffn_b1"], (128, NE, D)),
        "f1_b2": np.broadcast_to(inputs["L1_ffn_b2"], (128, NE, D)),
        "wl_rows": np.broadcast_to(inputs["L0_gnn_Wl"].T[:, :, None], (HD, HEADS, TP)),
    }
    return {name: np.ascontiguousarray(a) for name, a in laid.items()}


def kernel(**inputs):
    import concourse.bacc as _bacc
    from concourse.bass_utils import run_bass_kernel_spmd as _run

    nc = _bacc.Bacc("TRN2", target_bir_lowering=False, num_devices=1)
    arrays, ap = {}, {}
    for name, a in lay_out(inputs).items():
        arrays[f"in_{name}"] = a
        ap[name] = nc.dram_tensor(f"in_{name}", a.shape, mybir.dt.from_np(a.dtype), kind="ExternalInput").ap()
    out = nc.dram_tensor("out_0", (N, D), F32, kind="ExternalOutput").ap()
    gnn_and_experts(nc, ap, out)
    r = _run(nc, [arrays], core_ids=[0])
    return r.results[0]["out_0"]
```

```python
from contextlib import ExitStack

import concourse.bass as bass
import concourse.mybir as mybir
import numpy as np

F32 = mybir.dt.float32
F16 = mybir.dt.float16
I32 = mybir.dt.int32
U32 = mybir.dt.uint32
ALU = mybir.AluOpType
ACT = mybir.ActivationFunctionType
AX = mybir.AxisListType

N = 3125
E = 50000
D = 256
TP = 125
NT = N // TP
GT = 5
NG = NT // GT
GW = GT * TP
BANK = 512
BANKS = [(b, min(BANK, N - b)) for b in range(0, N, BANK)]
NB = len(BANKS)
WC = 17
WE = WC * 128
GC = 20
GWIN = E // (GC * TP)
RING = 6
GRING = 5
MID = 1600


def for_tiles(eng, step, n=NT):
    peel = 2 + n % 2
    for t in range(peel):
        step(t, t % 2, t // 2)
    with eng.Fori(0, (n - peel) // 2) as i:
        for j in range(2):
            step(i * 2 + (peel + j), (peel + j) % 2, i + (peel + j) // 2)


SR = 5


def for_ring(eng, step):
    for j in range(SR):
        step(j, j, 0)
    with eng.Fori(1, NT // SR) as g:
        for j in range(SR):
            step(g * SR + j, j, g)


def for_ring2(eng, step):
    for t in range(SR):
        step(t, t, 0, t % 2)
    with eng.Fori(0, (NT - SR) // (2 * SR)) as i:
        for n in range(2 * SR):
            t = SR + n
            step(i * (2 * SR) + t, n % SR, i * 2 + (1 + n // SR), t % 2)


def clear_semaphores(nc):
    nums = sorted(nc.released_uncleared_semaphores)
    with nc.Block() as block:
        @block.gpsimd
        def _(pool):
            first = 0
            for n in range(1, len(nums) + 1):
                if n == len(nums) or nums[n] != nums[n - 1] + 1:
                    pool.sem_clear(range(nums[first], nums[n - 1] + 1))
                    first = n


class Scratch:

    def __init__(self, nc, ctx):
        self.pool_sem = lambda name: ctx.enter_context(nc.semaphore(name))
        self.adj_t = nc.dram_tensor("adj_t", [NT, 128, NT, TP], F16).ap()
        self.slot_x = nc.dram_tensor("slot_x", [NBLK * SLOT, D], F32).ap()
        self.slot_y = nc.dram_tensor("slot_y", [NBLK * SLOT, D], F32).ap()
        self.y = [nc.dram_tensor(f"y{k}", [NT, TP, 2 * D], F16).ap() for k in (2, 3, 4, 5)]
        self.adj = nc.dram_tensor("adj", [NT, 128, NT, TP], F16).ap()


def consts(nc, ctx):
    ident = ctx.enter_context(nc.sbuf_tensor("ident", [128, 128], F32))
    ident16 = ctx.enter_context(nc.sbuf_tensor("ident16", [128, 128], F16))
    ones = ctx.enter_context(nc.sbuf_tensor("ones", [128, 128], F32))
    ones16 = ctx.enter_context(nc.sbuf_tensor("ones16", [128, 1], F16))
    made = ctx.enter_context(nc.semaphore("consts_made"))
    with nc.Block() as block:
        @block.gpsimd
        def _(pool):
            nc.gpsimd.memset(ident[:], 0.0).then_inc(made, 1)
            nc.gpsimd.memset(ident16[:], 0.0).then_inc(made, 1)
            nc.gpsimd.memset(ones[:], 1.0).then_inc(made, 1)
            nc.gpsimd.memset(ones16[:], 1.0).then_inc(made, 1)
            pool.wait_ge(made, 4)
            for m in (ident, ident16):
                nc.gpsimd.affine_select(out=m[:], in_=m[:], compare_op=ALU.not_equal, fill=1.0, base=0,
                                        pattern=[[-1, 128]], channel_multiplier=1).then_inc(made, 1)
            pool.wait_ge(made, 6)
    return ident, ident16, ones, ones16


HEADS = 4
HD = 64
HF = 2 * (HD + 1)
HROOM = 8192.0
EL, ER = 0, HEADS


class Attention:

    def __init__(self, nc, ctx):
        def sb(name, shape, dt):
            return ctx.enter_context(nc.sbuf_tensor(name, shape, dt))

        self.feats = sb("feats", [128, NT, HEADS, 2, HF], F16)
        self.rows = sb("el_rows", [128, HEADS * N], F32)
        self.lr = sb("lr", [128, NT, 2 * HEADS], F32)
        self.ner = sb("ner", [128, NT, HEADS], F32)
        self.pows = sb("pows", [128, 4, NT, HEADS], F32)
        self.vdeg = sb("vdeg", [128, NT, 4], F16)


def prepare(nc, x, w, wlr, wl_rows, src_dst, dst, dram, ident, ident16, ones, col_part, deg, xs, scales, att):
    feats, rows, lr, ner, pows, vdeg = att.feats, att.rows, att.lr, att.ner, att.pows, att.vdeg
    with ExitStack() as ctx:
        def sb(name, shape, dt):
            return ctx.enter_context(nc.sbuf_tensor(name, shape, dt))

        def sem(name):
            return ctx.enter_context(nc.semaphore(name))

        EP = E // TP
        HEAD = 3
        PB = 8
        rounds = [(q, min(PB, NT - q)) for q in range(0, NT, PB)]
        NR = len(rounds)
        TURN_AT = {5: 0, 8: 1, 11: 2, 14: 3}
        iota_r = sb("iota_r", [128, N], F16)
        iota_c = sb("iota_c", [128, TP], F16)
        cnt = sb("cnt", [128, NT + 2], F32)
        off_i = sb("off_i", [1, NT], I32)
        flag_i = sb("flag_i", [1, 1], I32)
        tile_base = sb("tile_base", [128, NT], F32)
        win_buf = sb("win", [128, NT * 2 * WC], I32)
        gwin = sb("gwin", [128, 2, GC], I32)
        gloc = sb("gloc", [128, 2, GC], F32)
        hot_c = sb("hot_c", [128, RING, TP], F16)
        hot_r = sb("hot_r", [128, RING, N], F16)
        zeros = sb("zeros", [128, TP], F16)
        strip = sb("strip", [128, 2, N], F16)
        turned = sb("turned", [128, 2, NT, TP], F16)
        tile_sum = sb("tile_sum", [128, 2, NT], F32)
        row_sum = sb("row_sum", [128, NT], F32)
        w_sb = sb("w_sb", [128, 2, HD], F32)
        wlr_sb = sb("wlr_sb", [HD, 2 * HEADS], F32)
        wl_sb = sb("wl_sb", [HD, HEADS, TP], F32)
        mx = sb("mx", [128, 4], F32)
        mrow = sb("mrow", [1, 8], F32)
        win = win_buf[:].rearrange("p (t s k) -> p t s k", s=2, k=WC)
        dst_a, dst_b = win_buf[:, 0:EP], win_buf[:, EP:2 * EP]
        h_all = rows[:, 0:NT * D].rearrange("p (t d) -> p t d", d=D)
        at = NT * D
        hT = rows[:, at:at + SR * 256].rearrange("p (j k n) -> p j k n", j=SR, k=2)
        at += SR * 256
        dst_f = rows[:, at:at + EP]
        less = rows[:, at + EP:at + 3 * EP].rearrange("p (i k) -> p i k", i=2)
        at += 3 * EP
        stats = rows[:, at:at + NT * 6].rearrange("p (t k) -> p t k", k=6)
        norm = rows[:, at + NT * 6:at + NT * 10].rearrange("p (i t k) -> p i t k", i=2, k=2)
        at += NT * 10
        row = rows[0:1, at:at + 8 * (NT + 2)].rearrange("p (i k) -> p i k", i=8)
        xs_flat = xs[:].rearrange("p t d -> p (t d)")
        f = xs_flat[0:TP, 0:NT * (HD + 1)].rearrange("p (t d) -> p t d", d=HD + 1)
        xw = xs_flat[0:TP, NT * (HD + 1):NT * (2 * HD + 1)].rearrange("p (t d) -> p t d", d=HD)
        xwT = xs_flat[0:HD, NT * (2 * HD + 1):NT * (2 * HD + 1) + N]
        loc_at = NT * (2 * HD + 1)
        loc_src, loc_dst = (xs_flat[:, loc_at + i * NT * WC:loc_at + (i + 1) * NT * WC].rearrange("p (t k) -> p t k", k=WC) for i in range(2))
        acc = ctx.enter_context(nc.psum_tensor("acc", [128, NB, BANK], F32))
        turn = ctx.enter_context(nc.psum_tensor("turn", [128, PB, 128], F16))
        small = acc[:, NB - 1, :]
        XWT, XW = 2 * 128, 3 * 128
        LR, MX, SC = 0, 256, 208

        edges_in = sem("edges_in")
        x_in = sem("x_in")
        w_in = sem("w_in")
        iotas = sem("iotas")
        dve_chain = sem("dve_chain")
        counted = sem("counted")
        summed = sem("summed")
        offsets = sem("offsets")
        windows_in = sem("windows_in")
        stats_made = sem("stats_made")
        norm_made = sem("norm_made")
        rooted = sem("rooted")
        h_made = sem("h_made")
        h_turned = sem("h_turned")
        hT_made = sem("hT_made")
        xw_done = sem("xw_done")
        xw_made = sem("xw_made")
        lr_done = sem("lr_done")
        lr_made = sem("lr_made")
        rows_done = sem("rows_done")
        rows_made = sem("rows_made")
        pows_made = sem("pows_made")
        maxima = sem("maxima")
        maxima_row = sem("maxima_row")
        scale_row = sem("scale_row")
        scale_all = sem("scale_all")
        scaled = sem("scaled")
        feat_chain = sem("feat_chain")
        local = sem("local")
        cleared = sem("cleared")
        hot_ready = sem("hot_ready")
        hot_used = sem("hot_used")
        bank_done = sem("bank_done")
        bank_free = sem("bank_free")
        strip_out = [sem("strip_out0"), sem("strip_out1")]
        turn_done = sem("turn_done")
        turn_free = sem("turn_free")
        turned_out = [sem("turned_out0"), sem("turned_out1")]
        summed_rows = sem("summed_rows")
        gwin_in = sem("gwin_in")
        gwin_used = sem("gwin_used")
        ghot_ready = sem("ghot_ready")
        ghot_used = sem("ghot_used")
        slots_seen = sem("slots_seen")

        with nc.Block() as block:
            @block.sync
            def _(sp):
                last = (TP - 1) * EP
                sp.dma_start(dst_a[0:TP, :], dst.rearrange("(p k) -> p k", k=EP)).then_inc(edges_in, 16)
                sp.dma_start(dst_b[0:TP - 1, :], dst[1:last + 1].rearrange("(p k) -> p k", k=EP)).then_inc(edges_in, 16)
                sp.dma_start(dst_b[TP - 1:TP, 0:EP - 1], dst[last + 1:E].rearrange("(p k) -> p k", p=1)).then_inc(edges_in, 16)
                sp.dma_start(dst_b[TP - 1:TP, EP - 1:EP], dst[E - 1:E].rearrange("(p k) -> p k", p=1)).then_inc(edges_in, 16)
                sp.dma_start(xs[0:TP], x.rearrange("(t p) d -> p t d", p=TP)).then_inc(x_in, 16)
                sp.dma_start(w_sb[:], w.rearrange("(k p) n -> p k n", k=2)).then_inc(w_in, 16)
                sp.dma_start(wlr_sb[:], wlr).then_inc(w_in, 16)
                sp.dma_start(wl_sb[:], wl_rows).then_inc(w_in, 16)
                sp.wait_ge(offsets, 1)
                with sp.Fori(0, NT) as t:
                    off = sp.value_load(off_i[0:1, bass.ds(t, 1)], min_val=0, max_val=E - WE)
                    sp.dma_start(win[:, bass.ds(t, 1), :, :].rearrange("p a s k -> p (a s) k"),
                                 src_dst[:, bass.ds(off, WE)].rearrange("s (p k) -> p s k", k=WC)).then_inc(windows_in, 16)
                general = sp.value_load(flag_i[0:1, 0:1], min_val=0, max_val=1)

                def store_turned(t, par):
                    sp.wait_ge(turn_free, (t + 1) * NR)
                    sp.dma_start(dram.adj[bass.ds(t, 1)].rearrange("a r k c -> r (a k) c"), turned[:, par]).then_inc(turned_out[par], 16)

                def tile(t, par, before):
                    with sp.If(general):
                        with sp.Fori(0, GWIN) as g:
                            sp.wait_ge(gwin_used, (t * GWIN + g) * 2 + 1)
                            first = g * (GC * TP)
                            for i in range(2):
                                sp.dma_start(gwin[0:TP, i, :], src_dst[i, bass.ds(first, GC * TP)].rearrange("(p k) -> p k", k=GC)).then_inc(gwin_in, 16)
                    sp.wait_ge(bank_free, (t + 2) * NB)
                    sp.dma_start(dram.adj_t[:, :, bass.ds(t, 1), :].rearrange("g c a r -> c g (a r)"),
                                 strip[:, par, :].rearrange("c (g r) -> c g r", g=NT)).then_inc(strip_out[par], 16)
                    if not isinstance(t, int) or t >= 1:
                        store_turned(t - 1, 1 - par)

                for_tiles(sp, tile)
                store_turned(NT - 1, (NT - 1) % 2)
                for out in (strip_out, turned_out):
                    sp.wait_ge(out[0], 16 * (NT // 2 + 1))
                    sp.wait_ge(out[1], 16 * (NT // 2))

            @block.gpsimd
            def _(pool):
                nc.gpsimd.iota(iota_r[:], [[1, N]], base=-MID, channel_multiplier=0,
                               allow_small_or_imprecise_dtypes=True).then_inc(iotas, 1)
                nc.gpsimd.iota(iota_c[:], [[1, TP]], base=0, channel_multiplier=0,
                               allow_small_or_imprecise_dtypes=True).then_inc(iotas, 1)
                nc.gpsimd.iota(tile_base[:], [[TP, NT]], base=0, channel_multiplier=0,
                               allow_small_or_imprecise_dtypes=True).then_inc(iotas, 1)
                nc.gpsimd.memset(zeros[:], 0.0).then_inc(cleared, 1)
                nc.gpsimd.memset(strip[:], 0.0).then_inc(cleared, 1)
                nc.gpsimd.memset(turned[:], 0.0).then_inc(cleared, 1)
                nc.gpsimd.memset(row_sum[:], 0.0).then_inc(cleared, 1)
                link = Chain(pool, feat_chain)
                pool.wait_ge(scaled, 1)
                for n in range(2 * HEADS):
                    h, kind = n // 2, n % 2
                    p = pows[0:TP, 2 + kind, :, h:h + 1]
                    o = kind * (HD + 1)
                    hi = feats[0:TP, :, h, 0, o:o + HD + 1]
                    link(nc.gpsimd.tensor_copy(f[:, :, HD:HD + 1], p))
                    link(nc.gpsimd.tensor_tensor(f[:, :, 0:HD], xw, p.to_broadcast([TP, NT, HD]), ALU.mult))
                    link(nc.gpsimd.tensor_copy(hi, f))
                    link(nc.gpsimd.tensor_tensor(feats[0:TP, :, h, 1, o:o + HD + 1], f, hi, ALU.subtract))

            @block.vector
            def _(dve):
                link = Chain(dve, dve_chain)

                dve.wait_ge(edges_in, 64)
                link(nc.vector.tensor_copy(dst_f[0:TP, :], dst_a[0:TP, :]))
                link(nc.vector.memset(cnt[:], 0.0))
                for t in range(1, NT + 1):
                    if t >= 3:
                        dve.wait_ge(dve_chain, t)
                    link.count += 1
                    nc.vector.tensor_scalar(less[0:TP, t % 2, :], dst_f[0:TP, :], float(TP * t), 0.0, ALU.is_lt,
                                            ALU.add, accum_out=cnt[0:TP, t:t + 1]).then_inc(dve_chain, 1)
                dve.wait_ge(dve_chain, link.count)
                link(nc.vector.tensor_tensor(less[0:TP, 0, :], dst_a[0:TP, :], dst_b[0:TP, :], ALU.is_gt))
                nc.vector.tensor_reduce(cnt[0:TP, NT + 1:NT + 2], less[0:TP, 0, :], AX.X, ALU.add).then_inc(counted, 1)
                dve.wait_ge(summed, 1)
                link(nc.vector.tensor_copy(row[:, 0, :], small[0:1, 0:NT + 2]))
                link(nc.vector.tensor_tensor(row[:, 1, 0:NT], row[:, 0, 1:NT + 1], row[:, 0, 0:NT], ALU.subtract))
                link(nc.vector.tensor_scalar(row[:, 2, 0:NT], row[:, 1, 0:NT], float(WE), None, ALU.is_gt))
                link(nc.vector.tensor_reduce(row[:, 3, 0:1], row[:, 2, 0:NT], AX.X, ALU.add))
                link(nc.vector.tensor_tensor(row[:, 4, 0:1], row[:, 3, 0:1], row[:, 0, NT + 1:NT + 2], ALU.add))
                link(nc.vector.tensor_scalar(flag_i[:], row[:, 4, 0:1], 0.5, None, ALU.is_gt))
                nc.vector.tensor_scalar(off_i[:], row[:, 0, 0:NT], float(E - WE), None, ALU.min).then_inc(offsets, 1)

                dve.wait_ge(x_in, 16)
                layer_norm_all(nc, dve, link, xs, h_all, stats, norm, stats_made, norm_made, rooted, h_made)

                dve.wait_ge(lr_done, 1)
                nc.vector.tensor_copy(lr[0:TP].rearrange("p t k -> p (t k)"), small[0:TP, LR:LR + NT * 2 * HEADS]).then_inc(lr_made, 1)
                dve.wait_ge(lr_made, 1)
                link(nc.vector.tensor_scalar(ner[0:TP], lr[0:TP, :, ER:ER + HEADS], -1.0, None, ALU.mult))
                dve.wait_ge(xw_made, 2 * NT)
                link(nc.vector.tensor_reduce(mx[0:TP, 0:1], xw, AX.XY, ALU.max, apply_absolute_value=True))
                dve.wait_ge(pows_made, 4)
                nc.vector.tensor_reduce(mx[0:TP, 1:2], pows[0:TP, 2:4], AX.XYZ, ALU.max).then_inc(maxima, 1)
                dve.wait_ge(maxima_row, 1)
                link(nc.vector.tensor_reduce(mrow[:, 0:2], small[0:1, MX:MX + 256].rearrange("p (k n) -> p k n", k=2)[:, :, 0:TP], AX.X, ALU.max))
                link(nc.vector.tensor_scalar(mrow[:, 2:3], mrow[:, 0:1], 1.0, None, ALU.max))
                link(nc.vector.tensor_tensor(mrow[:, 3:4], mrow[:, 2:3], mrow[:, 1:2], ALU.mult))
                link(nc.vector.tensor_scalar(mrow[:, 5:6], mrow[:, 3:4], 1.0 / HROOM, None, ALU.mult))
                nc.vector.reciprocal(mrow[:, 4:5], mrow[:, 5:6]).then_inc(scale_row, 1)
                dve.wait_ge(scale_all, 1)
                link(nc.vector.tensor_copy(scales[0:TP, 0:2], small[0:TP, SC:SC + 2]))
                nc.vector.tensor_scalar(pows[0:TP, 2:4], pows[0:TP, 2:4], scales[0:TP, 0:1], None, ALU.mult).then_inc(scaled, 1)

                dve.wait_ge(iotas, 3)
                dve.wait_ge(windows_in, 16 * NT)
                dve.wait_ge(rows_done, HEADS * NB)
                nc.vector.tensor_scalar(loc_src[:], win[:, :, 0, :], float(MID), None, ALU.subtract).then_inc(local, 1)
                nc.vector.tensor_tensor(loc_dst[:], win[:, :, 1, :], tile_base[:].to_broadcast([128, NT, WC]), ALU.subtract).then_inc(local, 1)
                dve.wait_ge(local, 2)
                general = dve.value_load(flag_i[0:1, 0:1], min_val=0, max_val=1)
                dve.sem_inc(gwin_used, 1)
                dve.wait_ge(cleared, 4)

                def chunk(ready, rows_, slot, c_of_edge, r_of_edge):
                    nc.vector.tensor_scalar(hot_c[0:rows_, slot, :], iota_c[0:rows_, :], c_of_edge, None,
                                            ALU.is_equal).then_inc(ready, 1)
                    nc.vector.tensor_scalar(hot_r[0:rows_, slot, :], iota_r[0:rows_, :], r_of_edge, None,
                                            ALU.is_equal).then_inc(ready, 1)

                def sum_rows(t, par):
                    dve.wait_ge(turn_free, (t + 1) * NR)
                    if not isinstance(t, int) or t >= 2:
                        dve.wait_ge(summed_rows, (t - 1) * 2)
                    nc.vector.tensor_reduce(tile_sum[0:TP, par], turned[0:TP, par], AX.X, ALU.add).then_inc(summed_rows, 1)
                    dve.wait_ge(summed_rows, t * 2 + 1)
                    nc.vector.tensor_tensor(row_sum[0:TP], row_sum[0:TP], tile_sum[0:TP, par], ALU.add).then_inc(summed_rows, 1)

                def tile(t, par, before):
                    for k in range(WC):
                        dve.wait_ge(hot_used, t * WC + k + 1 + (k < WC % RING and WC % RING > 0 and RING - WC % RING))
                        c = loc_dst[:, bass.ds(t, 1), k:k + 1].rearrange("p a k -> p (a k)")
                        r = loc_src[:, bass.ds(t, 1), k:k + 1].rearrange("p a k -> p (a k)")
                        chunk(hot_ready, 128, k % RING, c, r)
                        if k == RING and (not isinstance(t, int) or t >= 2):
                            sum_rows(t - 2, par)
                    with dve.If(general):
                        dve.wait_ge(hot_used, t * WC + WC + RING)
                        dve.sem_inc(slots_seen, 1)
                        with dve.Fori(0, GWIN) as g:
                            dve.wait_ge(gwin_in, (t * GWIN + g) * 32 + 32)
                            nc.vector.tensor_scalar(gloc[0:TP, 0, :], gwin[0:TP, 0, :], float(MID), None,
                                                    ALU.subtract).then_inc(gwin_used, 1)
                            nc.vector.tensor_scalar(gloc[0:TP, 1, :], gwin[0:TP, 1, :], tile_base[0:TP, bass.ds(t, 1)], None,
                                                    ALU.subtract).then_inc(gwin_used, 1)
                            dve.wait_ge(gwin_used, (t * GWIN + g) * 2 + 3)
                            for k in range(GC):
                                dve.wait_ge(ghot_used, (t * GWIN + g) * GC + k + 1)
                                chunk(ghot_ready, TP, k % GRING, gloc[0:TP, 1, k:k + 1], gloc[0:TP, 0, k:k + 1])
                            dve.wait_ge(ghot_ready, (t * GWIN + g) * (2 * GC) + 2 * GC)
                            dve.sem_inc(slots_seen, 1)
                        dve.wait_ge(ghot_used, (t * GWIN + GWIN) * GC + GRING)
                        dve.sem_inc(slots_seen, 1)

                for_tiles(dve, tile)
                for t in (NT - 2, NT - 1):
                    sum_rows(t, t % 2)
                dve.wait_ge(summed_rows, 2 * NT)
                dve.wait_ge(bank_free, (NT + 1) * NB)
                link(nc.vector.tensor_reduce(deg[0:TP, :, 1], col_part[0:TP], AX.X, ALU.add))
                link(nc.vector.tensor_copy(deg[0:TP, :, 0], row_sum[0:TP]))
                link(nc.vector.tensor_copy(vdeg[0:TP, :, 0:2], deg[0:TP, :, 0:2]))
                link(nc.vector.tensor_tensor(vdeg[0:TP, :, 2:4], deg[0:TP, :, 0:2], vdeg[0:TP, :, 0:2], ALU.subtract))

            @block.tensor
            def _(pe):
                pe.wait_ge(counted, 1)
                nc.tensor.matmul(small[0:1, 0:NT + 2], ones[0:TP, 0:1], cnt[0:TP, :], start=True, stop=True).then_inc(summed, 1)
                pe.sem_inc(hot_used, RING)
                pe.sem_inc(ghot_used, GRING)
                pe.wait_ge(w_in, 48)

                def product(t, j):
                    pe.wait_ge(hT_made, t + 1)
                    for k in range(2):
                        nc.tensor.matmul(acc[0:HD, j, XWT:XWT + TP], w_sb[:, k, :], hT[:, j, k, 0:TP], start=(k == 0), stop=(k == 1))
                    for k in range(2):
                        mm = nc.tensor.matmul(acc[0:TP, j, XW:XW + HD], hT[:, j, k, 0:TP], w_sb[:, k, :], start=(k == 0), stop=(k == 1))
                    mm.then_inc(xw_done, 1)

                def project(t, j):
                    pe.wait_ge(h_made, t + 1)
                    if t >= SR:
                        pe.wait_ge(xw_made, (t - SR + 1) * 2)
                    for k in range(2):
                        mm = nc.tensor.transpose(acc[:, j, k * 128:k * 128 + TP], h_all[0:TP, t, k * 128:(k + 1) * 128],
                                                 ident[0:TP, 0:TP])
                    mm.then_inc(h_turned, 1)
                    if t >= 1:
                        product(t - 1, (j - 1) % SR)

                for t in range(NT):
                    project(t, t % SR)
                product(NT - 1, (NT - 1) % SR)
                pe.wait_ge(xw_made, 2 * NT)
                for t in range(NT):
                    mm = nc.tensor.matmul(small[0:TP, LR + t * 2 * HEADS:LR + (t + 1) * 2 * HEADS], xwT[:, t * TP:(t + 1) * TP],
                                          wlr_sb[:], start=True, stop=True)
                mm.then_inc(lr_done, 1)
                for n in range(HEADS * NB):
                    h, b = n // NB, n % NB
                    lo, k = BANKS[b]
                    if n >= SR:
                        pe.wait_ge(rows_made, n - SR + 1)
                    nc.tensor.matmul(acc[0:TP, n % SR, 0:k], wl_sb[:, h, :], xwT[:, lo:lo + k], start=True,
                                     stop=True).then_inc(rows_done, 1)
                    if n == 2 * NB:
                        pe.wait_ge(maxima, 1)
                        for k in range(2):
                            mm = nc.tensor.transpose(small[0:1, MX + k * 128:MX + k * 128 + TP], mx[0:TP, k:k + 1], ident[0:TP, 0:TP])
                        mm.then_inc(maxima_row, 1)
                    if n == 3 * NB:
                        pe.wait_ge(scale_row, 1)
                        nc.tensor.matmul(small[0:TP, SC:SC + 2], ones[0:1, 0:TP], mrow[:, 4:6], start=True, stop=True).then_inc(scale_all, 1)

                pe.wait_ge(offsets, 1)
                general = pe.value_load(flag_i[0:1, 0:1], min_val=0, max_val=1)
                pe.wait_ge(cleared, 4)
                pe.wait_ge(iotas, 3)
                pe.wait_ge(scaled, 1)
                pe.wait_ge(rows_made, HEADS * NB)

                def product_of(slot, b):
                    lo, n = BANKS[b]
                    return acc[0:TP, b, 0:n], hot_c[:, slot, :], hot_r[:, slot, lo:lo + n]

                def turn_round(t, par, q):
                    rt0, n = rounds[q]
                    if q == 0:
                        pe.wait_ge(bank_free, (t + 2) * NB)
                    if not (isinstance(t, int) and t * NR + q == 0):
                        pe.wait_ge(turn_free, t * NR + q)
                    for i in range(n):
                        mm = nc.tensor.transpose(turn[0:TP, i, 0:TP], strip[0:TP, par, (rt0 + i) * TP:(rt0 + i + 1) * TP], ident16[0:TP, 0:TP])
                    mm.then_inc(turn_done, 1)

                def tile(t, par, before):
                    for b in range(NB):
                        pe.wait_ge(bank_free, t * NB + b + 1)
                        for k in range(HEAD):
                            if b == 0:
                                pe.wait_ge(hot_ready, t * (2 * WC) + 2 * k + 2)
                            mm = nc.tensor.matmul(*product_of(k % RING, b), start=(k == 0), stop=False)
                            if b == NB - 1:
                                mm.then_inc(hot_used, 1)
                    for k in range(HEAD, WC):
                        if k in TURN_AT and (not isinstance(t, int) or t >= 1):
                            turn_round(t - 1, 1 - par, TURN_AT[k])
                        pe.wait_ge(hot_ready, t * (2 * WC) + 2 * k + 2)
                        for b in range(NB):
                            mm = nc.tensor.matmul(*product_of(k % RING, b), start=False, stop=(k == WC - 1))
                        mm.then_inc(hot_used, 1)
                    with pe.If(general):
                        for b, (lo, n) in enumerate(BANKS):
                            nc.tensor.matmul(acc[0:TP, b, 0:n], zeros[0:TP, :], iota_r[0:TP, lo:lo + n], start=True,
                                             stop=False, skip_group_check=True)
                        with pe.Fori(0, GWIN) as g:
                            for k in range(GC):
                                pe.wait_ge(ghot_ready, (t * GWIN + g) * (2 * GC) + 2 * k + 2)
                                for b, (lo, n) in enumerate(BANKS):
                                    mm = nc.tensor.matmul(acc[0:TP, b, 0:n], hot_c[0:TP, k % GRING, :],
                                                          hot_r[0:TP, k % GRING, lo:lo + n], start=False, stop=False,
                                                          skip_group_check=True)
                                mm.then_inc(ghot_used, 1)
                    nc.tensor.matmul(acc[0:TP, NB - 1, 0:1], zeros[0:TP, :], iota_r[0:TP, 0:1], start=False, stop=True,
                                     skip_group_check=True).then_inc(bank_done, 1)

                for_tiles(pe, tile)
                for q in range(NR):
                    turn_round(NT - 1, (NT - 1) % 2, q)

            @block.scalar
            def _(act):
                act.sem_inc(bank_free, NB)
                act.wait_ge(norm_made, NT)
                nc.scalar.activation(norm[0:TP, 1, :, 0], norm[0:TP, 0, :, 1], ACT.Sqrt, bias=scales[0:TP, 3:4]).then_inc(rooted, 1)

                def put_product(t, j):
                    act.wait_ge(xw_done, t + 1)
                    nc.scalar.copy(xwT[:, bass.ds(t * TP, TP)], acc[0:HD, j, XWT:XWT + TP]).then_inc(xw_made, 1)
                    nc.scalar.copy(xw[:, bass.ds(t, 1), :].rearrange("p a k -> p (a k)"), acc[0:TP, j, XW:XW + HD]).then_inc(xw_made, 1)

                act.wait_ge(h_made, NT)

                def project(t, j, before):
                    act.wait_ge(h_turned, t + 1)
                    if not isinstance(before, int):
                        act.wait_ge(xw_done, t - SR + 1)
                    nc.scalar.copy(hT[:, j, :, 0:TP], acc[:, j, 0:256].rearrange("p (k n) -> p k n", k=2)[:, :, 0:TP]).then_inc(hT_made, 1)
                    if not isinstance(t, int) or t >= 1:
                        put_product(t - 1, (j - 1) % SR)

                for_ring(act, project)
                put_product(NT - 1, (NT - 1) % SR)
                act.wait_ge(lr_made, 1)
                for n, (kind, scale) in enumerate(((EL, 1.0), (EL, 0.2), (ER, 1.0), (ER, 0.2))):
                    nc.scalar.activation(pows[0:TP, n], lr[0:TP, :, kind:kind + HEADS], ACT.Exp, scale=scale).then_inc(pows_made, 1)
                for n in range(HEADS * NB):
                    h, b = n // NB, n % NB
                    lo, k = BANKS[b]
                    act.wait_ge(rows_done, n + 1)
                    nc.scalar.copy(rows[0:TP, h * N + lo:h * N + lo + k], acc[0:TP, n % SR, 0:k]).then_inc(rows_made, 1)

                act.wait_ge(cleared, 4)

                def tile(t, par, before):
                    act.wait_ge(bank_done, t + 1)
                    if not isinstance(before, int) or before:
                        act.wait_ge(strip_out[par], before * 16)
                        act.wait_ge(turn_done, (t - 1) * NR)
                    for b, (lo, n) in enumerate(BANKS):
                        col = col_part[0:TP, bass.ds(t, 1), b:b + 1].rearrange("p a k -> p (a k)")
                        nc.scalar.activation(strip[0:TP, par, lo:lo + n], acc[0:TP, b, 0:n], ACT.Copy,
                                             accum_out=col).then_inc(bank_free, 1)
                    if not isinstance(before, int) or before:
                        act.wait_ge(turned_out[par], before * 16)
                        act.wait_ge(summed_rows, (t - 1) * 2 - 1)
                    for q, (rt0, n) in enumerate(rounds):
                        act.wait_ge(turn_done, t * NR + q + 1)
                        nc.scalar.copy(turned[0:TP, par, rt0:rt0 + n, :], turn[0:TP, 0:n, 0:TP]).then_inc(turn_free, 1)

                for_tiles(act, tile)


def layer_norm_all(nc, dve, link, x, out, stats, norm, stats_made, norm_made, rooted, made):
    for t in range(NT):
        nc.vector.bn_stats(stats[0:TP, t, :], x[0:TP, t, :]).then_inc(stats_made, 1)
    dve.wait_ge(stats_made, NT)
    dve.sem_inc(stats_made, 1)
    for t in range(NT):
        nc.vector.bn_aggr(norm[0:TP, 0, t, :], stats[0:TP, t, :]).then_inc(norm_made, 1)
    dve.wait_ge(rooted, 1)
    link(nc.vector.reciprocal(norm[0:TP, 1, :, 1], norm[0:TP, 1, :, 0]))
    for t in range(NT):
        nc.vector.tensor_scalar(out[0:TP, t, :], x[0:TP, t, :], norm[0:TP, 0, t, 0:1], norm[0:TP, 1, t, 1:2],
                                ALU.subtract, ALU.mult).then_inc(made, 1)


class Chain:

    def __init__(self, eng, sem, passed=None):
        self.eng, self.sem, self.count, self.base = eng, sem, 0, 0
        self.passed = passed

    def __call__(self, ins):
        self.count += 1
        ins.then_inc(self.sem, 1)
        self.eng.wait_ge(self.sem, self.base + self.count)

    def at(self, base):
        self.base, self.count = base, 0


def graph_attention(nc, x, gat_b, dram, ones, att, deg, xs, scales):
    feats, rows, lr, ner, pows, vdeg = att.feats, att.rows, att.lr, att.ner, att.pows, att.vdeg
    MR = 20
    assert HEADS * NT % MR == 0
    with ExitStack() as ctx:
        def sb(name, shape, dt):
            return ctx.enter_context(nc.sbuf_tensor(name, shape, dt))

        def sem(name):
            return ctx.enter_context(nc.semaphore(name))

        strip = sb("g_strip", [128, NT, GT, TP], F16)
        mask = sb("mask", [128, MR, GW], F16)
        tot = sb("tot", [128, GT, 2 * HF + 4], F32)
        got = sb("got", [128, GT, 2 * HF], F32)
        tmp = sb("tmp", [128, 2, GT, HF], F32)
        num = sb("num", [128, GT, D], F32)
        den = sb("den", [128, GT, HEADS], F32)
        low = tot[:].rearrange("p t n -> p (t n)")[:, 0:GT * D].rearrange("p (t d) -> p t d", d=D)
        bias = sb("g_bias", [128, D], F32)
        acc = ctx.enter_context(nc.psum_tensor("g_acc", [128, GT, BANK], F32))
        strip_in = [sem(f"g_strip_in{j}") for j in range(GT)]
        mask_ready = sem("mask_ready")
        mask_used = sem("mask_used")
        phase_done = sem("phase_done")
        acc_free = sem("acc_free")
        tot_used = sem("tot_used")
        got_used = sem("got_used")
        pool_chain = sem("pool_chain")
        bias_in = sem("bias_in")
        x_in = sem("g_x_in")
        low_made = sem("low_made")
        exp_made = sem("exp_made")
        finished = sem("finished")
        passed = sem("g_passed")
        den_made = sem("den_made")
        den_turned = sem("den_turned")
        PD = GT + HEADS * (GT - 1)
        NP_ = HEADS + 1

        with nc.Block() as block:
            @block.sync
            def _(sp):
                def load(g):
                    for j in range(GT):
                        if not isinstance(g, int):
                            sp.wait_ge(mask_ready, g * (HEADS * NT) - NT + (j + 1) * GT)
                            sp.wait_ge(phase_done, g * PD - HEADS * (GT - 1))
                        for rt in range(GT):
                            sp.dma_start(strip[:, j * GT:(j + 1) * GT, rt, :],
                                         dram.adj_t[bass.ds(g * GT + rt, 1), :, j * GT:(j + 1) * GT, :].rearrange("g c a r -> c (g a) r")
                                         ).then_inc(strip_in[j], 16)

                def load_x(g):
                    if not isinstance(g, int):
                        sp.wait_ge(finished, g)
                    sp.dma_start(xs[0:TP, bass.ds(g * GT, GT), :], x[bass.ds(g * GW, GW), :].rearrange("(t p) d -> p t d", p=TP)
                                 ).then_inc(x_in, 16)

                load(0)
                sp.dma_start(bias[0:TP, :], gat_b).then_inc(bias_in, 16)
                load_x(0)
                with sp.Fori(1, NG) as g:
                    load(g)
                    load_x(g)

            @block.vector
            def _(dve):
                with dve.Fori(0, NG) as g:
                    for h in range(HEADS):
                        for ct in range(NT):
                            if h == 0 and ct % GT == 0:
                                dve.wait_ge(strip_in[ct // GT], g * (16 * GT) + 16 * GT)
                            dve.wait_ge(mask_used, g * (HEADS * NT) + (h * NT + ct + 1))
                            nc.vector.scalar_tensor_tensor(out=mask[0:TP, (h * NT + ct) % MR, :], in0=rows[0:TP, bass.ds(g * GW + h * N, GW)],
                                                           scalar=ner[0:TP, ct, h:h + 1], in1=strip[0:TP, ct].rearrange("c g r -> c (g r)"),
                                                           op0=ALU.is_ge, op1=ALU.mult).then_inc(mask_ready, 1)
                    dve.wait_ge(den_made, g + 1)
                    nc.vector.reciprocal(den[0:TP], den[0:TP]).then_inc(den_turned, 1)

            @block.tensor
            def _(pe):
                pe.sem_inc(mask_used, MR)
                with pe.Fori(0, NG) as g:
                    for ct in range(NT):
                        if ct % GT == 0:
                            pe.wait_ge(strip_in[ct // GT], g * (16 * GT) + 16 * GT)
                        for rt in range(GT):
                            if ct == 0:
                                pe.wait_ge(acc_free, g * (NP_ * GT) + rt + 1)
                            blk = strip[0:TP, ct, rt, :]
                            for part in range(2):
                                nc.tensor.matmul(acc[0:TP, rt, 0:HEADS * (HD + 1)], blk, feats[0:TP, ct, :, part, HD + 1:HF],
                                                 start=(ct == 0 and part == 0), stop=False, skip_group_check=True)
                            mm = nc.tensor.matmul(acc[0:TP, rt, 2 * HF:2 * HF + 4], blk, vdeg[0:TP, ct, :], start=False,
                                                  stop=(ct == NT - 1), skip_group_check=True)
                            if ct == NT - 1:
                                mm.then_inc(phase_done, 1)
                    for h in range(HEADS):
                        for ct in range(NT):
                            pe.wait_ge(mask_ready, g * (HEADS * NT) + (h * NT + ct + 1))
                            for rt in range(GT):
                                if ct == 0:
                                    pe.wait_ge(acc_free, g * (NP_ * GT) + ((h + 1) * GT + rt + 1))
                                mm = nc.tensor.matmul(acc[0:TP, rt, 0:2 * HF], mask[0:TP, (h * NT + ct) % MR, rt * TP:(rt + 1) * TP],
                                                      feats[0:TP, ct, h].rearrange("p a n -> p (a n)"), start=(ct == 0),
                                                      stop=(ct == NT - 1))
                                if ct == NT - 1 and rt < GT - 1:
                                    mm.then_inc(phase_done, 1)
                            mm.then_inc(mask_used, 1)

            @block.scalar
            def _(act):
                act.sem_inc(acc_free, GT)
                with act.Fori(0, NG) as g:
                    for ph in range(NP_):
                        for rt in range(GT):
                            if ph == 0 or rt < GT - 1:
                                act.wait_ge(phase_done, g * PD + (ph * (GT - 1) + (ph > 0) + rt + 1))
                            else:
                                act.wait_ge(mask_used, g * (HEADS * NT) + (ph * NT + MR))
                            if ph == 0:
                                if rt == 0:
                                    act.wait_ge(tot_used, g + 1)
                                nc.scalar.copy(tot[0:TP, rt, 0:2 * HF + 4], acc[0:TP, rt, 0:2 * HF + 4]).then_inc(acc_free, 1)
                            else:
                                if rt == 0:
                                    act.wait_ge(got_used, g * HEADS + ph)
                                nc.scalar.copy(got[0:TP, rt, :], acc[0:TP, rt, 0:2 * HF]).then_inc(acc_free, 1)
                    act.wait_ge(low_made, g + 1)
                    nc.scalar.activation(low[0:TP], low[0:TP], ACT.Exp).then_inc(exp_made, 1)

            @block.gpsimd
            def _(pool):
                pool.sem_inc(tot_used, 1)
                pool.sem_inc(got_used, 1)
                link = Chain(pool, pool_chain)
                pool.wait_ge(bias_in, 16)
                with pool.Fori(0, NG) as g:
                    link.at(g * (HEADS * 6 + 7))
                    pool.wait_ge(acc_free, g * (NP_ * GT) + 2 * GT)
                    link(nc.gpsimd.tensor_tensor(deg[0:TP, bass.ds(g * GT, GT), 2:4], tot[0:TP, :, 2 * HF:2 * HF + 2],
                                                 tot[0:TP, :, 2 * HF + 2:2 * HF + 4], ALU.add))
                    for h in range(HEADS):
                        s = got[0:TP]
                        a = pows[0:TP, 0, bass.ds(g * GT, GT), h:h + 1].to_broadcast([TP, GT, HD + 1])
                        a5 = pows[0:TP, 1, bass.ds(g * GT, GT), h:h + 1].to_broadcast([TP, GT, HD + 1])
                        b, b5 = tmp[0:TP, 0, :, 0:HD + 1], tmp[0:TP, 0, :, HD + 1:HF]
                        pool.wait_ge(acc_free, g * (NP_ * GT) + (h + 3) * GT)
                        link(nc.gpsimd.tensor_tensor(tmp[0:TP, 0], s[:, :, 0:HF], s[:, :, HF:2 * HF], ALU.add))
                        link(nc.gpsimd.tensor_tensor(tmp[0:TP, 1, :, 0:HD + 1], tot[0:TP, :, h * (HD + 1):(h + 1) * (HD + 1)], b5,
                                                     ALU.subtract))
                        link(nc.gpsimd.tensor_tensor(b, b, a, ALU.mult))
                        link(nc.gpsimd.tensor_tensor(b5, tmp[0:TP, 1, :, 0:HD + 1], a5, ALU.mult))
                        link(nc.gpsimd.tensor_tensor(num[0:TP, :, h * HD:(h + 1) * HD], tmp[0:TP, 0, :, 0:HD],
                                                     tmp[0:TP, 0, :, HD + 1:HD + 1 + HD], ALU.add))
                        link(nc.gpsimd.tensor_tensor(den[0:TP, :, h:h + 1], tmp[0:TP, 0, :, HD:HD + 1],
                                                     tmp[0:TP, 0, :, HF - 1:HF], ALU.add))
                        pool.sem_inc(got_used, 1)
                    heads = num[0:TP].rearrange("p t (h k) -> p (t h) k", h=HEADS)
                    den_f = den[0:TP].rearrange("p t h -> p (t h)")
                    pool.sem_inc(passed, 1)
                    nc.gpsimd.tensor_scalar(den[0:TP], den[0:TP], scales[0:TP, 1:2], 1e-12, ALU.mult, ALU.max).then_inc(den_made, 1)
                    pool.wait_ge(den_turned, g + 1)
                    pool.sem_inc(passed, 1)
                    link(nc.gpsimd.tensor_scalar(den[0:TP], den[0:TP], scales[0:TP, 1:2], None, ALU.mult))
                    link(nc.gpsimd.tensor_tensor(heads, heads, den_f.to_broadcast([TP, GT * HEADS, HD]), ALU.mult))
                    link(nc.gpsimd.tensor_tensor(num[0:TP], num[0:TP], bias[0:TP].rearrange("p (a d) -> p a d", a=1).to_broadcast([TP, GT, D]), ALU.add))
                    pool.sem_inc(passed, 1)
                    nc.gpsimd.tensor_scalar(low[0:TP], num[0:TP], 0.0, None, ALU.min).then_inc(low_made, 1)
                    link(nc.gpsimd.tensor_scalar(num[0:TP], num[0:TP], 0.0, -1.0, ALU.max, ALU.add))
                    pool.wait_ge(x_in, g * 16 + 16)
                    mine = xs[0:TP, bass.ds(g * GT, GT), :]
                    pool.sem_inc(passed, 1)
                    link(nc.gpsimd.tensor_tensor(mine, mine, num[0:TP], ALU.add))
                    pool.wait_ge(exp_made, g + 1)
                    pool.sem_inc(passed, 1)
                    link(nc.gpsimd.tensor_tensor(mine, mine, low[0:TP], ALU.add))
                    pool.sem_inc(finished, 1)
                    pool.sem_inc(tot_used, 1)


NE = 8
SLOT = 128
NBLK = (2 * N + NE * (SLOT - 1)) // SLOT


def mixture(nc, layer, xs, par, ident, ones, scales, dram_x, dram_y, hidden, pool_sem):
    norms = 2 if layer == 0 else 1
    KD = D // 128
    KH = hidden // 128
    with ExitStack() as ctx:
        def sb(name, shape, dt):
            return ctx.enter_context(nc.sbuf_tensor(f"m{layer}_{name}", shape, dt))

        def sem(name):
            return ctx.enter_context(nc.semaphore(f"m{layer}_{name}"))

        tok = sb("tok", [128, NT, D], F32)
        w1 = sb("w1", [128, NE, KD, hidden], F32)
        w2 = sb("w2", [128, NE, KH, D], F32)
        b1 = sb("b1", [128, NE, hidden], F32)
        b2 = sb("b2", [128, NE, D], F32)
        weight = sb("weight", [128, 2, NT], F32)
        pos = sb("pos", [128, 2, NT], U32)
        expert = sb("expert", [1, NBLK], I32)
        w_in = sem("w_in")
        zero_out = sem("zero_out")
        placed = pool_sem(f"m{layer}_placed")

        with ExitStack() as ctx2:
            def sb2(name, shape, dt):
                return ctx2.enter_context(nc.sbuf_tensor(f"r{layer}_{name}", shape, dt))

            def ps(name, shape):
                return ctx2.enter_context(nc.psum_tensor(f"r{layer}_{name}", shape, F32))

            def sem2(name):
                return ctx2.enter_context(nc.semaphore(f"r{layer}_{name}"))

            wr = sb2("wr", [128, KD, NE], F32)
            br = sb2("br", [1, NE], F32)
            gb = sb2("gb", [128, 2, D], F32)
            stats = sb2("stats", [128, NT, 6], F32)
            norm = sb2("norm", [128, 2, NT, 2], F32)
            mid = sb2("mid", [128, NT, D], F32) if layer == 0 else None
            tT = sb2("tT", [128, SR, KD, 128], F32)
            logit = sb2("logit", [128, NT, NE], F32)
            best = sb2("best", [128, NT, 8], F32)
            besti = sb2("besti", [128, NT, 8], U32)
            bestf = sb2("bestf", [128, NT, 2], F32)
            one = sb2("one", [128, 3, NT, NE], F32)
            iota8 = sb2("iota8", [128, NT, NE], F32)
            iota128 = sb2("iota128", [128, NE, NT], F32)
            iotab = sb2("iotab", [1, NBLK, NE - 1], F32)
            before = sb2("before", [128, 128], F32)
            place = sb2("place", [128, NT, NE], F32)
            sums = sb2("sums", [128, 3, NT, NE], F32)
            blocks = sb2("blocks", [128, NE, NT], F32)
            nblk = sb2("nblk", [128, 4, NE], F32)
            eb = sb2("eb", [1, NBLK, NE - 1], F32)
            ebs = sb2("ebs", [1, NBLK], F32)
            s25 = sb2("s25", [128, 4, NT], F32)
            zero = sb2("zero", [128, 8, D], F32)
            p_turn = ps("p_turn", [128, SR, BANK])
            p_log = ps("p_log", [128, BANK])
            p_pre = ps("p_pre", [128, BANK])
            p_tot = ps("p_tot", [128, BANK])

            r_in = sem2("r_in")
            chain = sem2("chain")
            stats_made = [sem2(f"stats_made{n}") for n in range(norms)]
            norm_made = [sem2(f"norm_made{n}") for n in range(norms)]
            rooted = [sem2(f"rooted{n}") for n in range(norms)]
            normed = [sem2(f"normed{n}") for n in range(norms)]
            scaled = sem2("scaled")
            tok_made = sem2("tok_made")
            turned = sem2("turned")
            tT_made = sem2("tT_made")
            log_done = sem2("log_done")
            made = sem2("made")
            shifted = sem2("shifted")
            expd = sem2("expd")
            ones_made = sem2("ones_made")
            counted = sem2("counted")
            placed_at = sem2("placed_at")

            with nc.Block() as block:
                @block.sync
                def _(sp):
                    sp.dma_start(wr[:], par["wr"].rearrange("(k p) e -> p k e", p=128)).then_inc(r_in, 16)
                    sp.dma_start(br[:], par["br"]).then_inc(r_in, 16)
                    if layer == 0:
                        sp.dma_start(gb[0:TP], par["gb"]).then_inc(r_in, 16)
                    sp.wait_ge(made, 1)
                    for lo in range(0, NBLK, 8):
                        n = min(8, NBLK - lo)
                        sp.dma_start(dram_x[lo * SLOT:(lo + n) * SLOT, :].rearrange("(k p) d -> p k d", p=SLOT),
                                     zero[:, 0:n, :]).then_inc(zero_out, 16)
                    sp.dma_start(w1[:], par["w1"].rearrange("e (k p) h -> p e k h", p=128)).then_inc(w_in, 16)
                    sp.dma_start(w2[:], par["w2"].rearrange("e (k p) h -> p e k h", p=128)).then_inc(w_in, 16)
                    sp.dma_start(b1[:], par["b1"]).then_inc(w_in, 16)
                    sp.dma_start(b2[:], par["b2"]).then_inc(w_in, 16)

                @block.gpsimd
                def _(pool):
                    nc.gpsimd.memset(zero[:], 0.0).then_inc(made, 1)
                    nc.gpsimd.iota(iota8[:], [[0, NT], [1, NE]], base=0, channel_multiplier=0,
                                   allow_small_or_imprecise_dtypes=True).then_inc(made, 1)
                    nc.gpsimd.iota(iota128[:], [[0, NE], [SLOT, NT]], base=0, channel_multiplier=0,
                                   allow_small_or_imprecise_dtypes=True).then_inc(made, 1)
                    nc.gpsimd.iota(iotab[:], [[1, NBLK], [0, NE - 1]], base=0, channel_multiplier=0,
                                   allow_small_or_imprecise_dtypes=True).then_inc(made, 1)
                    nc.gpsimd.affine_select(out=before[:], in_=ones[:], compare_op=ALU.is_gt, fill=0.0, base=0,
                                            pattern=[[1, 128]], channel_multiplier=-1).then_inc(made, 1)
                    pool.wait_ge(placed_at, 1)
                    pool.wait_ge(zero_out, 16 * -(-NBLK // 8))
                    for t in range(NT):
                        for c in range(2):
                            pool.indirect_dma_start(dram_x[:, :], bass.IndirectOffsetOnAxis(ap=pos[0:TP, c, t:t + 1], axis=0),
                                                    tok[0:TP, t, :], None).then_inc(placed, 16)
                    pool.wait_ge(placed, 16 * 2 * NT)

                @block.vector
                def _(dve):
                    link = Chain(dve, chain)
                    dve.wait_ge(r_in, 32 + 16 * (layer == 0))
                    if layer == 0:
                        layer_norm_all(nc, dve, link, xs, mid, stats, norm, stats_made[0], norm_made[0], rooted[0], normed[0])
                        dve.wait_ge(normed[0], NT)
                        layer_norm_all(nc, dve, link, mid, tok, stats, norm, stats_made[1], norm_made[1], rooted[1], normed[1])
                        for t in range(NT + 1):
                            if t < NT:
                                dve.wait_ge(normed[1], t + 1)
                                nc.vector.tensor_tensor(tok[0:TP, t], tok[0:TP, t], gb[0:TP, 0], ALU.mult).then_inc(scaled, 1)
                            if t >= 1:
                                dve.wait_ge(scaled, t)
                                nc.vector.tensor_tensor(tok[0:TP, t - 1], tok[0:TP, t - 1], gb[0:TP, 1], ALU.add).then_inc(tok_made, 1)
                    else:
                        layer_norm_all(nc, dve, link, xs, tok, stats, norm, stats_made[0], norm_made[0], rooted[0], tok_made)
                    dve.wait_ge(log_done, NT)
                    link(nc.vector.tensor_copy(logit[0:TP].rearrange("p t e -> p (t e)"), p_log[0:TP, 0:NT * NE]))
                    if layer == 1:
                        link(nc.vector.tensor_reduce(s25[0:TP, 0], logit[0:TP], AX.X, ALU.max))
                        nc.vector.tensor_tensor(logit[0:TP], logit[0:TP], s25[0:TP, 0].to_broadcast([TP, NT, NE]),
                                                ALU.subtract).then_inc(shifted, 1)
                        dve.wait_ge(expd, 1)
                        link(nc.vector.tensor_reduce(s25[0:TP, 1], logit[0:TP], AX.X, ALU.add))
                        link(nc.vector.reciprocal(s25[0:TP, 2], s25[0:TP, 1]))
                        link(nc.vector.tensor_tensor(logit[0:TP], logit[0:TP], s25[0:TP, 2].to_broadcast([TP, NT, NE]), ALU.mult))
                    for t in range(NT):
                        m = nc.vector.max(best[0:TP, t, :], logit[0:TP, t, :])
                    link(m)
                    for t in range(NT):
                        m = nc.vector.max_index(besti[0:TP, t, :], best[0:TP, t, :], logit[0:TP, t, :])
                    link(m)
                    if layer == 0:
                        nc.vector.tensor_tensor(s25[0:TP, 0], best[0:TP, :, 1], best[0:TP, :, 0], ALU.subtract).then_inc(shifted, 1)
                        dve.wait_ge(expd, 1)
                        link(nc.vector.tensor_scalar(s25[0:TP, 2], s25[0:TP, 1], 1.0, None, ALU.add))
                        link(nc.vector.reciprocal(weight[0:TP, 0], s25[0:TP, 2]))
                        link(nc.vector.tensor_tensor(weight[0:TP, 1], weight[0:TP, 0], s25[0:TP, 1], ALU.mult))
                    else:
                        link(nc.vector.tensor_tensor(s25[0:TP, 1], best[0:TP, :, 1], best[0:TP, :, 0], ALU.add))
                        link(nc.vector.tensor_scalar(s25[0:TP, 1], s25[0:TP, 1], 1e-12, None, ALU.max))
                        link(nc.vector.reciprocal(s25[0:TP, 2], s25[0:TP, 1]))
                        link(nc.vector.tensor_tensor(weight[0:TP, 0], best[0:TP, :, 0], s25[0:TP, 2], ALU.mult))
                        link(nc.vector.tensor_tensor(weight[0:TP, 1], best[0:TP, :, 1], s25[0:TP, 2], ALU.mult))
                    link(nc.vector.tensor_copy(bestf[0:TP], besti[0:TP, :, 0:2]))
                    dve.wait_ge(made, 5)
                    for c in range(2):
                        link(nc.vector.tensor_tensor(one[0:TP, c], iota8[0:TP], bestf[0:TP, :, c].to_broadcast([TP, NT, NE]),
                                                     ALU.is_equal))
                    nc.vector.tensor_tensor(one[0:TP, 2], one[0:TP, 0], one[0:TP, 1], ALU.add).then_inc(ones_made, 1)
                    dve.wait_ge(counted, 1)
                    link(nc.vector.tensor_copy(sums[0:TP, 0], p_tot[0:TP, 0:NT * NE].rearrange("p (t e) -> p t e", e=NE)))
                    cur = 0
                    step = 1
                    while step < NT:
                        new = 1 - cur
                        link(nc.vector.tensor_copy(sums[0:TP, new, 0:step], sums[0:TP, cur, 0:step]))
                        link(nc.vector.tensor_tensor(sums[0:TP, new, step:NT], sums[0:TP, cur, step:NT], sums[0:TP, cur, 0:NT - step], ALU.add))
                        cur, step = new, step * 2
                    link(nc.vector.tensor_tensor(blocks[0:TP], sums[0:TP, cur, NT - 1].to_broadcast([TP, NE, NT]), iota128[0:TP], ALU.is_gt))
                    link(nc.vector.tensor_reduce(nblk[0:TP, 0], blocks[0:TP], AX.X, ALU.add))
                    link(nc.vector.memset(nblk[0:TP, 1], 0.0))
                    for e in range(1, NE):
                        link(nc.vector.tensor_tensor(nblk[0:TP, 1, e:e + 1], nblk[0:TP, 1, e - 1:e], nblk[0:TP, 0, e - 1:e], ALU.add))
                    link(nc.vector.tensor_scalar(nblk[0:TP, 2], nblk[0:TP, 1], float(SLOT), None, ALU.mult))
                    link(nc.vector.tensor_tensor(place[0:TP], p_pre[0:TP, 0:NT * NE].rearrange("p (t e) -> p t e", e=NE),
                                                 nblk[0:TP, 2:3, :].to_broadcast([TP, NT, NE]), ALU.add))
                    link(nc.vector.tensor_tensor(place[0:TP, 1:NT], place[0:TP, 1:NT], sums[0:TP, cur, 0:NT - 1], ALU.add))
                    for c in range(2):
                        link(nc.vector.tensor_tensor(sums[0:TP, 2], place[0:TP], one[0:TP, c], ALU.mult))
                        link(nc.vector.tensor_reduce(s25[0:TP, 3], sums[0:TP, 2], AX.X, ALU.add))
                        link(nc.vector.tensor_copy(pos[0:TP, c], s25[0:TP, 3]))
                    link(nc.vector.tensor_tensor(eb[:], nblk[0:1, 1:2, 1:NE].to_broadcast([1, NBLK, NE - 1]), iotab[:], ALU.is_le))
                    link(nc.vector.tensor_reduce(ebs[:], eb[:], AX.X, ALU.add))
                    nc.vector.tensor_copy(expert[:], ebs[:]).then_inc(placed_at, 1)

                @block.scalar
                def _(act):
                    for n in range(norms):
                        act.wait_ge(norm_made[n], NT)
                        nc.scalar.activation(norm[0:TP, 1, :, 0], norm[0:TP, 0, :, 1], ACT.Sqrt, bias=scales[0:TP, 3:4]).then_inc(rooted[n], 1)

                    def tile(t, j, earlier):
                        act.wait_ge(turned, t + 1)
                        if not isinstance(earlier, int):
                            act.wait_ge(log_done, t + (1 - SR))
                        nc.scalar.copy(tT[:, j, :, 0:TP], p_turn[:, j, 0:KD * 128].rearrange("p (k n) -> p k n", k=KD)[:, :, 0:TP]).then_inc(tT_made, 1)

                    for_ring(act, tile)
                    act.wait_ge(shifted, 1)
                    if layer == 0:
                        nc.scalar.activation(s25[0:TP, 1], s25[0:TP, 0], ACT.Exp).then_inc(expd, 1)
                    else:
                        nc.scalar.activation(logit[0:TP], logit[0:TP], ACT.Exp).then_inc(expd, 1)

                @block.tensor
                def _(pe):
                    pe.wait_ge(r_in, 32 + 16 * (layer == 0))

                    def score(t):
                        pe.wait_ge(tT_made, t + 1)
                        out = p_log[0:TP, t * NE:(t + 1) * NE]
                        for k in range(KD):
                            nc.tensor.matmul(out, tT[:, t % SR, k, 0:TP], wr[:, k, :], start=(k == 0), stop=False)
                        nc.tensor.matmul(out, ones[0:1, 0:TP], br[:], start=False, stop=True).then_inc(log_done, 1)

                    for t in range(NT):
                        pe.wait_ge(tok_made, t + 1)
                        if t >= SR:
                            pe.wait_ge(tT_made, t - SR + 1)
                        for k in range(KD):
                            mm = nc.tensor.transpose(p_turn[:, t % SR, k * 128:k * 128 + TP], tok[0:TP, t, k * 128:(k + 1) * 128], ident[0:TP, 0:TP])
                        mm.then_inc(turned, 1)
                        if t >= 1:
                            score(t - 1)
                    score(NT - 1)
                    pe.wait_ge(ones_made, 1)
                    flat = one[0:TP, 2].rearrange("p t e -> p (t e)")
                    nc.tensor.matmul(p_pre[0:TP, 0:NT * NE], before[0:TP, 0:TP], flat, start=True, stop=True)
                    nc.tensor.matmul(p_tot[0:TP, 0:NT * NE], ones[0:TP, 0:TP], flat, start=True, stop=True).then_inc(counted, 1)

        with ExitStack() as ctx2:
            def sb2(name, shape, dt):
                return ctx2.enter_context(nc.sbuf_tensor(f"f{layer}_{name}", shape, dt))

            def ps(name, shape):
                return ctx2.enter_context(nc.psum_tensor(f"f{layer}_{name}", shape, F32))

            def sem2(name):
                return ctx2.enter_context(nc.semaphore(f"f{layer}_{name}"))

            xt = sb2("xt", [128, 2, D], F32)
            xT = sb2("xT", [128, 2, KD, 128], F32)
            hb = sb2("hb", [128, 2, hidden], F32)
            hT = sb2("hT", [128, 2, KH, 128], F32)
            yt = sb2("yt", [128, 2, D], F32)
            p_x = ps("p_x", [128, BANK])
            p_h = ps("p_h", [128, 2, BANK])
            p_t = ps("p_t", [128, 2, BANK])
            p_y = ps("p_y", [128, 2, BANK])
            x_in = [sem2("x_in0"), sem2("x_in1")]
            x_turned = sem2("x_turned")
            xT_made = sem2("xT_made")
            h_done = sem2("h_done")
            h_biased = sem2("h_biased")
            h_made = sem2("h_made")
            h_turned = sem2("h_turned")
            hT_made = sem2("hT_made")
            y_done = sem2("y_done")
            y_made = sem2("y_made")
            y_out = [pool_sem(f"f{layer}_y_out{n}") for n in range(2)]

            with nc.Block() as block:
                @block.sync
                def _(sp):
                    def blk(b, p, earlier):
                        if not isinstance(b, int) or b >= 2:
                            sp.wait_ge(x_turned, b - 1)
                        sp.dma_start(xt[:, p], dram_x[bass.ds(b * SLOT, SLOT), :]).then_inc(x_in[p], 16)

                    for_tiles(sp, blk, NBLK)

                @block.tensor
                def _(pe):
                    pe.wait_ge(w_in, 64)

                    def turn_x(b, p, earlier):
                        pe.wait_ge(x_in[p], earlier * 16 + 16)
                        if not isinstance(b, int) or b >= 1:
                            pe.wait_ge(xT_made, b)
                        for k in range(KD):
                            mm = nc.tensor.transpose(p_x[:, k * 128:(k + 1) * 128], xt[:, p, k * 128:(k + 1) * 128], ident[:])
                        mm.then_inc(x_turned, 1)

                    def up(b, p):
                        e = pe.value_load(expert[0:1, bass.ds(b, 1)], min_val=0, max_val=NE - 1)
                        pe.wait_ge(xT_made, b + 1)
                        if not isinstance(b, int) or b >= 2:
                            pe.wait_ge(h_biased, b - 1)
                        for k in range(KD):
                            mm = nc.tensor.matmul(p_h[:, p, 0:hidden], xT[:, p, k, :],
                                                  w1[:, bass.ds(e, 1), k, :].rearrange("p a h -> p (a h)"), start=(k == 0), stop=(k == KD - 1))
                        mm.then_inc(h_done, 1)

                    def turn_h(b, p):
                        pe.wait_ge(h_made, b + 1)
                        if not isinstance(b, int) or b >= 2:
                            pe.wait_ge(hT_made, b - 1)
                        for k in range(KH):
                            mm = nc.tensor.transpose(p_t[:, p, k * 128:(k + 1) * 128], hb[:, p, k * 128:(k + 1) * 128], ident[:])
                        mm.then_inc(h_turned, 1)

                    def down(b, p):
                        e = pe.value_load(expert[0:1, bass.ds(b, 1)], min_val=0, max_val=NE - 1)
                        pe.wait_ge(hT_made, b + 1)
                        if not isinstance(b, int) or b >= 2:
                            pe.wait_ge(y_made, b - 1)
                        for k in range(KH):
                            mm = nc.tensor.matmul(p_y[:, p, 0:D], hT[:, p, k, :],
                                                  w2[:, bass.ds(e, 1), k, :].rearrange("p a h -> p (a h)"), start=(k == 0), stop=(k == KH - 1))
                        mm.then_inc(y_done, 1)

                    def blk(b, p, earlier):
                        turn_x(b, p, earlier)
                        if not isinstance(b, int) or b >= 1:
                            turn_h(b - 1, 1 - p)
                        up(b, p)
                        if not isinstance(b, int) or b >= 1:
                            down(b - 1, 1 - p)

                    for_tiles(pe, blk, NBLK)
                    turn_h(NBLK - 1, (NBLK - 1) % 2)
                    down(NBLK - 1, (NBLK - 1) % 2)

                @block.scalar
                def _(act):
                    def gelu(b, p):
                        act.wait_ge(h_biased, b + 1)
                        nc.scalar.activation(hb[:, p], hb[:, p], ACT.Gelu).then_inc(h_made, 1)

                    def blk(b, p, earlier):
                        act.wait_ge(x_turned, b + 1)
                        if not isinstance(b, int) or b >= 2:
                            act.wait_ge(h_done, b - 1)
                        nc.scalar.copy(xT[:, p].rearrange("p k n -> p (k n)"), p_x[:, 0:D]).then_inc(xT_made, 1)
                        gelu(b, p)

                    for_tiles(act, blk, NBLK)

                @block.vector
                def _(dve):
                    def bias_h(b, p):
                        e = dve.value_load(expert[0:1, bass.ds(b, 1)], min_val=0, max_val=NE - 1)
                        dve.wait_ge(h_done, b + 1)
                        if not isinstance(b, int) or b >= 2:
                            dve.wait_ge(h_turned, b - 1)
                        nc.vector.tensor_tensor(hb[:, p], p_h[:, p, 0:hidden], b1[:, bass.ds(e, 1), :].rearrange("p a h -> p (a h)"),
                                                ALU.add).then_inc(h_biased, 1)

                    def copy_h(b, p):
                        dve.wait_ge(h_turned, b + 1)
                        if not isinstance(b, int) or b >= 2:
                            dve.wait_ge(y_done, b - 1)
                        nc.vector.tensor_copy(hT[:, p].rearrange("p k n -> p (k n)"), p_t[:, p, 0:hidden]).then_inc(hT_made, 1)

                    def bias_y(b, p, earlier):
                        e = dve.value_load(expert[0:1, bass.ds(b, 1)], min_val=0, max_val=NE - 1)
                        dve.wait_ge(y_done, b + 1)
                        if not isinstance(earlier, int) or earlier:
                            dve.wait_ge(y_out[p], earlier * 16)
                        nc.vector.tensor_tensor(yt[:, p], p_y[:, p, 0:D], b2[:, bass.ds(e, 1), :].rearrange("p a h -> p (a h)"),
                                                ALU.add).then_inc(y_made, 1)

                    def blk(b, p, earlier):
                        if not isinstance(b, int) or b >= 1:
                            copy_h(b - 1, 1 - p)
                        bias_h(b, p)
                        if not isinstance(b, int) or b >= 1:
                            bias_y(b - 1, 1 - p, earlier if p == 1 else earlier - 1)

                    dve.wait_ge(w_in, 64)
                    for_tiles(dve, blk, NBLK)
                    copy_h(NBLK - 1, (NBLK - 1) % 2)
                    bias_y(NBLK - 1, (NBLK - 1) % 2, (NBLK - 1) // 2)

                @block.gpsimd
                def _(pool):
                    def blk(b, p, earlier):
                        pool.wait_ge(y_made, b + 1)
                        pool.dma_start(dram_y[bass.ds(b * SLOT, SLOT), :], yt[:, p]).then_inc(y_out[p], 16)

                    for_tiles(pool, blk, NBLK)
                    pool.wait_ge(y_out[0], 16 * ((NBLK + 1) // 2))
                    pool.wait_ge(y_out[1], 16 * (NBLK // 2))

        with ExitStack() as ctx2:
            GB = 4
            got = ctx2.enter_context(nc.sbuf_tensor(f"c{layer}_got", [128, GB, 2, D], F32))
            got_in = [pool_sem(f"c{layer}_got_in{i}") for i in range(GB)]
            added = ctx2.enter_context(nc.semaphore(f"c{layer}_added"))
            with nc.Block() as block:
                @block.gpsimd
                def _(pool):
                    for t in range(NT):
                        if t >= GB:
                            pool.wait_ge(added, (t - GB) * 3 + 3)
                        for c in range(2):
                            pool.indirect_dma_start(got[0:TP, t % GB, c, :], None, dram_y[:, :],
                                                    bass.IndirectOffsetOnAxis(ap=pos[0:TP, c, t:t + 1], axis=0)).then_inc(got_in[t % GB], 16)

                @block.vector
                def _(dve):
                    for t in range(NT):
                        if layer == 1:
                            nc.vector.tensor_tensor(xs[0:TP, t], xs[0:TP, t], tok[0:TP, t], ALU.add).then_inc(added, 1)
                        else:
                            dve.sem_inc(added, 1)
                        dve.wait_ge(added, t * 3 + 1)
                        dve.wait_ge(got_in[t % GB], (t // GB) * 32 + 32)
                        for c in range(2):
                            nc.vector.scalar_tensor_tensor(out=xs[0:TP, t], in0=got[0:TP, t % GB, c], scalar=weight[0:TP, c, t:t + 1],
                                                           in1=xs[0:TP, t], op0=ALU.mult, op1=ALU.add).then_inc(added, 1)
                            dve.wait_ge(added, t * 3 + c + 2)


ZS = 1024.0
YROOM = 2048.0
ROWS, COLS, A_ROWS, A_COLS, T_ROWS, T_COLS = range(6)
IN_DEG = (COLS, ROWS, T_COLS, A_COLS, T_ROWS, A_ROWS)
OUT_DEG = (ROWS, COLS, A_ROWS, A_COLS, T_ROWS, T_COLS)


def graph_convolution(nc, xs, gw, gbias, dram, ident, ones, deg, scales):
    with ExitStack() as ctx:
        def sb(name, shape, dt):
            return ctx.enter_context(nc.sbuf_tensor(name, shape, dt))

        xl = sb("xl", [128, NT, D], F32)
        roots = sb("roots", [128, 2, 6, NT], F32)
        both = sb("both", [128, 2, NT], F32)

        vdeg = sb("c_vdeg", [128, NT, 4], F16)
        def roots_of(dve, act, link, first, last, big, pos, inv, big_made, big_rooted):
            if act is not None:
                act.wait_ge(big_made, 1)
                nc.scalar.activation(big[0:TP, first:last], big[0:TP, first:last], ACT.Sqrt).then_inc(big_rooted, 1)
                return
            if first == 0:
                link(nc.vector.tensor_scalar(big[0:TP, 0:2], deg[0:TP, :, 0:2].rearrange("p t k -> p k t"), 1.0, None, ALU.add))
            lo = max(first, 2)
            link(nc.vector.tensor_copy(big[0:TP, lo:last], deg[0:TP, :, lo:last].rearrange("p t k -> p k t")))
            link(nc.vector.tensor_scalar(pos[0:TP, first:last], big[0:TP, first:last], 0.0, None, ALU.is_gt))
            nc.vector.tensor_scalar(big[0:TP, first:last], big[0:TP, first:last], 1.0, None, ALU.max).then_inc(big_made, 1)
            dve.wait_ge(big_rooted, 1)
            link(nc.vector.reciprocal(inv[0:TP, first:last], big[0:TP, first:last]))
            link(nc.vector.tensor_tensor(inv[0:TP, first:last], inv[0:TP, first:last], pos[0:TP, first:last], ALU.mult))

        def roots_to_terms(link, first, last, inv):
            for k in range(6):
                if first <= IN_DEG[k] < last:
                    link(nc.vector.tensor_scalar(roots[0:TP, 0, k], inv[0:TP, IN_DEG[k]], ZS, None, ALU.mult))
                if first <= OUT_DEG[k] < last:
                    s = 1.0 / ZS if k < 2 else scales[0:TP, 5:6]
                    link(nc.vector.tensor_scalar(roots[0:TP, 1, k], inv[0:TP, OUT_DEG[k]], s, None, ALU.mult))
                if k < 2 and first == 0:
                    link(nc.vector.tensor_tensor(both[0:TP, k], inv[0:TP, IN_DEG[k]], inv[0:TP, OUT_DEG[k]], ALU.mult))

        with ExitStack() as ctx2:
            def sb2(name, shape, dt):
                return ctx2.enter_context(nc.sbuf_tensor(name, shape, dt))

            def sem(name):
                return ctx2.enter_context(nc.semaphore(name))

            stats = sb2("d_stats", [128, NT, 6], F32)
            norm = sb2("d_norm", [128, 2, NT, 2], F32)
            big = sb2("d_big", [128, 6, NT], F32)
            pos = sb2("d_pos", [128, 6, NT], F32)
            inv = sb2("d_inv", [128, 6, NT], F32)
            mx = sb2("d_mx", [128, 1], F32)
            mrow = sb2("d_mrow", [1, 4], F32)
            p_mx = ctx2.enter_context(nc.psum_tensor("p_mx", [128, BANK], F32))
            vdeg_made = sem("vdeg_made")
            chain = sem("d_chain")
            stats_made = sem("d_stats_made")
            norm_made = sem("d_norm_made")
            rooted = sem("d_rooted")
            xl_made = sem("xl_made")
            max_made = sem("max_made")
            max_turned = sem("max_turned")
            max_row = sem("max_row")
            max_all = sem("max_all")
            big_made = sem("big_made")
            big_rooted = sem("big_rooted")
            with nc.Block() as block:
                @block.tensor
                def _(pe):
                    pe.wait_ge(max_made, 1)
                    nc.tensor.transpose(p_mx[0:1, 0:TP], mx[0:TP, 0:1], ident[0:TP, 0:TP]).then_inc(max_turned, 1)
                    pe.wait_ge(max_row, 1)
                    nc.tensor.matmul(p_mx[0:TP, 128:130], ones[0:1, 0:TP], mrow[:, 1:3], start=True, stop=True).then_inc(max_all, 1)

                @block.scalar
                def _(act):
                    roots_of(None, act, None, 0, 4, big, pos, inv, big_made, big_rooted)
                    act.wait_ge(norm_made, NT)
                    nc.scalar.activation(norm[0:TP, 1, :, 0], norm[0:TP, 0, :, 1], ACT.Sqrt, bias=scales[0:TP, 3:4]).then_inc(rooted, 1)

                @block.vector
                def _(dve):
                    link = Chain(dve, chain)
                    nc.vector.tensor_reduce(mx[0:TP], deg[0:TP, :, 0:2], AX.XY, ALU.max).then_inc(max_made, 1)
                    nc.vector.tensor_copy(vdeg[0:TP, :, 0:2], deg[0:TP, :, 0:2]).then_inc(vdeg_made, 1)
                    dve.wait_ge(vdeg_made, 1)
                    nc.vector.tensor_tensor(vdeg[0:TP, :, 2:4], deg[0:TP, :, 0:2], vdeg[0:TP, :, 0:2], ALU.subtract).then_inc(vdeg_made, 1)
                    roots_of(dve, None, link, 0, 4, big, pos, inv, big_made, big_rooted)
                    dve.wait_ge(max_turned, 1)
                    link(nc.vector.tensor_reduce(mrow[:, 3:4], p_mx[0:1, 0:TP], AX.X, ALU.max))
                    link(nc.vector.tensor_scalar(mrow[:, 2:3], mrow[:, 3:4], 1.0 / YROOM, None, ALU.mult))
                    link(nc.vector.reciprocal(mrow[:, 0:1], mrow[:, 2:3]))
                    nc.vector.tensor_scalar(mrow[:, 1:2], mrow[:, 0:1], 1.0 / ZS, None, ALU.mult).then_inc(max_row, 1)
                    dve.wait_ge(max_all, 1)
                    link(nc.vector.tensor_copy(scales[0:TP, 4:6], p_mx[0:TP, 128:130]))
                    roots_to_terms(link, 0, 4, inv)
                    layer_norm_all(nc, dve, link, xs, xl, stats, norm, stats_made, norm_made, rooted, xl_made)
                    dve.wait_ge(xl_made, NT)

        def more_roots():
            with ExitStack() as ctx2:
                big, pos, inv = (ctx2.enter_context(nc.sbuf_tensor(f"t_{n}", [128, 6, NT], F32)) for n in ("big", "pos", "inv"))
                chain, big_made, big_rooted = (ctx2.enter_context(nc.semaphore(f"t_{n}")) for n in ("chain", "big_made", "big_rooted"))
                with nc.Block() as block:
                    @block.scalar
                    def _(act):
                        roots_of(None, act, None, 4, 6, big, pos, inv, big_made, big_rooted)

                    @block.vector
                    def _(dve):
                        link = Chain(dve, chain)
                        roots_of(dve, None, link, 4, 6, big, pos, inv, big_made, big_rooted)
                        roots_to_terms(link, 4, 6, inv)

        def inner(name, src, ks, ys, degrees):
            with ExitStack() as ctx2:
                def sb2(n, shape, dt):
                    return ctx2.enter_context(nc.sbuf_tensor(f"{name}_{n}", shape, dt))

                def sem(n):
                    return ctx2.enter_context(nc.semaphore(f"{name}_{n}"))

                strip = sb2("strip", [128, SR, NT, TP], F16)
                z = sb2("z", [128, NT, 2, 2, D], F16)
                y = sb2("y", [128, SR, 2, 2, D], F16)
                acc = ctx2.enter_context(nc.psum_tensor(f"{name}_acc", [128, SR, BANK], F32))
                p_deg = ctx2.enter_context(nc.psum_tensor(f"{name}_deg", [128, BANK], F32))
                part_deg = sb2("part_deg", [128, NT, 4], F32)
                deg_made = sem("deg_made")
                strip_in = [sem(f"strip_in{j}") for j in range(SR)]
                hi_made = sem("hi_made")
                lo_made = sem("lo_made")
                sum_done = sem("sum_done")
                y_hi = sem("y_hi")
                y_lo = sem("y_lo")
                y_out = [dram.pool_sem(f"{name}_y_out{j}") for j in range(SR)]
                with nc.Block() as block:
                    @block.sync
                    def _(sp):
                        def tile(t, j, before):
                            if not isinstance(before, int):
                                sp.wait_ge(sum_done, t + (1 - SR))
                            sp.dma_start(strip[:, j], src[bass.ds(t, 1)].rearrange("a r k c -> r (a k) c")).then_inc(strip_in[j], 16)

                        for_ring(sp, tile)

                    def deg_columns(t):
                        return p_deg[0:TP, bass.ds(t * 4, 4)]

                    @block.tensor
                    def _(pe):
                        def tile(t, j, before):
                            pe.wait_ge(strip_in[j], before * 16 + 16)
                            if not isinstance(before, int):
                                pe.wait_ge(y_lo, t + (1 - SR))
                            for kt in range(NT):
                                if isinstance(t, int) and t == 0:
                                    pe.wait_ge(lo_made, 2 * kt + 2)
                                if degrees:
                                    first = isinstance(t, int) and t == 0 and kt == 0
                                    nc.tensor.matmul(deg_columns(t), strip[0:TP, j, kt, :], vdeg[0:TP, kt, :],
                                                     start=first, stop=False, skip_group_check=True)
                                for part in range(2):
                                    mm = nc.tensor.matmul(acc[0:TP, j, :], strip[0:TP, j, kt, :],
                                                          z[0:TP, kt, part].rearrange("p k d -> p (k d)"),
                                                          start=(kt == 0 and part == 0), stop=(kt == NT - 1 and part == 1))
                            mm.then_inc(sum_done, 1)

                        for_ring(pe, tile)

                    @block.scalar
                    def _(act):
                        def split(t, j, before):
                            for i, k in enumerate(ks):
                                nc.scalar.activation(z[0:TP, bass.ds(t, 1), 0, i, :].rearrange("p a d -> p (a d)"),
                                                     xl[0:TP, bass.ds(t, 1), :].rearrange("p a d -> p (a d)"), ACT.Copy,
                                                     scale=roots[0:TP, 0, k, bass.ds(t, 1)]).then_inc(hi_made, 1)

                        for_ring(act, split)

                        def tile(t, j, before):
                            act.wait_ge(sum_done, t + 1)
                            if not isinstance(before, int):
                                act.wait_ge(y_out[j], before * 32)
                            nc.scalar.activation(y[0:TP, j, :, 0, :], acc[0:TP, j, :].rearrange("p (k d) -> p k d", k=2), ACT.Copy,
                                                 scale=scales[0:TP, 4:5]).then_inc(y_hi, 1)

                        for_ring(act, tile)

                    @block.vector
                    def _(dve):
                        def split(t, j, before):
                            for i, k in enumerate(ks):
                                dve.wait_ge(hi_made, t * 2 + i + 1)
                                nc.vector.scalar_tensor_tensor(
                                    out=z[0:TP, bass.ds(t, 1), 1, i, :].rearrange("p a d -> p (a d)"),
                                    in0=xl[0:TP, bass.ds(t, 1), :].rearrange("p a d -> p (a d)"), scalar=roots[0:TP, 0, k, bass.ds(t, 1)],
                                    in1=z[0:TP, bass.ds(t, 1), 0, i, :].rearrange("p a d -> p (a d)"), op0=ALU.mult,
                                    op1=ALU.subtract).then_inc(lo_made, 1)

                        for_ring(dve, split)

                        def tile(t, j, before):
                            dve.wait_ge(y_hi, t + 1)
                            nc.vector.scalar_tensor_tensor(out=y[0:TP, j, :, 1, :], in0=acc[0:TP, j, :].rearrange("p (k d) -> p k d", k=2),
                                                           scalar=scales[0:TP, 4:5], in1=y[0:TP, j, :, 0, :], op0=ALU.mult,
                                                           op1=ALU.subtract).then_inc(y_lo, 1)

                        for_ring(dve, tile)
                        if degrees:
                            nc.vector.tensor_copy(part_deg[0:TP].rearrange("p t k -> p (t k)"), p_deg[0:TP, 0:NT * 4]).then_inc(deg_made, 1)
                            dve.wait_ge(deg_made, 1)
                            nc.vector.tensor_tensor(deg[0:TP, :, T_ROWS:T_COLS + 1], part_deg[0:TP, :, 0:2], part_deg[0:TP, :, 2:4],
                                                    ALU.add).then_inc(deg_made, 1)

                    @block.gpsimd
                    def _(pool):
                        def tile(t, j, before):
                            pool.wait_ge(y_lo, t + 1)
                            for i in range(2):
                                pool.dma_start(ys[i][bass.ds(t, 1)].rearrange("a p n -> p (a n)"),
                                               y[0:TP, j, i].rearrange("p s d -> p (s d)")).then_inc(y_out[j], 16)

                        for_ring(pool, tile)
                        for j in range(SR):
                            pool.wait_ge(y_out[j], 32 * (NT // SR))

        def outer(name, src, ks, ys):
            with ExitStack() as ctx2:
                def sb2(n, shape, dt):
                    return ctx2.enter_context(nc.sbuf_tensor(f"{name}_{n}", shape, dt))

                def sem(n):
                    return ctx2.enter_context(nc.semaphore(f"{name}_{n}"))

                def ps(n, shape):
                    return ctx2.enter_context(nc.psum_tensor(f"{name}_{n}", shape, F32))

                KD = D // 128
                strip = sb2("strip", [128, SR, NT, TP], F16)
                z = sb2("z", [128, NT, 3, 2, D], F16)
                u = sb2("u", [128, 2, 3, D], F32)
                own = sb2("own", [128, 2, D], F32)
                uT = sb2("uT", [128, 3 * KD, 128], F32)
                w = sb2("w", [128, 3, KD, D], F32)
                b = sb2("b", [3, D], F32)
                acc = ps("acc", [128, 2, 2, BANK])
                turn = ps("turn", [128, 2, BANK])
                p_out = ps("out", [128, 2, BANK])
                strip_in = [sem(f"strip_in{j}") for j in range(SR)]
                z_in = [sem(f"z_in{c}") for c in range(SR)]
                w_in = sem("w_in")
                hi_made = sem("hi_made")
                lo_made = sem("lo_made")
                sum_done = sem("sum_done")
                own_made = sem("own_made")
                u_made = sem("u_made")
                u0_made = sem("u0_made")
                turned = sem("turned")
                uT_made = sem("uT_made")
                out_done = sem("out_done")
                added = sem("added")
                with nc.Block() as block:
                    @block.sync
                    def _(sp):
                        def features_and_weights():
                            for c in range(SR):
                                at = slice(c * GT, (c + 1) * GT)
                                for i in range(2):
                                    sp.dma_start(z[0:TP, at, i + 1].rearrange("p t s d -> p t (s d)"), ys[i][at].rearrange("t p n -> p t n")).then_inc(z_in[c], 16)
                            for n, k in enumerate(ks):
                                sp.dma_start(w[:, n], gw[k].rearrange("(k p) o -> p k o", p=128)).then_inc(w_in, 16)
                                sp.dma_start(b[n:n + 1, :], gbias[k:k + 1, :]).then_inc(w_in, 16)

                        def tile(t, j, before):
                            if not isinstance(before, int):
                                sp.wait_ge(sum_done, t + (1 - SR))
                            sp.dma_start(strip[:, j], src[bass.ds(t, 1)].rearrange("a r k c -> r (a k) c")).then_inc(strip_in[j], 16)
                            if isinstance(t, int) and t == 0:
                                features_and_weights()

                        for_ring(sp, tile)

                    @block.tensor
                    def _(pe):
                        def sums(j, p, kts, first=False):
                            for kt in kts:
                                if first and kt % GT == 0:
                                    pe.wait_ge(z_in[kt // GT], 32)
                                if first:
                                    pe.wait_ge(lo_made, kt + 1)
                                for part in range(2):
                                    for half, (k0, k1) in enumerate(((1, 3), (0, 1))):
                                        mm = nc.tensor.matmul(acc[0:TP, p, half, 0:(k1 - k0) * D].rearrange("p (k d) -> p k d", d=D),
                                                              strip[0:TP, j, kt, :], z[0:TP, kt, k0:k1, part, :],
                                                              start=(kt == 0 and part == 0), stop=(kt == NT - 1 and part == 1))
                            return mm

                        def turn_u(t, p):
                            pe.wait_ge(u_made, t * 2 + 2)
                            pe.wait_ge(u0_made, t + 1)
                            if not isinstance(t, int) or t >= 1:
                                pe.wait_ge(uT_made, t * 2)
                            for n in range(3 * KD):
                                mm = nc.tensor.transpose(turn[:, n // 4, (n % 4) * 128:(n % 4) * 128 + TP],
                                                         u[0:TP, p, n // KD, (n % KD) * 128:(n % KD + 1) * 128], ident[0:TP, 0:TP])
                            mm.then_inc(turned, 1)

                        def weigh(t, p):
                            pe.wait_ge(uT_made, t * 2 + 2)
                            if not isinstance(t, int) or t >= 2:
                                pe.wait_ge(added, t - 1)
                            for n in range(3 * KD):
                                nc.tensor.matmul(p_out[0:TP, p, 0:D], uT[:, n, 0:TP], w[:, n // KD, n % KD, :], start=(n == 0), stop=False)
                            nc.tensor.matmul(p_out[0:TP, p, 0:D], ones[0:3, 0:TP], b[:], start=False, stop=True).then_inc(out_done, 1)

                        def tile(t, j, before, p):
                            pe.wait_ge(strip_in[j], before * 16 + 16)
                            if not isinstance(t, int) or t >= 2:
                                pe.wait_ge(u_made, (t - 1) * 2)
                                pe.wait_ge(u0_made, t - 1)
                            first = isinstance(t, int) and t == 0
                            if isinstance(t, int) and t == 1:
                                pe.wait_ge(w_in, 96)
                            sums(j, p, range(0, 8), first)
                            if not isinstance(t, int) or t >= 1:
                                turn_u(t - 1, 1 - p)
                            sums(j, p, range(8, 16), first)
                            if not isinstance(t, int) or t >= 1:
                                weigh(t - 1, 1 - p)
                            sums(j, p, range(16, NT), first).then_inc(sum_done, 1)

                        for_ring2(pe, tile)
                        turn_u(NT - 1, (NT - 1) % 2)
                        weigh(NT - 1, (NT - 1) % 2)

                    @block.scalar
                    def _(act):
                        def split(t, j, before):
                            nc.scalar.activation(z[0:TP, bass.ds(t, 1), 0, 0, :].rearrange("p a d -> p (a d)"),
                                                 xl[0:TP, bass.ds(t, 1), :].rearrange("p a d -> p (a d)"), ACT.Copy,
                                                 scale=roots[0:TP, 0, ks[0], bass.ds(t, 1)]).then_inc(hi_made, 1)

                        for_ring(act, split)

                        def copy_turned(t):
                            act.wait_ge(turned, t + 1)
                            if not isinstance(t, int) or t >= 1:
                                act.wait_ge(out_done, t)
                            nc.scalar.copy(uT[:, 0:4, 0:TP], turn[:, 0].rearrange("p (n m) -> p n m", m=128)[:, :, 0:TP]).then_inc(uT_made, 1)
                            nc.scalar.copy(uT[:, 4:6, 0:TP], turn[:, 1, 0:256].rearrange("p (n m) -> p n m", m=128)[:, :, 0:TP]).then_inc(uT_made, 1)

                        def tile(t, j, before, p):
                            if not isinstance(t, int) or t >= 1:
                                copy_turned(t - 1)
                            if not isinstance(t, int) or t >= 2:
                                act.wait_ge(u0_made, t - 1)
                            nc.scalar.activation(own[0:TP, p], xl[0:TP, bass.ds(t, 1), :].rearrange("p a d -> p (a d)"), ACT.Copy,
                                                 scale=both[0:TP, ks[0], bass.ds(t, 1)]).then_inc(own_made, 1)
                            act.wait_ge(sum_done, t + 1)
                            if not isinstance(t, int) or t >= 2:
                                act.wait_ge(turned, t - 1)
                            nc.scalar.activation(u[0:TP, p, 1], acc[0:TP, p, 0, 0:D], ACT.Copy,
                                                 scale=roots[0:TP, 1, ks[1], bass.ds(t, 1)]).then_inc(u_made, 1)
                            nc.scalar.activation(u[0:TP, p, 2], acc[0:TP, p, 0, D:2 * D], ACT.Copy,
                                                 scale=roots[0:TP, 1, ks[2], bass.ds(t, 1)]).then_inc(u_made, 1)

                        for_ring2(act, tile)
                        copy_turned(NT - 1)

                    @block.vector
                    def _(dve):
                        def split(t, j, before):
                            dve.wait_ge(hi_made, t + 1)
                            nc.vector.scalar_tensor_tensor(
                                out=z[0:TP, bass.ds(t, 1), 0, 1, :].rearrange("p a d -> p (a d)"),
                                in0=xl[0:TP, bass.ds(t, 1), :].rearrange("p a d -> p (a d)"), scalar=roots[0:TP, 0, ks[0], bass.ds(t, 1)],
                                in1=z[0:TP, bass.ds(t, 1), 0, 0, :].rearrange("p a d -> p (a d)"), op0=ALU.mult,
                                op1=ALU.subtract).then_inc(lo_made, 1)

                        for_ring(dve, split)

                        def add(t, p):
                            dve.wait_ge(out_done, t + 1)
                            xt = xs[0:TP, bass.ds(t, 1), :].rearrange("p a d -> p (a d)")
                            nc.vector.tensor_tensor(xt, xt, p_out[0:TP, p, 0:D], ALU.add).then_inc(added, 1)

                        def tile(t, j, before, p):
                            dve.wait_ge(own_made, t + 1)
                            dve.wait_ge(sum_done, t + 1)
                            if not isinstance(t, int) or t >= 2:
                                dve.wait_ge(turned, t - 1)
                            nc.vector.scalar_tensor_tensor(out=u[0:TP, p, 0], in0=acc[0:TP, p, 1, 0:D],
                                                           scalar=roots[0:TP, 1, ks[0], bass.ds(t, 1)], in1=own[0:TP, p],
                                                           op0=ALU.mult, op1=ALU.add).then_inc(u0_made, 1)
                            if not isinstance(t, int) or t >= 1:
                                add(t - 1, 1 - p)

                        for_ring2(dve, tile)
                        add(NT - 1, (NT - 1) % 2)

        inner("it", dram.adj, (3, 5), (dram.y[1], dram.y[3]), True)
        more_roots()
        inner("ia", dram.adj_t, (2, 4), (dram.y[0], dram.y[2]), False)
        outer("oa", dram.adj_t, (0, 2, 3), (dram.y[0], dram.y[1]))
        outer("ot", dram.adj, (1, 4, 5), (dram.y[2], dram.y[3]))


def gnn_and_experts(nc, ap, out):
    with ExitStack() as ctx:
        dram = Scratch(nc, ctx)
        ident, ident16, ones, ones16 = consts(nc, ctx)
        col_part = ctx.enter_context(nc.sbuf_tensor("col_part", [128, NT, NB], F32))
        deg = ctx.enter_context(nc.sbuf_tensor("deg", [128, NT, 6], F32))
        xs = ctx.enter_context(nc.sbuf_tensor("xs", [128, NT, D], F32))
        scales = ctx.enter_context(nc.sbuf_tensor("scales", [128, 8], F32))
        fill = ctx.enter_context(nc.semaphore("fill"))
        with nc.Block() as block:
            @block.vector
            def _(dve):
                nc.vector.memset(scales[:, 3:4], 1e-5).then_inc(fill, 1)
                dve.wait_ge(fill, 1)
        with ExitStack() as ctx2:
            att = Attention(nc, ctx2)
            prepare(nc, ap["x"], ap["w"], ap["wlr"], ap["wl_rows"], ap["src_dst"], ap["dst"], dram, ident, ident16, ones,
                    col_part, deg, xs, scales, att)
            graph_attention(nc, ap["x"], ap["gat_b"], dram, ones, att, deg, xs, scales)
        mixture(nc, 0, xs, {k[3:]: v for k, v in ap.items() if k.startswith("f0_")}, ident, ones, scales, dram.slot_x, dram.slot_y, 512, dram.pool_sem)
        clear_semaphores(nc)
        graph_convolution(nc, xs, ap["g1_w"], ap["g1_b"], dram, ident, ones, deg, scales)
        clear_semaphores(nc)
        mixture(nc, 1, xs, {k[3:]: v for k, v in ap.items() if k.startswith("f1_")}, ident, ones, scales, dram.slot_x, dram.slot_y, 256, dram.pool_sem)
        stored = ctx.enter_context(nc.semaphore("stored"))
        with nc.Block() as block:
            @block.sync
            def _(sp):
                sp.dma_start(out.rearrange("(t p) d -> p t d", p=TP), xs[0:TP]).then_inc(stored, 16)
                sp.wait_ge(stored, 16)



def lay_out(inputs):
    inputs = {k: np.asarray(v) for k, v in inputs.items()}
    laid = {
        "x": inputs["x"], "src_dst": np.stack([inputs["src"], inputs["dst"]]), "dst": inputs["dst"],
        "w": inputs["L0_gnn_W"],
        "wlr": np.concatenate([inputs["L0_gnn_Wl"], inputs["L0_gnn_Wr"]]).T,
        "gat_b": np.broadcast_to(np.tile(inputs["L0_gnn_b"], HEADS), (TP, D)),
        "f0_gb": np.broadcast_to(np.stack([inputs["L0_ffn_gamma"], inputs["L0_ffn_beta"]]), (TP, 2, D)),
        "f0_wr": inputs["L0_ffn_Wr"], "f0_br": inputs["L0_ffn_br"][None],
        "f0_w1": inputs["L0_ffn_W1"], "f0_w2": inputs["L0_ffn_W2"],
        "f0_b1": np.broadcast_to(inputs["L0_ffn_b1"], (128, NE, 512)),
        "f0_b2": np.broadcast_to(inputs["L0_ffn_b2"], (128, NE, D)),
        "g1_w": inputs["L1_gnn_W"].transpose(0, 2, 1), "g1_b": inputs["L1_gnn_b"],
        "f1_wr": inputs["L1_ffn_router_w"].T, "f1_br": np.zeros((1, NE), np.float32),
        "f1_w1": inputs["L1_ffn_w1"], "f1_w2": inputs["L1_ffn_w2"],
        "f1_b1": np.broadcast_to(inputs["L1_ffn_b1"], (128, NE, D)),
        "f1_b2": np.broadcast_to(inputs["L1_ffn_b2"], (128, NE, D)),
        "wl_rows": np.broadcast_to(inputs["L0_gnn_Wl"].T[:, :, None], (HD, HEADS, TP)),
    }
    return {name: np.ascontiguousarray(a) for name, a in laid.items()}


def kernel(**inputs):
    import concourse.bacc as _bacc
    from concourse.bass_utils import run_bass_kernel_spmd as _run

    nc = _bacc.Bacc("TRN2", target_bir_lowering=False, num_devices=1)
    arrays, ap = {}, {}
    for name, a in lay_out(inputs).items():
        arrays[f"in_{name}"] = a
        ap[name] = nc.dram_tensor(f"in_{name}", a.shape, mybir.dt.from_np(a.dtype), kind="ExternalInput").ap()
    out = nc.dram_tensor("out_0", (N, D), F32, kind="ExternalOutput").ap()
    gnn_and_experts(nc, ap, out)
    r = _run(nc, [arrays], core_ids=[0])
    return r.results[0]["out_0"]
```

```python
from contextlib import ExitStack

import concourse.bass as bass
import concourse.mybir as mybir
import numpy as np

F32 = mybir.dt.float32
F16 = mybir.dt.float16
I32 = mybir.dt.int32
U32 = mybir.dt.uint32
ALU = mybir.AluOpType
ACT = mybir.ActivationFunctionType
AX = mybir.AxisListType

N = 3125
E = 50000
D = 256
TP = 125
NT = N // TP
GT = 5
NG = NT // GT
GW = GT * TP
BANK = 512
BANKS = [(b, min(BANK, N - b)) for b in range(0, N, BANK)]
NB = len(BANKS)
WC = 17
WE = WC * 128
GC = 20
GWIN = E // (GC * TP)
RING = 6
GRING = 5
MID = 1600


def for_tiles(eng, step, n=NT):
    peel = 2 + n % 2
    for t in range(peel):
        step(t, t % 2, t // 2)
    with eng.Fori(0, (n - peel) // 2) as i:
        for j in range(2):
            step(i * 2 + (peel + j), (peel + j) % 2, i + (peel + j) // 2)


def for_cycle(eng, step, n, size):
    peel = size + n % size
    for t in range(peel):
        step(t, t % size, t // size)
    with eng.Fori(0, (n - peel) // size) as i:
        for j in range(size):
            step(i * size + (peel + j), (peel + j) % size, i + (peel + j) // size)


SR = 5


def for_ring(eng, step):
    for j in range(SR):
        step(j, j, 0)
    with eng.Fori(1, NT // SR) as g:
        for j in range(SR):
            step(g * SR + j, j, g)


def for_ring2(eng, step):
    for t in range(SR):
        step(t, t, 0, t % 2)
    with eng.Fori(0, (NT - SR) // (2 * SR)) as i:
        for n in range(2 * SR):
            t = SR + n
            step(i * (2 * SR) + t, n % SR, i * 2 + (1 + n // SR), t % 2)


def clear_semaphores(nc):
    nums = sorted(nc.released_uncleared_semaphores)
    with nc.Block() as block:
        @block.gpsimd
        def _(pool):
            first = 0
            for n in range(1, len(nums) + 1):
                if n == len(nums) or nums[n] != nums[n - 1] + 1:
                    pool.sem_clear(range(nums[first], nums[n - 1] + 1))
                    first = n


class Scratch:

    def __init__(self, nc, ctx):
        self.pool_sem = lambda name: ctx.enter_context(nc.semaphore(name))
        self.adj_t = nc.dram_tensor("adj_t", [NT, 128, NT, TP], F16).ap()
        self.slot_x = nc.dram_tensor("slot_x", [NE * ROOM + SLOT, D], F32).ap()
        self.slot_y = nc.dram_tensor("slot_y", [NBLK * SLOT, D], F32).ap()
        self.y = [nc.dram_tensor(f"y{k}", [NT, TP, 2 * D], F16).ap() for k in (2, 3, 4, 5)]
        self.adj = nc.dram_tensor("adj", [NT, 128, NT, TP], F16).ap()


def consts(nc, ctx):
    ident = ctx.enter_context(nc.sbuf_tensor("ident", [128, 128], F32))
    ident16 = ctx.enter_context(nc.sbuf_tensor("ident16", [128, 128], F16))
    ones = ctx.enter_context(nc.sbuf_tensor("ones", [128, 128], F32))
    ones16 = ctx.enter_context(nc.sbuf_tensor("ones16", [128, 1], F16))
    made = ctx.enter_context(nc.semaphore("consts_made"))
    with nc.Block() as block:
        @block.gpsimd
        def _(pool):
            nc.gpsimd.memset(ident[:], 0.0).then_inc(made, 1)
            nc.gpsimd.memset(ident16[:], 0.0).then_inc(made, 1)
            nc.gpsimd.memset(ones[:], 1.0).then_inc(made, 1)
            nc.gpsimd.memset(ones16[:], 1.0).then_inc(made, 1)
            pool.wait_ge(made, 4)
            for m in (ident, ident16):
                nc.gpsimd.affine_select(out=m[:], in_=m[:], compare_op=ALU.not_equal, fill=1.0, base=0,
                                        pattern=[[-1, 128]], channel_multiplier=1).then_inc(made, 1)
            pool.wait_ge(made, 6)
    return ident, ident16, ones, ones16


HEADS = 4
HD = 64
HF = 2 * (HD + 1)
HROOM = 8192.0
EL, ER = 0, HEADS


class Attention:

    def __init__(self, nc, ctx):
        def sb(name, shape, dt):
            return ctx.enter_context(nc.sbuf_tensor(name, shape, dt))

        self.feats = sb("feats", [128, NT, HEADS, 2, HF], F16)
        self.rows = sb("el_rows", [128, HEADS * N], F32)
        self.lr = sb("lr", [128, NT, 2 * HEADS], F32)
        self.ner = sb("ner", [128, NT, HEADS], F32)
        self.pows = sb("pows", [128, 4, NT, HEADS], F32)
        self.vdeg = sb("vdeg", [128, NT, 4], F16)


def prepare(nc, x, w, wlr, wl_rows, src_dst, dst, dram, ident, ident16, ones, col_part, deg, xs, scales, att):
    feats, rows, lr, ner, pows, vdeg = att.feats, att.rows, att.lr, att.ner, att.pows, att.vdeg
    with ExitStack() as ctx:
        def sb(name, shape, dt):
            return ctx.enter_context(nc.sbuf_tensor(name, shape, dt))

        def sem(name):
            return ctx.enter_context(nc.semaphore(name))

        EP = E // TP
        HEAD = 3
        PB = 8
        rounds = [(q, min(PB, NT - q)) for q in range(0, NT, PB)]
        NR = len(rounds)
        TURN_AT = {5: 0, 8: 1, 11: 2, 14: 3}
        iota_r = sb("iota_r", [128, N], F16)
        iota_c = sb("iota_c", [128, TP], F16)
        cnt = sb("cnt", [128, NT + 2], F32)
        off_i = sb("off_i", [1, NT], I32)
        flag_i = sb("flag_i", [1, 1], I32)
        tile_base = sb("tile_base", [128, NT], F32)
        win_buf = sb("win", [128, NT * 2 * WC], I32)
        gwin = sb("gwin", [128, 2, GC], I32)
        gloc = sb("gloc", [128, 2, GC], F32)
        hot_c = sb("hot_c", [128, RING, TP], F16)
        hot_r = sb("hot_r", [128, RING, N], F16)
        zeros = sb("zeros", [128, TP], F16)
        strip = sb("strip", [128, 2, N], F16)
        turned = sb("turned", [128, 2, NT, TP], F16)
        tile_sum = sb("tile_sum", [128, 2, NT], F32)
        row_sum = sb("row_sum", [128, NT], F32)
        w_sb = sb("w_sb", [128, 2, HD], F32)
        wlr_sb = sb("wlr_sb", [HD, 2 * HEADS], F32)
        wl_sb = sb("wl_sb", [HD, HEADS, TP], F32)
        mx = sb("mx", [128, 4], F32)
        mrow = sb("mrow", [1, 8], F32)
        win = win_buf[:].rearrange("p (t s k) -> p t s k", s=2, k=WC)
        dst_a, dst_b = win_buf[:, 0:EP], win_buf[:, EP:2 * EP]
        h_all = rows[:, 0:NT * D].rearrange("p (t d) -> p t d", d=D)
        at = NT * D
        hT = rows[:, at:at + SR * 256].rearrange("p (j k n) -> p j k n", j=SR, k=2)
        at += SR * 256
        dst_f = rows[:, at:at + EP]
        less = rows[:, at + EP:at + 3 * EP].rearrange("p (i k) -> p i k", i=2)
        at += 3 * EP
        stats = rows[:, at:at + NT * 6].rearrange("p (t k) -> p t k", k=6)
        norm = rows[:, at + NT * 6:at + NT * 10].rearrange("p (i t k) -> p i t k", i=2, k=2)
        at += NT * 10
        row = rows[0:1, at:at + 8 * (NT + 2)].rearrange("p (i k) -> p i k", i=8)
        xs_flat = xs[:].rearrange("p t d -> p (t d)")
        f = xs_flat[0:TP, 0:NT * (HD + 1)].rearrange("p (t d) -> p t d", d=HD + 1)
        xw = xs_flat[0:TP, NT * (HD + 1):NT * (2 * HD + 1)].rearrange("p (t d) -> p t d", d=HD)
        xwT = xs_flat[0:HD, NT * (2 * HD + 1):NT * (2 * HD + 1) + N]
        loc_at = NT * (2 * HD + 1)
        loc_src, loc_dst = (xs_flat[:, loc_at + i * NT * WC:loc_at + (i + 1) * NT * WC].rearrange("p (t k) -> p t k", k=WC) for i in range(2))
        acc = ctx.enter_context(nc.psum_tensor("acc", [128, NB, BANK], F32))
        turn = ctx.enter_context(nc.psum_tensor("turn", [128, PB, 128], F16))
        small = acc[:, NB - 1, :]
        XWT, XW = 2 * 128, 3 * 128
        LR, MX, SC = 0, 256, 208

        edges_in = sem("edges_in")
        x_in = sem("x_in")
        w_in = sem("w_in")
        iotas = sem("iotas")
        dve_chain = sem("dve_chain")
        counted = sem("counted")
        summed = sem("summed")
        offsets = sem("offsets")
        windows_in = sem("windows_in")
        stats_made = sem("stats_made")
        norm_made = sem("norm_made")
        rooted = sem("rooted")
        h_made = sem("h_made")
        h_turned = sem("h_turned")
        hT_made = sem("hT_made")
        xw_done = sem("xw_done")
        xw_made = sem("xw_made")
        lr_done = sem("lr_done")
        lr_made = sem("lr_made")
        rows_done = sem("rows_done")
        rows_made = sem("rows_made")
        pows_made = sem("pows_made")
        maxima = sem("maxima")
        maxima_row = sem("maxima_row")
        scale_row = sem("scale_row")
        scale_all = sem("scale_all")
        scaled = sem("scaled")
        feat_chain = sem("feat_chain")
        local = sem("local")
        cleared = sem("cleared")
        hot_ready = sem("hot_ready")
        hot_used = sem("hot_used")
        bank_done = sem("bank_done")
        bank_free = sem("bank_free")
        strip_out = [sem("strip_out0"), sem("strip_out1")]
        turn_done = sem("turn_done")
        turn_free = sem("turn_free")
        turned_out = [sem("turned_out0"), sem("turned_out1")]
        summed_rows = sem("summed_rows")
        gwin_in = sem("gwin_in")
        gwin_used = sem("gwin_used")
        ghot_ready = sem("ghot_ready")
        ghot_used = sem("ghot_used")
        slots_seen = sem("slots_seen")

        with nc.Block() as block:
            @block.sync
            def _(sp):
                last = (TP - 1) * EP
                sp.dma_start(dst_a[0:TP, :], dst.rearrange("(p k) -> p k", k=EP)).then_inc(edges_in, 16)
                sp.dma_start(dst_b[0:TP - 1, :], dst[1:last + 1].rearrange("(p k) -> p k", k=EP)).then_inc(edges_in, 16)
                sp.dma_start(dst_b[TP - 1:TP, 0:EP - 1], dst[last + 1:E].rearrange("(p k) -> p k", p=1)).then_inc(edges_in, 16)
                sp.dma_start(dst_b[TP - 1:TP, EP - 1:EP], dst[E - 1:E].rearrange("(p k) -> p k", p=1)).then_inc(edges_in, 16)
                sp.dma_start(xs[0:TP], x.rearrange("(t p) d -> p t d", p=TP)).then_inc(x_in, 16)
                sp.dma_start(w_sb[:], w.rearrange("(k p) n -> p k n", k=2)).then_inc(w_in, 16)
                sp.dma_start(wlr_sb[:], wlr).then_inc(w_in, 16)
                sp.dma_start(wl_sb[:], wl_rows).then_inc(w_in, 16)
                sp.wait_ge(offsets, 1)
                with sp.Fori(0, NT) as t:
                    off = sp.value_load(off_i[0:1, bass.ds(t, 1)], min_val=0, max_val=E - WE)
                    sp.dma_start(win[:, bass.ds(t, 1), :, :].rearrange("p a s k -> p (a s) k"),
                                 src_dst[:, bass.ds(off, WE)].rearrange("s (p k) -> p s k", k=WC)).then_inc(windows_in, 16)
                general = sp.value_load(flag_i[0:1, 0:1], min_val=0, max_val=1)

                def store_turned(t, par):
                    sp.wait_ge(turn_free, (t + 1) * NR)
                    sp.dma_start(dram.adj[bass.ds(t, 1)].rearrange("a r k c -> r (a k) c"), turned[:, par]).then_inc(turned_out[par], 16)

                def tile(t, par, before):
                    with sp.If(general):
                        with sp.Fori(0, GWIN) as g:
                            sp.wait_ge(gwin_used, (t * GWIN + g) * 2 + 1)
                            first = g * (GC * TP)
                            for i in range(2):
                                sp.dma_start(gwin[0:TP, i, :], src_dst[i, bass.ds(first, GC * TP)].rearrange("(p k) -> p k", k=GC)).then_inc(gwin_in, 16)
                    sp.wait_ge(bank_free, (t + 2) * NB)
                    sp.dma_start(dram.adj_t[:, :, bass.ds(t, 1), :].rearrange("g c a r -> c g (a r)"),
                                 strip[:, par, :].rearrange("c (g r) -> c g r", g=NT)).then_inc(strip_out[par], 16)
                    if not isinstance(t, int) or t >= 1:
                        store_turned(t - 1, 1 - par)

                for_tiles(sp, tile)
                store_turned(NT - 1, (NT - 1) % 2)
                for out in (strip_out, turned_out):
                    sp.wait_ge(out[0], 16 * (NT // 2 + 1))
                    sp.wait_ge(out[1], 16 * (NT // 2))

            @block.gpsimd
            def _(pool):
                nc.gpsimd.iota(iota_r[:], [[1, N]], base=-MID, channel_multiplier=0,
                               allow_small_or_imprecise_dtypes=True).then_inc(iotas, 1)
                nc.gpsimd.iota(iota_c[:], [[1, TP]], base=0, channel_multiplier=0,
                               allow_small_or_imprecise_dtypes=True).then_inc(iotas, 1)
                nc.gpsimd.iota(tile_base[:], [[TP, NT]], base=0, channel_multiplier=0,
                               allow_small_or_imprecise_dtypes=True).then_inc(iotas, 1)
                nc.gpsimd.memset(zeros[:], 0.0).then_inc(cleared, 1)
                nc.gpsimd.memset(strip[:], 0.0).then_inc(cleared, 1)
                nc.gpsimd.memset(turned[:], 0.0).then_inc(cleared, 1)
                nc.gpsimd.memset(row_sum[:], 0.0).then_inc(cleared, 1)
                link = Chain(pool, feat_chain)
                pool.wait_ge(scaled, 1)
                for n in range(2 * HEADS):
                    h, kind = n // 2, n % 2
                    p = pows[0:TP, 2 + kind, :, h:h + 1]
                    o = kind * (HD + 1)
                    hi = feats[0:TP, :, h, 0, o:o + HD + 1]
                    link(nc.gpsimd.tensor_copy(f[:, :, HD:HD + 1], p))
                    link(nc.gpsimd.tensor_tensor(f[:, :, 0:HD], xw, p.to_broadcast([TP, NT, HD]), ALU.mult))
                    link(nc.gpsimd.tensor_copy(hi, f))
                    link(nc.gpsimd.tensor_tensor(feats[0:TP, :, h, 1, o:o + HD + 1], f, hi, ALU.subtract))

            @block.vector
            def _(dve):
                link = Chain(dve, dve_chain)

                dve.wait_ge(edges_in, 64)
                link(nc.vector.tensor_copy(dst_f[0:TP, :], dst_a[0:TP, :]))
                link(nc.vector.memset(cnt[:], 0.0))
                for t in range(1, NT + 1):
                    if t >= 3:
                        dve.wait_ge(dve_chain, t)
                    link.count += 1
                    nc.vector.tensor_scalar(less[0:TP, t % 2, :], dst_f[0:TP, :], float(TP * t), 0.0, ALU.is_lt,
                                            ALU.add, accum_out=cnt[0:TP, t:t + 1]).then_inc(dve_chain, 1)
                dve.wait_ge(dve_chain, link.count)
                link(nc.vector.tensor_tensor(less[0:TP, 0, :], dst_a[0:TP, :], dst_b[0:TP, :], ALU.is_gt))
                nc.vector.tensor_reduce(cnt[0:TP, NT + 1:NT + 2], less[0:TP, 0, :], AX.X, ALU.add).then_inc(counted, 1)
                dve.wait_ge(summed, 1)
                link(nc.vector.tensor_copy(row[:, 0, :], small[0:1, 0:NT + 2]))
                link(nc.vector.tensor_tensor(row[:, 1, 0:NT], row[:, 0, 1:NT + 1], row[:, 0, 0:NT], ALU.subtract))
                link(nc.vector.tensor_scalar(row[:, 2, 0:NT], row[:, 1, 0:NT], float(WE), None, ALU.is_gt))
                link(nc.vector.tensor_reduce(row[:, 3, 0:1], row[:, 2, 0:NT], AX.X, ALU.add))
                link(nc.vector.tensor_tensor(row[:, 4, 0:1], row[:, 3, 0:1], row[:, 0, NT + 1:NT + 2], ALU.add))
                link(nc.vector.tensor_scalar(flag_i[:], row[:, 4, 0:1], 0.5, None, ALU.is_gt))
                nc.vector.tensor_scalar(off_i[:], row[:, 0, 0:NT], float(E - WE), None, ALU.min).then_inc(offsets, 1)

                dve.wait_ge(x_in, 16)
                layer_norm_all(nc, dve, link, xs, h_all, stats, norm, stats_made, norm_made, rooted, h_made)

                dve.wait_ge(lr_done, 1)
                nc.vector.tensor_copy(lr[0:TP].rearrange("p t k -> p (t k)"), small[0:TP, LR:LR + NT * 2 * HEADS]).then_inc(lr_made, 1)
                dve.wait_ge(lr_made, 1)
                link(nc.vector.tensor_scalar(ner[0:TP], lr[0:TP, :, ER:ER + HEADS], -1.0, None, ALU.mult))
                dve.wait_ge(xw_made, 2 * NT)
                link(nc.vector.tensor_reduce(mx[0:TP, 0:1], xw, AX.XY, ALU.max, apply_absolute_value=True))
                dve.wait_ge(pows_made, 4)
                nc.vector.tensor_reduce(mx[0:TP, 1:2], pows[0:TP, 2:4], AX.XYZ, ALU.max).then_inc(maxima, 1)
                dve.wait_ge(maxima_row, 1)
                link(nc.vector.tensor_reduce(mrow[:, 0:2], small[0:1, MX:MX + 256].rearrange("p (k n) -> p k n", k=2)[:, :, 0:TP], AX.X, ALU.max))
                link(nc.vector.tensor_scalar(mrow[:, 2:3], mrow[:, 0:1], 1.0, None, ALU.max))
                link(nc.vector.tensor_tensor(mrow[:, 3:4], mrow[:, 2:3], mrow[:, 1:2], ALU.mult))
                link(nc.vector.tensor_scalar(mrow[:, 5:6], mrow[:, 3:4], 1.0 / HROOM, None, ALU.mult))
                nc.vector.reciprocal(mrow[:, 4:5], mrow[:, 5:6]).then_inc(scale_row, 1)
                dve.wait_ge(scale_all, 1)
                link(nc.vector.tensor_copy(scales[0:TP, 0:2], small[0:TP, SC:SC + 2]))
                nc.vector.tensor_scalar(pows[0:TP, 2:4], pows[0:TP, 2:4], scales[0:TP, 0:1], None, ALU.mult).then_inc(scaled, 1)

                dve.wait_ge(iotas, 3)
                dve.wait_ge(windows_in, 16 * NT)
                dve.wait_ge(rows_done, HEADS * NB)
                nc.vector.tensor_scalar(loc_src[:], win[:, :, 0, :], float(MID), None, ALU.subtract).then_inc(local, 1)
                nc.vector.tensor_tensor(loc_dst[:], win[:, :, 1, :], tile_base[:].to_broadcast([128, NT, WC]), ALU.subtract).then_inc(local, 1)
                dve.wait_ge(local, 2)
                general = dve.value_load(flag_i[0:1, 0:1], min_val=0, max_val=1)
                dve.sem_inc(gwin_used, 1)
                dve.wait_ge(cleared, 4)

                def chunk(ready, rows_, slot, c_of_edge, r_of_edge):
                    nc.vector.tensor_scalar(hot_c[0:rows_, slot, :], iota_c[0:rows_, :], c_of_edge, None,
                                            ALU.is_equal).then_inc(ready, 1)
                    nc.vector.tensor_scalar(hot_r[0:rows_, slot, :], iota_r[0:rows_, :], r_of_edge, None,
                                            ALU.is_equal).then_inc(ready, 1)

                def sum_rows(t, par):
                    dve.wait_ge(turn_free, (t + 1) * NR)
                    if not isinstance(t, int) or t >= 2:
                        dve.wait_ge(summed_rows, (t - 1) * 2)
                    nc.vector.tensor_reduce(tile_sum[0:TP, par], turned[0:TP, par], AX.X, ALU.add).then_inc(summed_rows, 1)
                    dve.wait_ge(summed_rows, t * 2 + 1)
                    nc.vector.tensor_tensor(row_sum[0:TP], row_sum[0:TP], tile_sum[0:TP, par], ALU.add).then_inc(summed_rows, 1)

                def tile(t, par, before):
                    for k in range(WC):
                        dve.wait_ge(hot_used, t * WC + k + 1 + (k < WC % RING and WC % RING > 0 and RING - WC % RING))
                        c = loc_dst[:, bass.ds(t, 1), k:k + 1].rearrange("p a k -> p (a k)")
                        r = loc_src[:, bass.ds(t, 1), k:k + 1].rearrange("p a k -> p (a k)")
                        chunk(hot_ready, 128, k % RING, c, r)
                        if k == RING and (not isinstance(t, int) or t >= 2):
                            sum_rows(t - 2, par)
                    with dve.If(general):
                        dve.wait_ge(hot_used, t * WC + WC + RING)
                        dve.sem_inc(slots_seen, 1)
                        with dve.Fori(0, GWIN) as g:
                            dve.wait_ge(gwin_in, (t * GWIN + g) * 32 + 32)
                            nc.vector.tensor_scalar(gloc[0:TP, 0, :], gwin[0:TP, 0, :], float(MID), None,
                                                    ALU.subtract).then_inc(gwin_used, 1)
                            nc.vector.tensor_scalar(gloc[0:TP, 1, :], gwin[0:TP, 1, :], tile_base[0:TP, bass.ds(t, 1)], None,
                                                    ALU.subtract).then_inc(gwin_used, 1)
                            dve.wait_ge(gwin_used, (t * GWIN + g) * 2 + 3)
                            for k in range(GC):
                                dve.wait_ge(ghot_used, (t * GWIN + g) * GC + k + 1)
                                chunk(ghot_ready, TP, k % GRING, gloc[0:TP, 1, k:k + 1], gloc[0:TP, 0, k:k + 1])
                            dve.wait_ge(ghot_ready, (t * GWIN + g) * (2 * GC) + 2 * GC)
                            dve.sem_inc(slots_seen, 1)
                        dve.wait_ge(ghot_used, (t * GWIN + GWIN) * GC + GRING)
                        dve.sem_inc(slots_seen, 1)

                for_tiles(dve, tile)
                for t in (NT - 2, NT - 1):
                    sum_rows(t, t % 2)
                dve.wait_ge(summed_rows, 2 * NT)
                dve.wait_ge(bank_free, (NT + 1) * NB)
                link(nc.vector.tensor_reduce(deg[0:TP, :, 1], col_part[0:TP], AX.X, ALU.add))
                link(nc.vector.tensor_copy(deg[0:TP, :, 0], row_sum[0:TP]))
                link(nc.vector.tensor_copy(vdeg[0:TP, :, 0:2], deg[0:TP, :, 0:2]))
                link(nc.vector.tensor_tensor(vdeg[0:TP, :, 2:4], deg[0:TP, :, 0:2], vdeg[0:TP, :, 0:2], ALU.subtract))

            @block.tensor
            def _(pe):
                pe.wait_ge(counted, 1)
                nc.tensor.matmul(small[0:1, 0:NT + 2], ones[0:TP, 0:1], cnt[0:TP, :], start=True, stop=True).then_inc(summed, 1)
                pe.sem_inc(hot_used, RING)
                pe.sem_inc(ghot_used, GRING)
                pe.wait_ge(w_in, 48)

                def product(t, j):
                    pe.wait_ge(hT_made, t + 1)
                    for k in range(2):
                        nc.tensor.matmul(acc[0:HD, j, XWT:XWT + TP], w_sb[:, k, :], hT[:, j, k, 0:TP], start=(k == 0), stop=(k == 1))
                    for k in range(2):
                        mm = nc.tensor.matmul(acc[0:TP, j, XW:XW + HD], hT[:, j, k, 0:TP], w_sb[:, k, :], start=(k == 0), stop=(k == 1))
                    mm.then_inc(xw_done, 1)

                def project(t, j):
                    pe.wait_ge(h_made, t + 1)
                    if t >= SR:
                        pe.wait_ge(xw_made, (t - SR + 1) * 2)
                    for k in range(2):
                        mm = nc.tensor.transpose(acc[:, j, k * 128:k * 128 + TP], h_all[0:TP, t, k * 128:(k + 1) * 128],
                                                 ident[0:TP, 0:TP])
                    mm.then_inc(h_turned, 1)
                    if t >= 1:
                        product(t - 1, (j - 1) % SR)

                for t in range(NT):
                    project(t, t % SR)
                product(NT - 1, (NT - 1) % SR)
                pe.wait_ge(xw_made, 2 * NT)
                for t in range(NT):
                    mm = nc.tensor.matmul(small[0:TP, LR + t * 2 * HEADS:LR + (t + 1) * 2 * HEADS], xwT[:, t * TP:(t + 1) * TP],
                                          wlr_sb[:], start=True, stop=True)
                mm.then_inc(lr_done, 1)
                for n in range(HEADS * NB):
                    h, b = n // NB, n % NB
                    lo, k = BANKS[b]
                    if n >= SR:
                        pe.wait_ge(rows_made, n - SR + 1)
                    nc.tensor.matmul(acc[0:TP, n % SR, 0:k], wl_sb[:, h, :], xwT[:, lo:lo + k], start=True,
                                     stop=True).then_inc(rows_done, 1)
                    if n == 2 * NB:
                        pe.wait_ge(maxima, 1)
                        for k in range(2):
                            mm = nc.tensor.transpose(small[0:1, MX + k * 128:MX + k * 128 + TP], mx[0:TP, k:k + 1], ident[0:TP, 0:TP])
                        mm.then_inc(maxima_row, 1)
                    if n == 3 * NB:
                        pe.wait_ge(scale_row, 1)
                        nc.tensor.matmul(small[0:TP, SC:SC + 2], ones[0:1, 0:TP], mrow[:, 4:6], start=True, stop=True).then_inc(scale_all, 1)

                pe.wait_ge(offsets, 1)
                general = pe.value_load(flag_i[0:1, 0:1], min_val=0, max_val=1)
                pe.wait_ge(cleared, 4)
                pe.wait_ge(iotas, 3)
                pe.wait_ge(scaled, 1)
                pe.wait_ge(rows_made, HEADS * NB)

                def product_of(slot, b):
                    lo, n = BANKS[b]
                    return acc[0:TP, b, 0:n], hot_c[:, slot, :], hot_r[:, slot, lo:lo + n]

                def turn_round(t, par, q):
                    rt0, n = rounds[q]
                    if q == 0:
                        pe.wait_ge(bank_free, (t + 2) * NB)
                    if not (isinstance(t, int) and t * NR + q == 0):
                        pe.wait_ge(turn_free, t * NR + q)
                    for i in range(n):
                        mm = nc.tensor.transpose(turn[0:TP, i, 0:TP], strip[0:TP, par, (rt0 + i) * TP:(rt0 + i + 1) * TP], ident16[0:TP, 0:TP])
                    mm.then_inc(turn_done, 1)

                def tile(t, par, before):
                    for b in range(NB):
                        pe.wait_ge(bank_free, t * NB + b + 1)
                        for k in range(HEAD):
                            if b == 0:
                                pe.wait_ge(hot_ready, t * (2 * WC) + 2 * k + 2)
                            mm = nc.tensor.matmul(*product_of(k % RING, b), start=(k == 0), stop=False)
                            if b == NB - 1:
                                mm.then_inc(hot_used, 1)
                    for k in range(HEAD, WC):
                        if k in TURN_AT and (not isinstance(t, int) or t >= 1):
                            turn_round(t - 1, 1 - par, TURN_AT[k])
                        pe.wait_ge(hot_ready, t * (2 * WC) + 2 * k + 2)
                        for b in range(NB):
                            mm = nc.tensor.matmul(*product_of(k % RING, b), start=False, stop=(k == WC - 1))
                        mm.then_inc(hot_used, 1)
                    with pe.If(general):
                        for b, (lo, n) in enumerate(BANKS):
                            nc.tensor.matmul(acc[0:TP, b, 0:n], zeros[0:TP, :], iota_r[0:TP, lo:lo + n], start=True,
                                             stop=False, skip_group_check=True)
                        with pe.Fori(0, GWIN) as g:
                            for k in range(GC):
                                pe.wait_ge(ghot_ready, (t * GWIN + g) * (2 * GC) + 2 * k + 2)
                                for b, (lo, n) in enumerate(BANKS):
                                    mm = nc.tensor.matmul(acc[0:TP, b, 0:n], hot_c[0:TP, k % GRING, :],
                                                          hot_r[0:TP, k % GRING, lo:lo + n], start=False, stop=False,
                                                          skip_group_check=True)
                                mm.then_inc(ghot_used, 1)
                    nc.tensor.matmul(acc[0:TP, NB - 1, 0:1], zeros[0:TP, :], iota_r[0:TP, 0:1], start=False, stop=True,
                                     skip_group_check=True).then_inc(bank_done, 1)

                for_tiles(pe, tile)
                for q in range(NR):
                    turn_round(NT - 1, (NT - 1) % 2, q)

            @block.scalar
            def _(act):
                act.sem_inc(bank_free, NB)
                act.wait_ge(norm_made, NT)
                nc.scalar.activation(norm[0:TP, 1, :, 0], norm[0:TP, 0, :, 1], ACT.Sqrt, bias=scales[0:TP, 3:4]).then_inc(rooted, 1)

                def put_product(t, j):
                    act.wait_ge(xw_done, t + 1)
                    nc.scalar.copy(xwT[:, bass.ds(t * TP, TP)], acc[0:HD, j, XWT:XWT + TP]).then_inc(xw_made, 1)
                    nc.scalar.copy(xw[:, bass.ds(t, 1), :].rearrange("p a k -> p (a k)"), acc[0:TP, j, XW:XW + HD]).then_inc(xw_made, 1)

                act.wait_ge(h_made, NT)

                def project(t, j, before):
                    act.wait_ge(h_turned, t + 1)
                    if not isinstance(before, int):
                        act.wait_ge(xw_done, t - SR + 1)
                    nc.scalar.copy(hT[:, j, :, 0:TP], acc[:, j, 0:256].rearrange("p (k n) -> p k n", k=2)[:, :, 0:TP]).then_inc(hT_made, 1)
                    if not isinstance(t, int) or t >= 1:
                        put_product(t - 1, (j - 1) % SR)

                for_ring(act, project)
                put_product(NT - 1, (NT - 1) % SR)
                act.wait_ge(lr_made, 1)
                for n, (kind, scale) in enumerate(((EL, 1.0), (EL, 0.2), (ER, 1.0), (ER, 0.2))):
                    nc.scalar.activation(pows[0:TP, n], lr[0:TP, :, kind:kind + HEADS], ACT.Exp, scale=scale).then_inc(pows_made, 1)
                for n in range(HEADS * NB):
                    h, b = n // NB, n % NB
                    lo, k = BANKS[b]
                    act.wait_ge(rows_done, n + 1)
                    nc.scalar.copy(rows[0:TP, h * N + lo:h * N + lo + k], acc[0:TP, n % SR, 0:k]).then_inc(rows_made, 1)

                act.wait_ge(cleared, 4)

                def tile(t, par, before):
                    act.wait_ge(bank_done, t + 1)
                    if not isinstance(before, int) or before:
                        act.wait_ge(strip_out[par], before * 16)
                        act.wait_ge(turn_done, (t - 1) * NR)
                    for b, (lo, n) in enumerate(BANKS):
                        col = col_part[0:TP, bass.ds(t, 1), b:b + 1].rearrange("p a k -> p (a k)")
                        nc.scalar.activation(strip[0:TP, par, lo:lo + n], acc[0:TP, b, 0:n], ACT.Copy,
                                             accum_out=col).then_inc(bank_free, 1)
                    if not isinstance(before, int) or before:
                        act.wait_ge(turned_out[par], before * 16)
                        act.wait_ge(summed_rows, (t - 1) * 2 - 1)
                    for q, (rt0, n) in enumerate(rounds):
                        act.wait_ge(turn_done, t * NR + q + 1)
                        nc.scalar.copy(turned[0:TP, par, rt0:rt0 + n, :], turn[0:TP, 0:n, 0:TP]).then_inc(turn_free, 1)

                for_tiles(act, tile)


def layer_norm_some(nc, dve, link, x, out, tiles, stats, norm, stats_made, before, norm_made, rooted, roots_before, made):
    count = (before + 1) * len(tiles)
    for t in tiles:
        nc.vector.bn_stats(stats[0:TP, t, :], x[0:TP, t, :]).then_inc(stats_made, 1)
    dve.wait_ge(stats_made, count + before)
    dve.sem_inc(stats_made, 1)
    for t in tiles:
        nc.vector.bn_aggr(norm[0:TP, 0, t, :], stats[0:TP, t, :]).then_inc(norm_made, 1)
    dve.wait_ge(rooted, roots_before + 1)
    T = slice(tiles[0], tiles[-1] + 1)
    link(nc.vector.reciprocal(norm[0:TP, 1, T, 1], norm[0:TP, 1, T, 0]))
    for t in tiles:
        nc.vector.tensor_scalar(out[0:TP, t, :], x[0:TP, t, :], norm[0:TP, 0, t, 0:1], norm[0:TP, 1, t, 1:2],
                                ALU.subtract, ALU.mult).then_inc(made, 1)


def layer_norm_all(nc, dve, link, x, out, stats, norm, stats_made, norm_made, rooted, made):
    layer_norm_some(nc, dve, link, x, out, range(NT), stats, norm, stats_made, 0, norm_made, rooted, 0, made)


class Chain:

    def __init__(self, eng, sem, passed=None):
        self.eng, self.sem, self.count, self.base = eng, sem, 0, 0
        self.passed = passed

    def __call__(self, ins):
        self.count += 1
        ins.then_inc(self.sem, 1)
        self.eng.wait_ge(self.sem, self.base + self.count)

    def at(self, base):
        self.base, self.count = base, 0


def graph_attention(nc, x, gat_b, dram, ones, att, deg, xs, scales):
    feats, rows, lr, ner, pows, vdeg = att.feats, att.rows, att.lr, att.ner, att.pows, att.vdeg
    MR = 20
    assert HEADS * NT % MR == 0
    with ExitStack() as ctx:
        def sb(name, shape, dt):
            return ctx.enter_context(nc.sbuf_tensor(name, shape, dt))

        def sem(name):
            return ctx.enter_context(nc.semaphore(name))

        strip = sb("g_strip", [128, NT, GT, TP], F16)
        mask = sb("mask", [128, MR, GW], F16)
        tot = sb("tot", [128, GT, 2 * HF + 4], F32)
        got = sb("got", [128, GT, 2 * HF], F32)
        tmp = sb("tmp", [128, 2, GT, HF], F32)
        num = sb("num", [128, GT, D], F32)
        den = sb("den", [128, GT, HEADS], F32)
        low = tot[:].rearrange("p t n -> p (t n)")[:, 0:GT * D].rearrange("p (t d) -> p t d", d=D)
        bias = sb("g_bias", [128, D], F32)
        acc = ctx.enter_context(nc.psum_tensor("g_acc", [128, GT, BANK], F32))
        strip_in = [sem(f"g_strip_in{j}") for j in range(GT)]
        mask_ready = sem("mask_ready")
        mask_used = sem("mask_used")
        phase_done = sem("phase_done")
        acc_free = sem("acc_free")
        tot_used = sem("tot_used")
        got_used = sem("got_used")
        pool_chain = sem("pool_chain")
        bias_in = sem("bias_in")
        x_in = sem("g_x_in")
        low_made = sem("low_made")
        exp_made = sem("exp_made")
        finished = sem("finished")
        passed = sem("g_passed")
        den_made = sem("den_made")
        den_turned = sem("den_turned")
        PD = GT + HEADS * (GT - 1)
        NP_ = HEADS + 1

        with nc.Block() as block:
            @block.sync
            def _(sp):
                def load(g):
                    for j in range(GT):
                        if not isinstance(g, int):
                            sp.wait_ge(mask_ready, g * (HEADS * NT) - NT + (j + 1) * GT)
                            sp.wait_ge(phase_done, g * PD - HEADS * (GT - 1))
                        for rt in range(GT):
                            sp.dma_start(strip[:, j * GT:(j + 1) * GT, rt, :],
                                         dram.adj_t[bass.ds(g * GT + rt, 1), :, j * GT:(j + 1) * GT, :].rearrange("g c a r -> c (g a) r")
                                         ).then_inc(strip_in[j], 16)

                def load_x(g):
                    if not isinstance(g, int):
                        sp.wait_ge(finished, g)
                    sp.dma_start(xs[0:TP, bass.ds(g * GT, GT), :], x[bass.ds(g * GW, GW), :].rearrange("(t p) d -> p t d", p=TP)
                                 ).then_inc(x_in, 16)

                load(0)
                sp.dma_start(bias[0:TP, :], gat_b).then_inc(bias_in, 16)
                load_x(0)
                with sp.Fori(1, NG) as g:
                    load(g)
                    load_x(g)

            @block.vector
            def _(dve):
                with dve.Fori(0, NG) as g:
                    for h in range(HEADS):
                        for ct in range(NT):
                            if h == 0 and ct % GT == 0:
                                dve.wait_ge(strip_in[ct // GT], g * (16 * GT) + 16 * GT)
                            dve.wait_ge(mask_used, g * (HEADS * NT) + (h * NT + ct + 1))
                            nc.vector.scalar_tensor_tensor(out=mask[0:TP, (h * NT + ct) % MR, :], in0=rows[0:TP, bass.ds(g * GW + h * N, GW)],
                                                           scalar=ner[0:TP, ct, h:h + 1], in1=strip[0:TP, ct].rearrange("c g r -> c (g r)"),
                                                           op0=ALU.is_ge, op1=ALU.mult).then_inc(mask_ready, 1)
                    dve.wait_ge(den_made, g + 1)
                    nc.vector.reciprocal(den[0:TP], den[0:TP]).then_inc(den_turned, 1)

            @block.tensor
            def _(pe):
                pe.sem_inc(mask_used, MR)
                with pe.Fori(0, NG) as g:
                    for ct in range(NT):
                        if ct % GT == 0:
                            pe.wait_ge(strip_in[ct // GT], g * (16 * GT) + 16 * GT)
                        for rt in range(GT):
                            if ct == 0:
                                pe.wait_ge(acc_free, g * (NP_ * GT) + rt + 1)
                            blk = strip[0:TP, ct, rt, :]
                            for part in range(2):
                                nc.tensor.matmul(acc[0:TP, rt, 0:HEADS * (HD + 1)], blk, feats[0:TP, ct, :, part, HD + 1:HF],
                                                 start=(ct == 0 and part == 0), stop=False, skip_group_check=True)
                            mm = nc.tensor.matmul(acc[0:TP, rt, 2 * HF:2 * HF + 4], blk, vdeg[0:TP, ct, :], start=False,
                                                  stop=(ct == NT - 1), skip_group_check=True)
                            if ct == NT - 1:
                                mm.then_inc(phase_done, 1)
                    for h in range(HEADS):
                        for ct in range(NT):
                            pe.wait_ge(mask_ready, g * (HEADS * NT) + (h * NT + ct + 1))
                            for rt in range(GT):
                                if ct == 0:
                                    pe.wait_ge(acc_free, g * (NP_ * GT) + ((h + 1) * GT + rt + 1))
                                mm = nc.tensor.matmul(acc[0:TP, rt, 0:2 * HF], mask[0:TP, (h * NT + ct) % MR, rt * TP:(rt + 1) * TP],
                                                      feats[0:TP, ct, h].rearrange("p a n -> p (a n)"), start=(ct == 0),
                                                      stop=(ct == NT - 1))
                                if ct == NT - 1 and rt < GT - 1:
                                    mm.then_inc(phase_done, 1)
                            mm.then_inc(mask_used, 1)

            @block.scalar
            def _(act):
                act.sem_inc(acc_free, GT)
                with act.Fori(0, NG) as g:
                    for ph in range(NP_):
                        for rt in range(GT):
                            if ph == 0 or rt < GT - 1:
                                act.wait_ge(phase_done, g * PD + (ph * (GT - 1) + (ph > 0) + rt + 1))
                            else:
                                act.wait_ge(mask_used, g * (HEADS * NT) + (ph * NT + MR))
                            if ph == 0:
                                if rt == 0:
                                    act.wait_ge(tot_used, g + 1)
                                nc.scalar.copy(tot[0:TP, rt, 0:2 * HF + 4], acc[0:TP, rt, 0:2 * HF + 4]).then_inc(acc_free, 1)
                            else:
                                if rt == 0:
                                    act.wait_ge(got_used, g * HEADS + ph)
                                nc.scalar.copy(got[0:TP, rt, :], acc[0:TP, rt, 0:2 * HF]).then_inc(acc_free, 1)
                    act.wait_ge(low_made, g + 1)
                    nc.scalar.activation(low[0:TP], low[0:TP], ACT.Exp).then_inc(exp_made, 1)

            @block.gpsimd
            def _(pool):
                pool.sem_inc(tot_used, 1)
                pool.sem_inc(got_used, 1)
                link = Chain(pool, pool_chain)
                pool.wait_ge(bias_in, 16)
                with pool.Fori(0, NG) as g:
                    link.at(g * (HEADS * 6 + 7))
                    pool.wait_ge(acc_free, g * (NP_ * GT) + 2 * GT)
                    link(nc.gpsimd.tensor_tensor(deg[0:TP, bass.ds(g * GT, GT), 2:4], tot[0:TP, :, 2 * HF:2 * HF + 2],
                                                 tot[0:TP, :, 2 * HF + 2:2 * HF + 4], ALU.add))
                    for h in range(HEADS):
                        s = got[0:TP]
                        a = pows[0:TP, 0, bass.ds(g * GT, GT), h:h + 1].to_broadcast([TP, GT, HD + 1])
                        a5 = pows[0:TP, 1, bass.ds(g * GT, GT), h:h + 1].to_broadcast([TP, GT, HD + 1])
                        b, b5 = tmp[0:TP, 0, :, 0:HD + 1], tmp[0:TP, 0, :, HD + 1:HF]
                        pool.wait_ge(acc_free, g * (NP_ * GT) + (h + 3) * GT)
                        link(nc.gpsimd.tensor_tensor(tmp[0:TP, 0], s[:, :, 0:HF], s[:, :, HF:2 * HF], ALU.add))
                        link(nc.gpsimd.tensor_tensor(tmp[0:TP, 1, :, 0:HD + 1], tot[0:TP, :, h * (HD + 1):(h + 1) * (HD + 1)], b5,
                                                     ALU.subtract))
                        link(nc.gpsimd.tensor_tensor(b, b, a, ALU.mult))
                        link(nc.gpsimd.tensor_tensor(b5, tmp[0:TP, 1, :, 0:HD + 1], a5, ALU.mult))
                        link(nc.gpsimd.tensor_tensor(num[0:TP, :, h * HD:(h + 1) * HD], tmp[0:TP, 0, :, 0:HD],
                                                     tmp[0:TP, 0, :, HD + 1:HD + 1 + HD], ALU.add))
                        link(nc.gpsimd.tensor_tensor(den[0:TP, :, h:h + 1], tmp[0:TP, 0, :, HD:HD + 1],
                                                     tmp[0:TP, 0, :, HF - 1:HF], ALU.add))
                        pool.sem_inc(got_used, 1)
                    heads = num[0:TP].rearrange("p t (h k) -> p (t h) k", h=HEADS)
                    den_f = den[0:TP].rearrange("p t h -> p (t h)")
                    pool.sem_inc(passed, 1)
                    nc.gpsimd.tensor_scalar(den[0:TP], den[0:TP], scales[0:TP, 1:2], 1e-12, ALU.mult, ALU.max).then_inc(den_made, 1)
                    pool.wait_ge(den_turned, g + 1)
                    pool.sem_inc(passed, 1)
                    link(nc.gpsimd.tensor_scalar(den[0:TP], den[0:TP], scales[0:TP, 1:2], None, ALU.mult))
                    link(nc.gpsimd.tensor_tensor(heads, heads, den_f.to_broadcast([TP, GT * HEADS, HD]), ALU.mult))
                    link(nc.gpsimd.tensor_tensor(num[0:TP], num[0:TP], bias[0:TP].rearrange("p (a d) -> p a d", a=1).to_broadcast([TP, GT, D]), ALU.add))
                    pool.sem_inc(passed, 1)
                    nc.gpsimd.tensor_scalar(low[0:TP], num[0:TP], 0.0, None, ALU.min).then_inc(low_made, 1)
                    link(nc.gpsimd.tensor_scalar(num[0:TP], num[0:TP], 0.0, -1.0, ALU.max, ALU.add))
                    pool.wait_ge(x_in, g * 16 + 16)
                    mine = xs[0:TP, bass.ds(g * GT, GT), :]
                    pool.sem_inc(passed, 1)
                    link(nc.gpsimd.tensor_tensor(mine, mine, num[0:TP], ALU.add))
                    pool.wait_ge(exp_made, g + 1)
                    pool.sem_inc(passed, 1)
                    link(nc.gpsimd.tensor_tensor(mine, mine, low[0:TP], ALU.add))
                    pool.sem_inc(finished, 1)
                    pool.sem_inc(tot_used, 1)


NE = 8
SLOT = 128
NBLK = (2 * N + NE * (SLOT - 1)) // SLOT
ROOM = -(-N // SLOT) * SLOT + SLOT


ROWS, COLS, A_ROWS, A_COLS, T_ROWS, T_COLS = range(6)


def mixture(nc, layer, xs, par, ident, ones, scales, deg, adj, dram_x, dram_y, hidden, pool_sem, out=None):
    norms = 2 if layer == 0 else 1
    assert NBLK % 4 == 0
    KD = D // 128
    KH = hidden // 128
    with ExitStack() as ctx:
        def sb(name, shape, dt):
            return ctx.enter_context(nc.sbuf_tensor(f"m{layer}_{name}", shape, dt))

        def sem(name):
            return ctx.enter_context(nc.semaphore(f"m{layer}_{name}"))

        tok = sb("tok", [128, NT, D], F32)
        w1 = sb("w1", [128, NE, KD, hidden], F32)
        w2 = sb("w2", [128, NE, KH, D], F32)
        b1 = sb("b1", [128, NE, hidden], F32)
        b2 = sb("b2", [128, NE, D], F32)
        weight = sb("weight", [128, 2, NT], F32)
        pos = sb("pos", [128, 2, NT], U32)
        expert = sb("expert", [1, NBLK], I32)
        first_row = sb("first_row", [1, NBLK], I32)
        w_in = sem("w_in")
        zero_out = sem("zero_out")
        placed = pool_sem(f"m{layer}_placed")

        with ExitStack() as ctx2:
            def sb2(name, shape, dt):
                return ctx2.enter_context(nc.sbuf_tensor(f"r{layer}_{name}", shape, dt))

            def ps(name, shape):
                return ctx2.enter_context(nc.psum_tensor(f"r{layer}_{name}", shape, F32))

            def sem2(name):
                return ctx2.enter_context(nc.semaphore(f"r{layer}_{name}"))

            TR = 4
            wr = sb2("wr", [128, KD, NE], F32)
            br = sb2("br", [1, NE], F32)
            gb = sb2("gb", [128, 2, D], F32)
            stats = sb2("stats", [128, NT, 6], F32)
            norm = sb2("norm", [128, 2, NT, 2], F32)
            tT = sb2("tT", [128, TR, KD, 128], F32)
            logit = sb2("logit", [128, NT, NE], F32)
            best = sb2("best", [128, NT, 8], F32)
            besti = sb2("besti", [128, NT, 8], U32)
            bestf = sb2("bestf", [128, NT, 2], F32)
            one = sb2("one", [128, 3, NT, NE], F32)
            below = sb2("below", [128, NT + 1, NE], F32)
            iota8 = sb2("iota8", [128, GT, NE], F32)
            room = sb2("room", [128, GT, NE], F32)
            iota128 = sb2("iota128", [128, NE, NT], F32)
            iotab = sb2("iotab", [1, NBLK, NE], F32)
            before = sb2("before", [128, 128], F32)
            place = sb2("place", [128, NT, NE], F32)
            chosen = sb2("chosen", [128, NT, NE], F32)
            xpos = sb2("xpos", [128, 2, NT], U32)
            total = sb2("total", [128, NE], F32)
            blocks = sb2("blocks", [128, NE, NT], F32)
            nblk = sb2("nblk", [128, NE], F32)
            start = sb2("start", [128, NE + 1], F32)
            shift = sb2("shift", [128, NE], F32)
            skip = sb2("skip", [128, NE], F32)
            tail = sb2("tail", [128, NE], F32)
            tail_row = sb2("tail_row", [1, NE], I32)
            past = sb2("past", [1, 2, NBLK, NE], F32)
            table = sb2("table", [1, 4, NBLK], F32)
            s25 = sb2("s25", [128, 4, NT], F32)
            zero = sb2("zero", [128, D], F32)
            p_turn = ps("p_turn", [128, TR, BANK])
            p_log = ps("p_log", [128, 2, BANK])
            p_cnt = ps("p_cnt", [128, BANK])
            if layer == 0:
                d_strip = sb2("d_strip", [128, SR, NT, TP], F16)
                vdeg = sb2("vdeg", [128, NT, 4], F16)
                part_deg = sb2("part_deg", [128, NT, 4], F32)
                p_deg = ps("p_deg", [128, BANK])
                d_strip_in = [sem2(f"d_strip_in{j}") for j in range(SR)]
                vdeg_made = sem2("vdeg_made")
                deg_done = sem2("deg_done")

            r_in = sem2("r_in")
            chain = sem2("chain")
            stats_made = sem2("stats_made")
            norm_made = sem2("norm_made")
            rooted = sem2("rooted")
            normed = sem2("normed")
            scaled = sem2("scaled")
            tok_made = sem2("tok_made")
            turned = sem2("turned")
            tT_made = sem2("tT_made")
            log_done = sem2("log_done")
            log_free = sem2("log_free")
            made = sem2("made")
            shifted = sem2("shifted")
            expd = sem2("expd")
            ones_made = sem2("ones_made")
            counted = sem2("counted")
            placed_at = sem2("placed_at")
            tails_at = sem2("tails_at")

            def tiles_of(g):
                return range(g * GT, (g + 1) * GT)

            with nc.Block() as block:
                @block.sync
                def _(sp):
                    sp.dma_start(wr[:], par["wr"].rearrange("(k p) e -> p k e", p=128)).then_inc(r_in, 16)
                    sp.dma_start(br[:], par["br"]).then_inc(r_in, 16)
                    if layer == 0:
                        sp.dma_start(gb[0:TP], par["gb"]).then_inc(r_in, 16)

                        def load_strip(t, j, before):
                            if not isinstance(before, int):
                                sp.wait_ge(deg_done, t + (1 - SR))
                            sp.dma_start(d_strip[:, j], adj[bass.ds(t, 1)].rearrange("a r k c -> r (a k) c")).then_inc(d_strip_in[j], 16)

                        for_ring(sp, load_strip)
                    sp.dma_start(w1[:], par["w1"].rearrange("e (k p) h -> p e k h", p=128)).then_inc(w_in, 16)
                    sp.dma_start(w2[:], par["w2"].rearrange("e (k p) h -> p e k h", p=128)).then_inc(w_in, 16)
                    sp.dma_start(b1[:], par["b1"]).then_inc(w_in, 16)
                    sp.dma_start(b2[:], par["b2"]).then_inc(w_in, 16)
                    sp.wait_ge(made, 1)
                    sp.dma_start(dram_x[NE * ROOM:NE * ROOM + SLOT, :], zero[:]).then_inc(zero_out, 16)
                    sp.wait_ge(tails_at, 1)
                    for e in range(NE):
                        row = sp.value_load(tail_row[0:1, e:e + 1], min_val=0, max_val=NE * ROOM - SLOT)
                        sp.dma_start(dram_x[bass.ds(row, SLOT), :], zero[:]).then_inc(zero_out, 16)
                    sp.wait_ge(zero_out, 16 * (NE + 1))

                @block.gpsimd
                def _(pool):
                    nc.gpsimd.memset(zero[:], 0.0).then_inc(made, 1)
                    for out, pattern in ((iota8, [[0, GT], [1, NE]]), (room, [[0, GT], [ROOM, NE]]), (iota128, [[0, NE], [SLOT, NT]]),
                                         (iotab, [[1, NBLK], [0, NE]])):
                        nc.gpsimd.iota(out[:], pattern, base=0, channel_multiplier=0,
                                       allow_small_or_imprecise_dtypes=True).then_inc(made, 1)
                    nc.gpsimd.memset(below[:, 0], 0.0).then_inc(made, 1)
                    nc.gpsimd.memset(start[:], 0.0).then_inc(made, 1)
                    nc.gpsimd.affine_select(out=before[:], in_=ones[:], compare_op=ALU.is_gt, fill=0.0, base=0,
                                            pattern=[[1, 128]], channel_multiplier=-1).then_inc(made, 1)
                    for g in range(NG):
                        pool.wait_ge(placed_at, g + 1)
                        for t in tiles_of(g):
                            for c in range(2):
                                pool.indirect_dma_start(dram_x[:, :], bass.IndirectOffsetOnAxis(ap=xpos[0:TP, c, t:t + 1], axis=0),
                                                        tok[0:TP, t, :], None).then_inc(placed, 16)
                    pool.wait_ge(placed, 16 * 2 * NT)

                @block.vector
                def _(dve):
                    link = Chain(dve, chain)
                    dve.wait_ge(r_in, 32 + 16 * (layer == 0))
                    if layer == 0:
                        nc.vector.tensor_copy(vdeg[0:TP, :, 0:2], deg[0:TP, :, 0:2]).then_inc(vdeg_made, 1)
                        dve.wait_ge(vdeg_made, 1)
                        nc.vector.tensor_tensor(vdeg[0:TP, :, 2:4], deg[0:TP, :, 0:2], vdeg[0:TP, :, 0:2], ALU.subtract).then_inc(vdeg_made, 1)

                    def normalise(g):
                        ts = tiles_of(g)
                        if layer == 1:
                            layer_norm_some(nc, dve, link, xs, tok, ts, stats, norm, stats_made, g, norm_made, rooted, g, tok_made)
                            return
                        layer_norm_some(nc, dve, link, xs, tok, ts, stats, norm, stats_made, 2 * g, norm_made, rooted, 2 * g, normed)
                        dve.wait_ge(normed, (2 * g + 1) * GT)
                        layer_norm_some(nc, dve, link, tok, tok, ts, stats, norm, stats_made, 2 * g + 1, norm_made, rooted, 2 * g + 1, normed)
                        for n, t in enumerate(list(ts) + [ts[-1] + 1]):
                            if n < GT:
                                dve.wait_ge(normed, (2 * g + 1) * GT + n + 1)
                                nc.vector.tensor_tensor(tok[0:TP, t], tok[0:TP, t], gb[0:TP, 0], ALU.mult).then_inc(scaled, 1)
                            if n >= 1:
                                dve.wait_ge(scaled, t)
                                nc.vector.tensor_tensor(tok[0:TP, t - 1], tok[0:TP, t - 1], gb[0:TP, 1], ALU.add).then_inc(tok_made, 1)

                    def pick(c, T, out):
                        n = T.stop - T.start
                        link(nc.vector.tensor_tensor(chosen[0:TP, T], place[0:TP, T], one[0:TP, c, T], ALU.mult))
                        link(nc.vector.tensor_reduce(s25[0:TP, 3, T], chosen[0:TP, T], AX.X, ALU.add))
                        return nc.vector.tensor_copy(out[0:TP, c, T], s25[0:TP, 3, T])

                    def route(g):
                        T = slice(g * GT, (g + 1) * GT)
                        lg = logit[0:TP, T]
                        dve.wait_ge(log_done, (g + 1) * GT)
                        nc.vector.tensor_copy(lg.rearrange("p t e -> p (t e)"), p_log[0:TP, g % 2, 0:GT * NE]).then_inc(log_free, 1)
                        dve.wait_ge(log_free, g + 1)
                        if layer == 1:
                            link(nc.vector.tensor_reduce(s25[0:TP, 0, T], lg, AX.X, ALU.max))
                            nc.vector.tensor_tensor(lg, lg, s25[0:TP, 0, T].to_broadcast([TP, GT, NE]), ALU.subtract).then_inc(shifted, 1)
                            dve.wait_ge(expd, g + 1)
                            link(nc.vector.tensor_reduce(s25[0:TP, 1, T], lg, AX.X, ALU.add))
                            link(nc.vector.reciprocal(s25[0:TP, 2, T], s25[0:TP, 1, T]))
                            link(nc.vector.tensor_tensor(lg, lg, s25[0:TP, 2, T].to_broadcast([TP, GT, NE]), ALU.mult))
                        for t in tiles_of(g):
                            m = nc.vector.max(best[0:TP, t, :], logit[0:TP, t, :])
                        link(m)
                        for t in tiles_of(g):
                            m = nc.vector.max_index(besti[0:TP, t, :], best[0:TP, t, :], logit[0:TP, t, :])
                        link(m)
                        first, second = best[0:TP, T, 0], best[0:TP, T, 1]
                        if layer == 0:
                            nc.vector.tensor_tensor(s25[0:TP, 0, T], second, first, ALU.subtract).then_inc(shifted, 1)
                        link(nc.vector.tensor_copy(bestf[0:TP, T], besti[0:TP, T, 0:2]))
                        if g == 0:
                            dve.wait_ge(made, 8)
                        for c in range(2):
                            link(nc.vector.tensor_tensor(one[0:TP, c, T], iota8[0:TP], bestf[0:TP, T, c].to_broadcast([TP, GT, NE]),
                                                         ALU.is_equal))
                        link(nc.vector.tensor_tensor(one[0:TP, 2, T], one[0:TP, 0, T], one[0:TP, 1, T], ALU.add))
                        for t in tiles_of(g):
                            link(nc.vector.tensor_tensor(below[0:TP, t + 1], below[0:TP, t], one[0:TP, 2, t], ALU.add))
                        dve.sem_inc(ones_made, 1)
                        if layer == 0:
                            dve.wait_ge(expd, g + 1)
                            link(nc.vector.tensor_scalar(s25[0:TP, 2, T], s25[0:TP, 1, T], 1.0, None, ALU.add))
                            link(nc.vector.reciprocal(weight[0:TP, 0, T], s25[0:TP, 2, T]))
                            link(nc.vector.tensor_tensor(weight[0:TP, 1, T], weight[0:TP, 0, T], s25[0:TP, 1, T], ALU.mult))
                        else:
                            link(nc.vector.tensor_tensor(s25[0:TP, 1, T], second, first, ALU.add))
                            link(nc.vector.tensor_scalar(s25[0:TP, 1, T], s25[0:TP, 1, T], 1e-12, None, ALU.max))
                            link(nc.vector.reciprocal(s25[0:TP, 2, T], s25[0:TP, 1, T]))
                            link(nc.vector.tensor_tensor(weight[0:TP, 0, T], first, s25[0:TP, 2, T], ALU.mult))
                            link(nc.vector.tensor_tensor(weight[0:TP, 1, T], second, s25[0:TP, 2, T], ALU.mult))
                        dve.wait_ge(counted, g + 1)
                        link(nc.vector.tensor_tensor(place[0:TP, T], p_cnt[0:TP, 0:GT * NE].rearrange("p (t e) -> p t e", e=NE), room[0:TP], ALU.add))
                        link(pick(0, T, xpos))
                        pick(1, T, xpos).then_inc(placed_at, 1)
                        dve.wait_ge(placed_at, g + 1)

                    normalise(0)
                    for g in range(NG):
                        if g + 1 < NG:
                            normalise(g + 1)
                        route(g)
                    dve.wait_ge(counted, NG + 1)
                    link(nc.vector.tensor_copy(total[0:TP], p_cnt[0:TP, 0:NE]))
                    link(nc.vector.tensor_tensor(tail[0:1], total[0:1], room[0:1, 0], ALU.add))
                    nc.vector.tensor_copy(tail_row[:], tail[0:1]).then_inc(tails_at, 1)
                    link(nc.vector.tensor_tensor(blocks[0:TP], total[0:TP].to_broadcast([TP, NE, NT]), iota128[0:TP], ALU.is_gt))
                    link(nc.vector.tensor_reduce(nblk[0:TP], blocks[0:TP], AX.X, ALU.add))
                    for e in range(NE):
                        link(nc.vector.tensor_tensor(start[0:TP, e + 1:e + 2], start[0:TP, e:e + 1], nblk[0:TP, e:e + 1], ALU.add))
                    link(nc.vector.scalar_tensor_tensor(out=shift[0:TP], in0=start[0:TP, 0:NE], scalar=float(SLOT), in1=room[0:TP, 0],
                                                        op0=ALU.mult, op1=ALU.subtract))
                    link(nc.vector.tensor_tensor(place[0:TP], place[0:TP], shift[0:TP].rearrange("p (a e) -> p a e", a=1).to_broadcast([TP, NT, NE]), ALU.add))
                    for c in range(2):
                        link(pick(c, slice(0, NT), pos))
                    link(nc.vector.tensor_tensor(past[:, 0], start[0:1, 1:NE + 1].rearrange("p (a e) -> p a e", a=1).to_broadcast([1, NBLK, NE]), iotab[:], ALU.is_le))
                    link(nc.vector.tensor_scalar(skip[0:1], nblk[0:1], -float(SLOT), float(ROOM), ALU.mult, ALU.add))
                    link(nc.vector.tensor_tensor(past[:, 1], past[:, 0], skip[0:1].rearrange("p (a e) -> p a e", a=1).to_broadcast([1, NBLK, NE]), ALU.mult))
                    link(nc.vector.tensor_reduce(table[:, 0:2], past[:], AX.X, ALU.add))
                    link(nc.vector.tensor_scalar(expert[:], table[:, 0], float(NE - 1), None, ALU.min))
                    link(nc.vector.scalar_tensor_tensor(out=table[:, 2], in0=iotab[:, :, 0], scalar=float(SLOT), in1=table[:, 1],
                                                        op0=ALU.mult, op1=ALU.add))
                    link(nc.vector.tensor_scalar(first_row[:], table[:, 2], float(NE * ROOM), None, ALU.min))
                    if layer == 0:
                        dve.wait_ge(deg_done, NT)
                        link(nc.vector.tensor_copy(part_deg[0:TP].rearrange("p t k -> p (t k)"), p_deg[0:TP, 0:NT * 4]))
                        link(nc.vector.tensor_tensor(deg[0:TP, :, T_ROWS:T_COLS + 1], part_deg[0:TP, :, 0:2], part_deg[0:TP, :, 2:4], ALU.add))

                @block.scalar
                def _(act):
                    def roots(g):
                        for n in range(norms):
                            act.wait_ge(norm_made, (norms * g + n + 1) * GT)
                            T = slice(g * GT, (g + 1) * GT)
                            nc.scalar.activation(norm[0:TP, 1, T, 0], norm[0:TP, 0, T, 1], ACT.Sqrt, bias=scales[0:TP, 3:4]).then_inc(rooted, 1)

                    roots(0)
                    for g in range(NG):
                        for t in tiles_of(g):
                            act.wait_ge(turned, t + 1)
                            if t >= TR:
                                act.wait_ge(log_done, t - TR + 1)
                            nc.scalar.copy(tT[:, t % TR, :, 0:TP], p_turn[:, t % TR, 0:KD * 128].rearrange("p (k n) -> p k n", k=KD)[:, :, 0:TP]).then_inc(tT_made, 1)
                        if g + 1 < NG:
                            roots(g + 1)
                        act.wait_ge(shifted, g + 1)
                        T = slice(g * GT, (g + 1) * GT)
                        if layer == 0:
                            nc.scalar.activation(s25[0:TP, 1, T], s25[0:TP, 0, T], ACT.Exp).then_inc(expd, 1)
                        else:
                            nc.scalar.activation(logit[0:TP, T], logit[0:TP, T], ACT.Exp).then_inc(expd, 1)

                @block.tensor
                def _(pe):
                    pe.wait_ge(r_in, 32 + 16 * (layer == 0))
                    if layer == 0:
                        pe.wait_ge(vdeg_made, 2)

                    def degrees(t):
                        pe.wait_ge(d_strip_in[t % SR], t // SR * 16 + 16)
                        for kt in range(NT):
                            mm = nc.tensor.matmul(p_deg[0:TP, t * 4:t * 4 + 4], d_strip[0:TP, t % SR, kt, :], vdeg[0:TP, kt, :],
                                                  start=(kt == 0), stop=(kt == NT - 1))
                        mm.then_inc(deg_done, 1)

                    def score(t):
                        pe.wait_ge(tT_made, t + 1)
                        g = t // GT
                        if t % GT == 0 and g >= 2:
                            pe.wait_ge(log_free, g - 1)
                        out = p_log[0:TP, g % 2, t % GT * NE:(t % GT + 1) * NE]
                        for k in range(KD):
                            nc.tensor.matmul(out, tT[:, t % TR, k, 0:TP], wr[:, k, :], start=(k == 0), stop=False)
                        nc.tensor.matmul(out, ones[0:1, 0:TP], br[:], start=False, stop=True).then_inc(log_done, 1)

                    def scores(g):
                        for t in tiles_of(g):
                            pe.wait_ge(tok_made, t + 1)
                            if t >= TR:
                                pe.wait_ge(tT_made, t - TR + 1)
                            for k in range(KD):
                                mm = nc.tensor.transpose(p_turn[:, t % TR, k * 128:k * 128 + TP], tok[0:TP, t, k * 128:(k + 1) * 128], ident[0:TP, 0:TP])
                            mm.then_inc(turned, 1)
                            if t % GT:
                                score(t - 1)
                        score(g * GT + GT - 1)

                    for g in range(NG):
                        scores(g)
                        if layer == 0:
                            for t in tiles_of(g):
                                degrees(t)
                        T = slice(g * GT, (g + 1) * GT)
                        pe.wait_ge(ones_made, g + 1)
                        if g >= 1:
                            pe.wait_ge(placed_at, g)
                        nc.tensor.matmul(p_cnt[0:TP, 0:GT * NE], before[0:TP, 0:TP], one[0:TP, 2, T].rearrange("p t e -> p (t e)"), start=True, stop=False)
                        nc.tensor.matmul(p_cnt[0:TP, 0:GT * NE], ones[0:TP, 0:TP], below[0:TP, T].rearrange("p t e -> p (t e)"), start=False,
                                         stop=True).then_inc(counted, 1)
                    pe.wait_ge(placed_at, NG)
                    nc.tensor.matmul(p_cnt[0:TP, 0:NE], ones[0:TP, 0:TP], below[0:TP, NT], start=True, stop=True).then_inc(counted, 1)

        with ExitStack() as ctx2:
            def sb2(name, shape, dt):
                return ctx2.enter_context(nc.sbuf_tensor(f"f{layer}_{name}", shape, dt))

            def ps(name, shape):
                return ctx2.enter_context(nc.psum_tensor(f"f{layer}_{name}", shape, F32))

            def sem2(name):
                return ctx2.enter_context(nc.semaphore(f"f{layer}_{name}"))

            XR = 4
            xt = sb2("xt", [128, XR, D], F32)
            xT = sb2("xT", [128, 2, KD, 128], F32)
            hb = sb2("hb", [128, 2, hidden], F32)
            hT = sb2("hT", [128, 2, KH, 128], F32)
            yt = sb2("yt", [128, XR, D], F32)
            p_x = ps("p_x", [128, BANK])
            p_h = ps("p_h", [128, 2, BANK])
            p_t = ps("p_t", [128, 2, BANK])
            p_y = ps("p_y", [128, 2, BANK])
            x_in = [sem2(f"x_in{n}") for n in range(XR)]
            x_turned = sem2("x_turned")
            xT_made = sem2("xT_made")
            h_done = sem2("h_done")
            h_biased = sem2("h_biased")
            h_made = sem2("h_made")
            h_turned = sem2("h_turned")
            hT_made = sem2("hT_made")
            y_done = sem2("y_done")
            y_made = sem2("y_made")
            y_out = [sem2(f"y_out{n}") for n in range(XR)]

            with nc.Block() as block:
                @block.sync
                def _(sp):
                    def blk(b, j, earlier):
                        row = sp.value_load(first_row[0:1, bass.ds(b, 1)], min_val=0, max_val=NE * ROOM)
                        if not isinstance(b, int) or b >= XR:
                            sp.wait_ge(x_turned, b - XR + 1)
                        sp.dma_start(xt[:, j], dram_x[bass.ds(row, SLOT), :]).then_inc(x_in[j], 16)

                    for_cycle(sp, blk, NBLK, XR)

                @block.tensor
                def _(pe):
                    pe.wait_ge(w_in, 64)

                    def turn_x(b, j, earlier):
                        pe.wait_ge(x_in[j], earlier * 16 + 16)
                        if not isinstance(b, int) or b >= 1:
                            pe.wait_ge(xT_made, b)
                        for k in range(KD):
                            mm = nc.tensor.transpose(p_x[:, k * 128:(k + 1) * 128], xt[:, j, k * 128:(k + 1) * 128], ident[:])
                        mm.then_inc(x_turned, 1)

                    def up(b, p):
                        e = pe.value_load(expert[0:1, bass.ds(b, 1)], min_val=0, max_val=NE - 1)
                        pe.wait_ge(xT_made, b + 1)
                        if not isinstance(b, int) or b >= 2:
                            pe.wait_ge(h_biased, b - 1)
                        for k in range(KD):
                            mm = nc.tensor.matmul(p_h[:, p, 0:hidden], xT[:, p, k, :],
                                                  w1[:, bass.ds(e, 1), k, :].rearrange("p a h -> p (a h)"), start=(k == 0), stop=(k == KD - 1))
                        mm.then_inc(h_done, 1)

                    def turn_h(b, p):
                        pe.wait_ge(h_made, b + 1)
                        if not isinstance(b, int) or b >= 2:
                            pe.wait_ge(hT_made, b - 1)
                        for k in range(KH):
                            mm = nc.tensor.transpose(p_t[:, p, k * 128:(k + 1) * 128], hb[:, p, k * 128:(k + 1) * 128], ident[:])
                        mm.then_inc(h_turned, 1)

                    def down(b, p):
                        e = pe.value_load(expert[0:1, bass.ds(b, 1)], min_val=0, max_val=NE - 1)
                        pe.wait_ge(hT_made, b + 1)
                        if not isinstance(b, int) or b >= 2:
                            pe.wait_ge(y_made, b - 1)
                        for k in range(KH):
                            mm = nc.tensor.matmul(p_y[:, p, 0:D], hT[:, p, k, :],
                                                  w2[:, bass.ds(e, 1), k, :].rearrange("p a h -> p (a h)"), start=(k == 0), stop=(k == KH - 1))
                        mm.then_inc(y_done, 1)

                    def blk(b, j, earlier):
                        p = j % 2
                        if isinstance(b, int) and b == 0:
                            turn_x(0, 0, 0)
                        turn_x(b + 1, (j + 1) % XR, earlier + (j + 1) // XR)
                        up(b, p)
                        if not isinstance(b, int) or b >= 1:
                            turn_h(b - 1, 1 - p)
                        if not isinstance(b, int) or b >= 2:
                            down(b - 2, p)

                    for_cycle(pe, blk, NBLK - 1, XR)
                    last = NBLK - 1
                    up(last, last % 2)
                    turn_h(last - 1, (last - 1) % 2)
                    down(last - 2, last % 2)
                    turn_h(last, last % 2)
                    down(last - 1, (last - 1) % 2)
                    down(last, last % 2)

                @block.scalar
                def _(act):
                    def gelu(b, p):
                        act.wait_ge(h_biased, b + 1)
                        nc.scalar.activation(hb[:, p], hb[:, p], ACT.Gelu).then_inc(h_made, 1)

                    def copy_x(b, p):
                        act.wait_ge(x_turned, b + 1)
                        if not isinstance(b, int) or b >= 2:
                            act.wait_ge(h_done, b - 1)
                        nc.scalar.copy(xT[:, p].rearrange("p k n -> p (k n)"), p_x[:, 0:D]).then_inc(xT_made, 1)

                    def store(b, j):
                        act.wait_ge(y_made, b + 1)
                        act.dma_start(dram_y[bass.ds(b * SLOT, SLOT), :], yt[:, j]).then_inc(y_out[j], 16)

                    def blk(b, j, earlier):
                        if isinstance(b, int) and b == 0:
                            copy_x(0, 0)
                        copy_x(b + 1, (j + 1) % 2)
                        gelu(b, j % 2)
                        if not isinstance(b, int) or b >= 3:
                            store(b - 3, (j - 3) % XR)

                    for_cycle(act, blk, NBLK - 1, XR)
                    gelu(NBLK - 1, (NBLK - 1) % 2)
                    for b in range(NBLK - 4, NBLK):
                        store(b, b % XR)
                    for j in range(XR):
                        act.wait_ge(y_out[j], 16 * (NBLK // XR))

                @block.vector
                def _(dve):
                    def bias_h(b, p):
                        e = dve.value_load(expert[0:1, bass.ds(b, 1)], min_val=0, max_val=NE - 1)
                        dve.wait_ge(h_done, b + 1)
                        if not isinstance(b, int) or b >= 2:
                            dve.wait_ge(h_turned, b - 1)
                        nc.vector.tensor_tensor(hb[:, p], p_h[:, p, 0:hidden], b1[:, bass.ds(e, 1), :].rearrange("p a h -> p (a h)"),
                                                ALU.add).then_inc(h_biased, 1)

                    def copy_h(b, p):
                        dve.wait_ge(h_turned, b + 1)
                        if not isinstance(b, int) or b >= 2:
                            dve.wait_ge(y_done, b - 1)
                        nc.vector.tensor_copy(hT[:, p].rearrange("p k n -> p (k n)"), p_t[:, p, 0:hidden]).then_inc(hT_made, 1)

                    def bias_y(b, j, earlier):
                        p = j % 2
                        e = dve.value_load(expert[0:1, bass.ds(b, 1)], min_val=0, max_val=NE - 1)
                        dve.wait_ge(y_done, b + 1)
                        if not isinstance(earlier, int) or earlier:
                            dve.wait_ge(y_out[j], earlier * 16)
                        nc.vector.tensor_tensor(yt[:, j], p_y[:, p, 0:D], b2[:, bass.ds(e, 1), :].rearrange("p a h -> p (a h)"),
                                                ALU.add).then_inc(y_made, 1)

                    def blk(b, j, earlier):
                        bias_h(b, j % 2)
                        if not isinstance(b, int) or b >= 1:
                            copy_h(b - 1, (j - 1) % 2)
                        if not isinstance(b, int) or b >= 2:
                            bias_y(b - 2, (j - 2) % XR, earlier - (j < 2))

                    dve.wait_ge(w_in, 64)
                    for_cycle(dve, blk, NBLK, XR)
                    last = NBLK - 1
                    copy_h(last, last % 2)
                    bias_y(last - 1, (last - 1) % XR, (last - 1) // XR)
                    bias_y(last, last % XR, last // XR)

        with ExitStack() as ctx2:
            GB = 4
            stored = ctx2.enter_context(nc.semaphore(f"c{layer}_stored"))
            got = ctx2.enter_context(nc.sbuf_tensor(f"c{layer}_got", [128, GB, 2, D], F32))
            got_in = [pool_sem(f"c{layer}_got_in{i}") for i in range(GB)]
            added = ctx2.enter_context(nc.semaphore(f"c{layer}_added"))
            with nc.Block() as block:
                if out is not None:
                    @block.sync
                    def _(sp):
                        for g in range(NG):
                            sp.wait_ge(added, (g + 1) * GT * 3)
                            sp.dma_start(out[g * GW:(g + 1) * GW, :].rearrange("(t p) d -> p t d", p=TP), xs[0:TP, g * GT:(g + 1) * GT]).then_inc(stored, 16)
                        sp.wait_ge(stored, 16 * NG)

                @block.gpsimd
                def _(pool):
                    for t in range(NT):
                        if t >= GB:
                            pool.wait_ge(added, (t - GB) * 3 + 3)
                        for c in range(2):
                            pool.indirect_dma_start(got[0:TP, t % GB, c, :], None, dram_y[:, :],
                                                    bass.IndirectOffsetOnAxis(ap=pos[0:TP, c, t:t + 1], axis=0)).then_inc(got_in[t % GB], 16)

                @block.vector
                def _(dve):
                    for t in range(NT):
                        if layer == 1:
                            nc.vector.tensor_tensor(xs[0:TP, t], xs[0:TP, t], tok[0:TP, t], ALU.add).then_inc(added, 1)
                        else:
                            dve.sem_inc(added, 1)
                        dve.wait_ge(added, t * 3 + 1)
                        dve.wait_ge(got_in[t % GB], (t // GB) * 32 + 32)
                        for c in range(2):
                            nc.vector.scalar_tensor_tensor(out=xs[0:TP, t], in0=got[0:TP, t % GB, c], scalar=weight[0:TP, c, t:t + 1],
                                                           in1=xs[0:TP, t], op0=ALU.mult, op1=ALU.add).then_inc(added, 1)
                            dve.wait_ge(added, t * 3 + c + 2)


ZS = 1024.0
YROOM = 2048.0
IN_DEG = (COLS, ROWS, T_COLS, A_COLS, T_ROWS, A_ROWS)
OUT_DEG = (ROWS, COLS, A_ROWS, A_COLS, T_ROWS, T_COLS)


def graph_convolution(nc, xs, gw, gbias, dram, ident, ones, deg, scales):
    with ExitStack() as ctx:
        def sb(name, shape, dt):
            return ctx.enter_context(nc.sbuf_tensor(name, shape, dt))

        xl = sb("xl", [128, NT, D], F32)
        roots = sb("roots", [128, 2, 6, NT], F32)
        both = sb("both", [128, 2, NT], F32)

        with ExitStack() as ctx2:
            def sb2(name, shape, dt):
                return ctx2.enter_context(nc.sbuf_tensor(name, shape, dt))

            def sem(name):
                return ctx2.enter_context(nc.semaphore(name))

            stats = sb2("d_stats", [128, NT, 6], F32)
            norm = sb2("d_norm", [128, 2, NT, 2], F32)
            big = sb2("d_big", [128, 6, NT], F32)
            pos = sb2("d_pos", [128, 6, NT], F32)
            inv = sb2("d_inv", [128, 6, NT], F32)
            mx = sb2("d_mx", [128, 1], F32)
            mrow = sb2("d_mrow", [1, 4], F32)
            p_mx = ctx2.enter_context(nc.psum_tensor("p_mx", [128, BANK], F32))
            chain = sem("d_chain")
            stats_made = sem("d_stats_made")
            norm_made = sem("d_norm_made")
            rooted = sem("d_rooted")
            xl_made = sem("xl_made")
            max_made = sem("max_made")
            max_turned = sem("max_turned")
            max_row = sem("max_row")
            max_all = sem("max_all")
            big_made = sem("big_made")
            big_rooted = sem("big_rooted")
            with nc.Block() as block:
                @block.tensor
                def _(pe):
                    pe.wait_ge(max_made, 1)
                    nc.tensor.transpose(p_mx[0:1, 0:TP], mx[0:TP, 0:1], ident[0:TP, 0:TP]).then_inc(max_turned, 1)
                    pe.wait_ge(max_row, 1)
                    nc.tensor.matmul(p_mx[0:TP, 128:130], ones[0:1, 0:TP], mrow[:, 1:3], start=True, stop=True).then_inc(max_all, 1)

                @block.scalar
                def _(act):
                    act.wait_ge(big_made, 1)
                    nc.scalar.activation(big[0:TP], big[0:TP], ACT.Sqrt).then_inc(big_rooted, 1)
                    act.wait_ge(norm_made, NT)
                    nc.scalar.activation(norm[0:TP, 1, :, 0], norm[0:TP, 0, :, 1], ACT.Sqrt, bias=scales[0:TP, 3:4]).then_inc(rooted, 1)

                @block.vector
                def _(dve):
                    link = Chain(dve, chain)
                    nc.vector.tensor_reduce(mx[0:TP], deg[0:TP, :, 0:2], AX.XY, ALU.max).then_inc(max_made, 1)
                    link(nc.vector.tensor_scalar(big[0:TP, 0:2], deg[0:TP, :, 0:2].rearrange("p t k -> p k t"), 1.0, None, ALU.add))
                    link(nc.vector.tensor_copy(big[0:TP, 2:6], deg[0:TP, :, 2:6].rearrange("p t k -> p k t")))
                    link(nc.vector.tensor_scalar(pos[0:TP], big[0:TP], 0.0, None, ALU.is_gt))
                    nc.vector.tensor_scalar(big[0:TP], big[0:TP], 1.0, None, ALU.max).then_inc(big_made, 1)
                    dve.wait_ge(big_rooted, 1)
                    link(nc.vector.reciprocal(inv[0:TP], big[0:TP]))
                    link(nc.vector.tensor_tensor(inv[0:TP], inv[0:TP], pos[0:TP], ALU.mult))
                    dve.wait_ge(max_turned, 1)
                    link(nc.vector.tensor_reduce(mrow[:, 3:4], p_mx[0:1, 0:TP], AX.X, ALU.max))
                    link(nc.vector.tensor_scalar(mrow[:, 2:3], mrow[:, 3:4], 1.0 / YROOM, None, ALU.mult))
                    link(nc.vector.reciprocal(mrow[:, 0:1], mrow[:, 2:3]))
                    nc.vector.tensor_scalar(mrow[:, 1:2], mrow[:, 0:1], 1.0 / ZS, None, ALU.mult).then_inc(max_row, 1)
                    dve.wait_ge(max_all, 1)
                    link(nc.vector.tensor_copy(scales[0:TP, 4:6], p_mx[0:TP, 128:130]))
                    for k in range(6):
                        link(nc.vector.tensor_scalar(roots[0:TP, 0, k], inv[0:TP, IN_DEG[k]], ZS, None, ALU.mult))
                        s = 1.0 / ZS if k < 2 else scales[0:TP, 5:6]
                        link(nc.vector.tensor_scalar(roots[0:TP, 1, k], inv[0:TP, OUT_DEG[k]], s, None, ALU.mult))
                        if k < 2:
                            link(nc.vector.tensor_tensor(both[0:TP, k], inv[0:TP, IN_DEG[k]], inv[0:TP, OUT_DEG[k]], ALU.mult))
                    layer_norm_all(nc, dve, link, xs, xl, stats, norm, stats_made, norm_made, rooted, xl_made)
                    dve.wait_ge(xl_made, NT)

        def inner(name, src, ks, ys):
            with ExitStack() as ctx2:
                def sb2(n, shape, dt):
                    return ctx2.enter_context(nc.sbuf_tensor(f"{name}_{n}", shape, dt))

                def sem(n):
                    return ctx2.enter_context(nc.semaphore(f"{name}_{n}"))

                strip = sb2("strip", [128, SR, NT, TP], F16)
                z = sb2("z", [128, NT, 2, 2, D], F16)
                y = sb2("y", [128, SR, 2, 2, D], F16)
                acc = ctx2.enter_context(nc.psum_tensor(f"{name}_acc", [128, SR, BANK], F32))
                strip_in = [sem(f"strip_in{j}") for j in range(SR)]
                hi_made = sem("hi_made")
                lo_made = sem("lo_made")
                sum_done = sem("sum_done")
                y_hi = sem("y_hi")
                y_lo = sem("y_lo")
                y_out = [dram.pool_sem(f"{name}_y_out{j}") for j in range(SR)]
                with nc.Block() as block:
                    @block.sync
                    def _(sp):
                        def tile(t, j, before):
                            if not isinstance(before, int):
                                sp.wait_ge(sum_done, t + (1 - SR))
                            sp.dma_start(strip[:, j], src[bass.ds(t, 1)].rearrange("a r k c -> r (a k) c")).then_inc(strip_in[j], 16)

                        for_ring(sp, tile)

                    @block.tensor
                    def _(pe):
                        def tile(t, j, before):
                            pe.wait_ge(strip_in[j], before * 16 + 16)
                            if not isinstance(before, int):
                                pe.wait_ge(y_lo, t + (1 - SR))
                            for kt in range(NT):
                                if isinstance(t, int) and t == 0:
                                    pe.wait_ge(lo_made, 2 * kt + 2)
                                for part in range(2):
                                    mm = nc.tensor.matmul(acc[0:TP, j, :], strip[0:TP, j, kt, :],
                                                          z[0:TP, kt, part].rearrange("p k d -> p (k d)"),
                                                          start=(kt == 0 and part == 0), stop=(kt == NT - 1 and part == 1))
                            mm.then_inc(sum_done, 1)

                        for_ring(pe, tile)

                    @block.scalar
                    def _(act):
                        def split(t, j, before):
                            for i, k in enumerate(ks):
                                nc.scalar.activation(z[0:TP, bass.ds(t, 1), 0, i, :].rearrange("p a d -> p (a d)"),
                                                     xl[0:TP, bass.ds(t, 1), :].rearrange("p a d -> p (a d)"), ACT.Copy,
                                                     scale=roots[0:TP, 0, k, bass.ds(t, 1)]).then_inc(hi_made, 1)

                        for_ring(act, split)

                        def tile(t, j, before):
                            act.wait_ge(sum_done, t + 1)
                            if not isinstance(before, int):
                                act.wait_ge(y_out[j], before * 32)
                            nc.scalar.activation(y[0:TP, j, :, 0, :], acc[0:TP, j, :].rearrange("p (k d) -> p k d", k=2), ACT.Copy,
                                                 scale=scales[0:TP, 4:5]).then_inc(y_hi, 1)

                        for_ring(act, tile)

                    @block.vector
                    def _(dve):
                        def split(t, j, before):
                            for i, k in enumerate(ks):
                                dve.wait_ge(hi_made, t * 2 + i + 1)
                                nc.vector.scalar_tensor_tensor(
                                    out=z[0:TP, bass.ds(t, 1), 1, i, :].rearrange("p a d -> p (a d)"),
                                    in0=xl[0:TP, bass.ds(t, 1), :].rearrange("p a d -> p (a d)"), scalar=roots[0:TP, 0, k, bass.ds(t, 1)],
                                    in1=z[0:TP, bass.ds(t, 1), 0, i, :].rearrange("p a d -> p (a d)"), op0=ALU.mult,
                                    op1=ALU.subtract).then_inc(lo_made, 1)

                        for_ring(dve, split)

                        def tile(t, j, before):
                            dve.wait_ge(y_hi, t + 1)
                            nc.vector.scalar_tensor_tensor(out=y[0:TP, j, :, 1, :], in0=acc[0:TP, j, :].rearrange("p (k d) -> p k d", k=2),
                                                           scalar=scales[0:TP, 4:5], in1=y[0:TP, j, :, 0, :], op0=ALU.mult,
                                                           op1=ALU.subtract).then_inc(y_lo, 1)

                        for_ring(dve, tile)

                    @block.gpsimd
                    def _(pool):
                        def tile(t, j, before):
                            pool.wait_ge(y_lo, t + 1)
                            for i in range(2):
                                pool.dma_start(ys[i][bass.ds(t, 1)].rearrange("a p n -> p (a n)"),
                                               y[0:TP, j, i].rearrange("p s d -> p (s d)")).then_inc(y_out[j], 16)

                        for_ring(pool, tile)
                        for j in range(SR):
                            pool.wait_ge(y_out[j], 32 * (NT // SR))

        def outer(name, src, ks, ys):
            with ExitStack() as ctx2:
                def sb2(n, shape, dt):
                    return ctx2.enter_context(nc.sbuf_tensor(f"{name}_{n}", shape, dt))

                def sem(n):
                    return ctx2.enter_context(nc.semaphore(f"{name}_{n}"))

                def ps(n, shape):
                    return ctx2.enter_context(nc.psum_tensor(f"{name}_{n}", shape, F32))

                KD = D // 128
                strip = sb2("strip", [128, SR, NT, TP], F16)
                z = sb2("z", [128, NT, 3, 2, D], F16)
                u = sb2("u", [128, 2, 3, D], F32)
                own = sb2("own", [128, 2, D], F32)
                uT = sb2("uT", [128, 3 * KD, 128], F32)
                w = sb2("w", [128, 3, KD, D], F32)
                b = sb2("b", [3, D], F32)
                acc = ps("acc", [128, 2, 2, BANK])
                turn = ps("turn", [128, 2, BANK])
                p_out = ps("out", [128, 2, BANK])
                strip_in = [sem(f"strip_in{j}") for j in range(SR)]
                z_in = [sem(f"z_in{c}") for c in range(SR)]
                w_in = sem("w_in")
                hi_made = sem("hi_made")
                lo_made = sem("lo_made")
                sum_done = sem("sum_done")
                own_made = sem("own_made")
                u_made = sem("u_made")
                u0_made = sem("u0_made")
                turned = sem("turned")
                uT_made = sem("uT_made")
                out_done = sem("out_done")
                added = sem("added")
                with nc.Block() as block:
                    @block.sync
                    def _(sp):
                        def features_and_weights():
                            for c in range(SR):
                                at = slice(c * GT, (c + 1) * GT)
                                for i in range(2):
                                    sp.dma_start(z[0:TP, at, i + 1].rearrange("p t s d -> p t (s d)"), ys[i][at].rearrange("t p n -> p t n")).then_inc(z_in[c], 16)
                            for n, k in enumerate(ks):
                                sp.dma_start(w[:, n], gw[k].rearrange("(k p) o -> p k o", p=128)).then_inc(w_in, 16)
                                sp.dma_start(b[n:n + 1, :], gbias[k:k + 1, :]).then_inc(w_in, 16)

                        def tile(t, j, before):
                            if not isinstance(before, int):
                                sp.wait_ge(sum_done, t + (1 - SR))
                            sp.dma_start(strip[:, j], src[bass.ds(t, 1)].rearrange("a r k c -> r (a k) c")).then_inc(strip_in[j], 16)
                            if isinstance(t, int) and t == 0:
                                features_and_weights()

                        for_ring(sp, tile)

                    @block.tensor
                    def _(pe):
                        def sums(j, p, kts, first=False):
                            for kt in kts:
                                if first and kt % GT == 0:
                                    pe.wait_ge(z_in[kt // GT], 32)
                                if first:
                                    pe.wait_ge(lo_made, kt + 1)
                                for part in range(2):
                                    for half, (k0, k1) in enumerate(((1, 3), (0, 1))):
                                        mm = nc.tensor.matmul(acc[0:TP, p, half, 0:(k1 - k0) * D].rearrange("p (k d) -> p k d", d=D),
                                                              strip[0:TP, j, kt, :], z[0:TP, kt, k0:k1, part, :],
                                                              start=(kt == 0 and part == 0), stop=(kt == NT - 1 and part == 1))
                            return mm

                        def turn_u(t, p):
                            pe.wait_ge(u_made, t * 2 + 2)
                            pe.wait_ge(u0_made, t + 1)
                            if not isinstance(t, int) or t >= 1:
                                pe.wait_ge(uT_made, t * 2)
                            for n in range(3 * KD):
                                mm = nc.tensor.transpose(turn[:, n // 4, (n % 4) * 128:(n % 4) * 128 + TP],
                                                         u[0:TP, p, n // KD, (n % KD) * 128:(n % KD + 1) * 128], ident[0:TP, 0:TP])
                            mm.then_inc(turned, 1)

                        def weigh(t, p):
                            pe.wait_ge(uT_made, t * 2 + 2)
                            if not isinstance(t, int) or t >= 2:
                                pe.wait_ge(added, t - 1)
                            for n in range(3 * KD):
                                nc.tensor.matmul(p_out[0:TP, p, 0:D], uT[:, n, 0:TP], w[:, n // KD, n % KD, :], start=(n == 0), stop=False)
                            nc.tensor.matmul(p_out[0:TP, p, 0:D], ones[0:3, 0:TP], b[:], start=False, stop=True).then_inc(out_done, 1)

                        def tile(t, j, before, p):
                            pe.wait_ge(strip_in[j], before * 16 + 16)
                            if not isinstance(t, int) or t >= 2:
                                pe.wait_ge(u_made, (t - 1) * 2)
                                pe.wait_ge(u0_made, t - 1)
                            first = isinstance(t, int) and t == 0
                            if isinstance(t, int) and t == 1:
                                pe.wait_ge(w_in, 96)
                            sums(j, p, range(0, 8), first)
                            if not isinstance(t, int) or t >= 1:
                                turn_u(t - 1, 1 - p)
                            sums(j, p, range(8, 16), first)
                            if not isinstance(t, int) or t >= 1:
                                weigh(t - 1, 1 - p)
                            sums(j, p, range(16, NT), first).then_inc(sum_done, 1)

                        for_ring2(pe, tile)
                        turn_u(NT - 1, (NT - 1) % 2)
                        weigh(NT - 1, (NT - 1) % 2)

                    @block.scalar
                    def _(act):
                        def split(t, j, before):
                            nc.scalar.activation(z[0:TP, bass.ds(t, 1), 0, 0, :].rearrange("p a d -> p (a d)"),
                                                 xl[0:TP, bass.ds(t, 1), :].rearrange("p a d -> p (a d)"), ACT.Copy,
                                                 scale=roots[0:TP, 0, ks[0], bass.ds(t, 1)]).then_inc(hi_made, 1)

                        for_ring(act, split)

                        def copy_turned(t):
                            act.wait_ge(turned, t + 1)
                            if not isinstance(t, int) or t >= 1:
                                act.wait_ge(out_done, t)
                            nc.scalar.copy(uT[:, 0:4, 0:TP], turn[:, 0].rearrange("p (n m) -> p n m", m=128)[:, :, 0:TP]).then_inc(uT_made, 1)
                            nc.scalar.copy(uT[:, 4:6, 0:TP], turn[:, 1, 0:256].rearrange("p (n m) -> p n m", m=128)[:, :, 0:TP]).then_inc(uT_made, 1)

                        def tile(t, j, before, p):
                            if not isinstance(t, int) or t >= 1:
                                copy_turned(t - 1)
                            if not isinstance(t, int) or t >= 2:
                                act.wait_ge(u0_made, t - 1)
                            nc.scalar.activation(own[0:TP, p], xl[0:TP, bass.ds(t, 1), :].rearrange("p a d -> p (a d)"), ACT.Copy,
                                                 scale=both[0:TP, ks[0], bass.ds(t, 1)]).then_inc(own_made, 1)
                            act.wait_ge(sum_done, t + 1)
                            if not isinstance(t, int) or t >= 2:
                                act.wait_ge(turned, t - 1)
                            nc.scalar.activation(u[0:TP, p, 1], acc[0:TP, p, 0, 0:D], ACT.Copy,
                                                 scale=roots[0:TP, 1, ks[1], bass.ds(t, 1)]).then_inc(u_made, 1)
                            nc.scalar.activation(u[0:TP, p, 2], acc[0:TP, p, 0, D:2 * D], ACT.Copy,
                                                 scale=roots[0:TP, 1, ks[2], bass.ds(t, 1)]).then_inc(u_made, 1)

                        for_ring2(act, tile)
                        copy_turned(NT - 1)

                    @block.vector
                    def _(dve):
                        def split(t, j, before):
                            dve.wait_ge(hi_made, t + 1)
                            nc.vector.scalar_tensor_tensor(
                                out=z[0:TP, bass.ds(t, 1), 0, 1, :].rearrange("p a d -> p (a d)"),
                                in0=xl[0:TP, bass.ds(t, 1), :].rearrange("p a d -> p (a d)"), scalar=roots[0:TP, 0, ks[0], bass.ds(t, 1)],
                                in1=z[0:TP, bass.ds(t, 1), 0, 0, :].rearrange("p a d -> p (a d)"), op0=ALU.mult,
                                op1=ALU.subtract).then_inc(lo_made, 1)

                        for_ring(dve, split)

                        def add(t, p):
                            dve.wait_ge(out_done, t + 1)
                            xt = xs[0:TP, bass.ds(t, 1), :].rearrange("p a d -> p (a d)")
                            nc.vector.tensor_tensor(xt, xt, p_out[0:TP, p, 0:D], ALU.add).then_inc(added, 1)

                        def tile(t, j, before, p):
                            dve.wait_ge(own_made, t + 1)
                            dve.wait_ge(sum_done, t + 1)
                            if not isinstance(t, int) or t >= 2:
                                dve.wait_ge(turned, t - 1)
                            nc.vector.scalar_tensor_tensor(out=u[0:TP, p, 0], in0=acc[0:TP, p, 1, 0:D],
                                                           scalar=roots[0:TP, 1, ks[0], bass.ds(t, 1)], in1=own[0:TP, p],
                                                           op0=ALU.mult, op1=ALU.add).then_inc(u0_made, 1)
                            if not isinstance(t, int) or t >= 1:
                                add(t - 1, 1 - p)

                        for_ring2(dve, tile)
                        add(NT - 1, (NT - 1) % 2)

        inner("ia", dram.adj_t, (2, 4), (dram.y[0], dram.y[2]))
        inner("it", dram.adj, (3, 5), (dram.y[1], dram.y[3]))
        outer("oa", dram.adj_t, (0, 2, 3), (dram.y[0], dram.y[1]))
        outer("ot", dram.adj, (1, 4, 5), (dram.y[2], dram.y[3]))


def gnn_and_experts(nc, ap, out):
    with ExitStack() as ctx:
        dram = Scratch(nc, ctx)
        ident, ident16, ones, ones16 = consts(nc, ctx)
        col_part = ctx.enter_context(nc.sbuf_tensor("col_part", [128, NT, NB], F32))
        deg = ctx.enter_context(nc.sbuf_tensor("deg", [128, NT, 6], F32))
        xs = ctx.enter_context(nc.sbuf_tensor("xs", [128, NT, D], F32))
        scales = ctx.enter_context(nc.sbuf_tensor("scales", [128, 8], F32))
        fill = ctx.enter_context(nc.semaphore("fill"))
        with nc.Block() as block:
            @block.vector
            def _(dve):
                nc.vector.memset(scales[:, 3:4], 1e-5).then_inc(fill, 1)
                dve.wait_ge(fill, 1)
        with ExitStack() as ctx2:
            att = Attention(nc, ctx2)
            prepare(nc, ap["x"], ap["w"], ap["wlr"], ap["wl_rows"], ap["src_dst"], ap["dst"], dram, ident, ident16, ones,
                    col_part, deg, xs, scales, att)
            graph_attention(nc, ap["x"], ap["gat_b"], dram, ones, att, deg, xs, scales)
        mixture(nc, 0, xs, {k[3:]: v for k, v in ap.items() if k.startswith("f0_")}, ident, ones, scales, deg, dram.adj, dram.slot_x, dram.slot_y, 512, dram.pool_sem)
        clear_semaphores(nc)
        graph_convolution(nc, xs, ap["g1_w"], ap["g1_b"], dram, ident, ones, deg, scales)
        clear_semaphores(nc)
        mixture(nc, 1, xs, {k[3:]: v for k, v in ap.items() if k.startswith("f1_")}, ident, ones, scales, deg, dram.adj, dram.slot_x, dram.slot_y, 256, dram.pool_sem, out)


def lay_out(inputs):
    inputs = {k: np.asarray(v) for k, v in inputs.items()}
    laid = {
        "x": inputs["x"], "src_dst": np.stack([inputs["src"], inputs["dst"]]), "dst": inputs["dst"],
        "w": inputs["L0_gnn_W"],
        "wlr": np.concatenate([inputs["L0_gnn_Wl"], inputs["L0_gnn_Wr"]]).T,
        "gat_b": np.broadcast_to(np.tile(inputs["L0_gnn_b"], HEADS), (TP, D)),
        "f0_gb": np.broadcast_to(np.stack([inputs["L0_ffn_gamma"], inputs["L0_ffn_beta"]]), (TP, 2, D)),
        "f0_wr": inputs["L0_ffn_Wr"], "f0_br": inputs["L0_ffn_br"][None],
        "f0_w1": inputs["L0_ffn_W1"], "f0_w2": inputs["L0_ffn_W2"],
        "f0_b1": np.broadcast_to(inputs["L0_ffn_b1"], (128, NE, 512)),
        "f0_b2": np.broadcast_to(inputs["L0_ffn_b2"], (128, NE, D)),
        "g1_w": inputs["L1_gnn_W"].transpose(0, 2, 1), "g1_b": inputs["L1_gnn_b"],
        "f1_wr": inputs["L1_ffn_router_w"].T, "f1_br": np.zeros((1, NE), np.float32),
        "f1_w1": inputs["L1_ffn_w1"], "f1_w2": inputs["L1_ffn_w2"],
        "f1_b1": np.broadcast_to(inputs["L1_ffn_b1"], (128, NE, D)),
        "f1_b2": np.broadcast_to(inputs["L1_ffn_b2"], (128, NE, D)),
        "wl_rows": np.broadcast_to(inputs["L0_gnn_Wl"].T[:, :, None], (HD, HEADS, TP)),
    }
    return {name: np.ascontiguousarray(a) for name, a in laid.items()}


def kernel(**inputs):
    import concourse.bacc as _bacc
    from concourse.bass_utils import run_bass_kernel_spmd as _run

    nc = _bacc.Bacc("TRN2", target_bir_lowering=False, num_devices=1)
    arrays, ap = {}, {}
    for name, a in lay_out(inputs).items():
        arrays[f"in_{name}"] = a
        ap[name] = nc.dram_tensor(f"in_{name}", a.shape, mybir.dt.from_np(a.dtype), kind="ExternalInput").ap()
    out = nc.dram_tensor("out_0", (N, D), F32, kind="ExternalOutput").ap()
    gnn_and_experts(nc, ap, out)
    r = _run(nc, [arrays], core_ids=[0])
    return r.results[0]["out_0"]
```
